# Optimizing a Trainium2 kernel written in Bass

```python
import numpy as np
import jax
import jax.numpy as jnp

def _softmax(x, axis=-1):
    return jax.nn.softmax(x, axis=axis)

def _gelu(x):
    return jax.nn.gelu(x, approximate=True)

def _silu(x):
    return jax.nn.silu(x)

def _sigmoid(x):
    return jax.nn.sigmoid(x)

def _layernorm(x, axis=-1, eps=1e-05):
    m = jnp.mean(x, axis=axis, keepdims=True)
    v = jnp.var(x, axis=axis, keepdims=True)
    return (x - m) / jnp.sqrt(v + eps)

def _scatter_add(tgt, idx, src, axis=0):
    return tgt.at[idx].add(src)

def _segment_sum(src, seg, n):
    return jax.ops.segment_sum(src, seg, n)
kernel_name = 'mk_seq_preln_d2_jaxref_r4_104152'

def setup_inputs(seed: int=0):
    np.random.seed(seed)
    _w = jnp.asarray

    def _L0_attn_setup():
        import jax, jax.numpy as jnp
        import numpy as np
        D_MODEL = 512
        D_INNER = 1024
        D_XB = 128
        D_STATE = 16
        D_CONV = 4
        DT_RANK = 128
        BATCH = 2
        SEQLEN = 256
        NXB = D_XB // D_STATE
        NC = D_INNER // D_STATE
        REP = NC // NXB
        DPG = D_INNER // NC

        def _mamba_fwd(hidden_states, W_in, W_dt, b_dt, conv_w, conv_b, A_log, D_param, W_out):
            b, l, _ = hidden_states.shape
            A = -jnp.exp(A_log)
            zxbcdt = hidden_states @ W_in.T
            splits = np.cumsum([D_INNER, D_XB, D_XB, D_INNER])
            z, x, Bm, Cm, dtl = jnp.split(zxbcdt, splits, axis=-1)
            dt_full = dtl @ W_dt.T + b_dt
            delta = jax.nn.softplus(dt_full + b_dt)
            x = x.transpose(0, 2, 1).reshape(b, NXB, D_STATE, l)
            x = jnp.repeat(x, REP, axis=1).reshape(b, D_INNER, l)
            x = jax.lax.conv_general_dilated(x, conv_w, (1,), [(D_CONV - 1, 0)], dimension_numbers=('NCH', 'OIH', 'NCH'), feature_group_count=D_INNER)
            x = jax.nn.silu(x + conv_b[None, :, None])
            Bg = jnp.repeat(Bm.reshape(b, l, NXB, D_STATE), REP, axis=2)
            Cg = Cm.reshape(b, l, NC, D_STATE)
            u_t = x.transpose(2, 0, 1)
            d_t = delta.transpose(1, 0, 2)
            B_t = Bg.transpose(1, 0, 2, 3)
            C_t = Cg.transpose(1, 0, 2, 3)
            A_g = A.reshape(NC, DPG, D_STATE)

            def step(state, inp):
                u, dlt, Bs, Cs = inp
                dA = jnp.exp(dlt.reshape(b, NC, DPG)[..., None] * A_g)
                du = (dlt * u).reshape(b, NC, DPG)
                state = dA * state + du[..., None] * Bs[:, :, None, :]
                y = jnp.einsum('bgdn,bgn->bgd', state, Cs).reshape(b, D_INNER)
                return (state, y)
            init = jnp.zeros((b, NC, DPG, D_STATE), jnp.float32)
            _, ys = jax.lax.scan(step, init, (u_t, d_t, B_t, C_t))
            y = ys.transpose(1, 0, 2)
            y = y + x.transpose(0, 2, 1) * D_param
            y = y * jax.nn.silu(z)
            return y @ W_out.T
        key = jax.random.key(seed)
        ks = jax.random.split(key, 8)
        s = 0.02
        hidden_states = jax.random.normal(ks[0], (BATCH, SEQLEN, D_MODEL), jnp.float32)
        W_in = jax.random.normal(ks[1], (2 * D_XB + 2 * D_INNER + DT_RANK, D_MODEL), jnp.float32) * s
        dt_std = DT_RANK ** (-0.5)
        W_dt = jax.random.uniform(ks[2], (D_INNER, DT_RANK), jnp.float32, -dt_std, dt_std)
        dt = jnp.exp(jax.random.uniform(ks[3], (D_INNER,), jnp.float32) * (np.log(0.1) - np.log(0.001)) + np.log(0.001))
        dt = jnp.clip(dt, 0.0001)
        b_dt = dt + jnp.log(-jnp.expm1(-dt))
        conv_w = jax.random.normal(ks[4], (D_INNER, 1, D_CONV), jnp.float32) * D_CONV ** (-0.5)
        conv_b = jnp.zeros((D_INNER,), jnp.float32)
        A_log = jnp.log(jnp.tile(jnp.arange(1, D_STATE + 1, dtype=jnp.float32), (D_INNER, 1)))
        D_param = jnp.ones((D_INNER,), jnp.float32)
        W_out = jax.random.normal(ks[5], (D_MODEL, D_INNER), jnp.float32) * s
        return dict(hidden_states=hidden_states, W_in=W_in, W_dt=W_dt, b_dt=b_dt, conv_w=conv_w, conv_b=conv_b, A_log=A_log, D_param=D_param, W_out=W_out)
    _L0_attn_in = _L0_attn_setup()

    def _L0_ffn_setup():
        import jax, jax.numpy as jnp
        import numpy as np
        B, L, D = (4, 1024, 512)
        DF = 4 * D
        CAPACITY_RATIO = 0.5
        key = jax.random.key(seed)
        ks = jax.random.split(key, 4)
        s = 0.02
        return {'x': jax.random.normal(ks[0], (B, L, D), dtype=jnp.float32), 'w_r': jax.random.normal(ks[1], (D,), dtype=jnp.float32) * s, 'b_r': jnp.zeros((), dtype=jnp.float32), 'w1': jax.random.normal(ks[2], (D, DF), dtype=jnp.float32) * s, 'b1': jnp.zeros((DF,), dtype=jnp.float32), 'w2': jax.random.normal(ks[3], (DF, D), dtype=jnp.float32) * s, 'b2': jnp.zeros((D,), dtype=jnp.float32)}
    _L0_ffn_in = _L0_ffn_setup()

    def _L1_attn_setup():
        import jax, jax.numpy as jnp
        import numpy as np
        import math
        D_MODEL = 512
        NUM_HEAD = 16
        HEAD_DIM = D_MODEL // NUM_HEAD

        def _trunc_normal(key, shape, std):
            return jax.random.truncated_normal(key, -3.0, 3.0, shape, dtype=jnp.float32) * std
        key = jax.random.key(seed)
        kx, kp, ko = jax.random.split(key, 3)
        b, s = (4, 512)
        x = jax.random.normal(kx, (b, s, D_MODEL), dtype=jnp.float32)
        sigma_p = math.sqrt(2.0 / (D_MODEL + 3 * D_MODEL))
        w_project = _trunc_normal(kp, (3 * D_MODEL, D_MODEL), sigma_p)
        sigma_o = math.sqrt(2.0 / (D_MODEL + D_MODEL))
        w_out = _trunc_normal(ko, (D_MODEL, D_MODEL), sigma_o)
        return {'x': x, 'w_project': w_project, 'w_out': w_out}
    _L1_attn_in = _L1_attn_setup()

    def _L1_ffn_setup():
        import jax, jax.numpy as jnp
        import numpy as np
        B, S, H = (4, 256, 512)
        E = 16
        K = 2
        I = 256
        N_SHARED = 2
        I_SHARED = I * N_SHARED
        RATIO = 0.1
        EPS = 1e-09

        def _swiglu(x, wg, wu, wd):
            return jax.nn.silu(x @ wg) * (x @ wu) @ wd
        key = jax.random.key(seed)
        ks = jax.random.split(key, 9)
        scale = 0.02
        x = jax.random.normal(ks[0], (B, S, H), dtype=jnp.float32)
        centroids = jax.random.normal(ks[1], (E, H), dtype=jnp.float32)
        gate_bias = jnp.zeros((E,), dtype=jnp.float32)
        wg_s = jax.random.normal(ks[2], (H, I_SHARED), dtype=jnp.float32) * scale
        wu_s = jax.random.normal(ks[3], (H, I_SHARED), dtype=jnp.float32) * scale
        wd_s = jax.random.normal(ks[4], (I_SHARED, H), dtype=jnp.float32) * scale
        wg = jax.random.normal(ks[5], (E, H, I), dtype=jnp.float32) * scale
        wu = jax.random.normal(ks[6], (E, H, I), dtype=jnp.float32) * scale
        wd = jax.random.normal(ks[7], (E, I, H), dtype=jnp.float32) * scale
        return {'x': x, 'centroids': centroids, 'gate_bias': gate_bias, 'wg_s': wg_s, 'wu_s': wu_s, 'wd_s': wd_s, 'wg': wg, 'wu': wu, 'wd': wd}
    _L1_ffn_in = _L1_ffn_setup()
    _d = {'L0_attn_hidden_states': _L0_attn_in['hidden_states'], 'L0_attn_W_in': _L0_attn_in['W_in'], 'L0_attn_W_dt': _L0_attn_in['W_dt'], 'L0_attn_b_dt': _L0_attn_in['b_dt'], 'L0_attn_conv_w': _L0_attn_in['conv_w'], 'L0_attn_conv_b': _L0_attn_in['conv_b'], 'L0_attn_A_log': _L0_attn_in['A_log'], 'L0_attn_D_param': _L0_attn_in['D_param'], 'L0_attn_W_out': _L0_attn_in['W_out'], 'L0_ffn_w_r': _L0_ffn_in['w_r'], 'L0_ffn_b_r': _L0_ffn_in['b_r'], 'L0_ffn_w1': _L0_ffn_in['w1'], 'L0_ffn_b1': _L0_ffn_in['b1'], 'L0_ffn_w2': _L0_ffn_in['w2'], 'L0_ffn_b2': _L0_ffn_in['b2'], 'L1_attn_w_project': _L1_attn_in['w_project'], 'L1_attn_w_out': _L1_attn_in['w_out'], 'L1_ffn_centroids': _L1_ffn_in['centroids'], 'L1_ffn_gate_bias': _L1_ffn_in['gate_bias'], 'L1_ffn_wg_s': _L1_ffn_in['wg_s'], 'L1_ffn_wu_s': _L1_ffn_in['wu_s'], 'L1_ffn_wd_s': _L1_ffn_in['wd_s'], 'L1_ffn_wg': _L1_ffn_in['wg'], 'L1_ffn_wu': _L1_ffn_in['wu'], 'L1_ffn_wd': _L1_ffn_in['wd']}
    _x0 = _d['L0_attn_hidden_states']
    _d['L0_attn_hidden_states'] = jax.random.normal(jax.random.fold_in(jax.random.key(seed), 1), (2, 1024, 512), dtype=_x0.dtype)
    del _x0
    return _d

def reference(L0_attn_hidden_states, L0_attn_W_in, L0_attn_W_dt, L0_attn_b_dt, L0_attn_conv_w, L0_attn_conv_b, L0_attn_A_log, L0_attn_D_param, L0_attn_W_out, L0_ffn_w_r, L0_ffn_b_r, L0_ffn_w1, L0_ffn_b1, L0_ffn_w2, L0_ffn_b2, L1_attn_w_project, L1_attn_w_out, L1_ffn_centroids, L1_ffn_gate_bias, L1_ffn_wg_s, L1_ffn_wu_s, L1_ffn_wd_s, L1_ffn_wg, L1_ffn_wu, L1_ffn_wd):

    def _L0_attn_ref(hidden_states, W_in, W_dt, b_dt, conv_w, conv_b, A_log, D_param, W_out):
        import jax, jax.numpy as jnp
        import numpy as np
        D_MODEL = 512
        D_INNER = 1024
        D_XB = 128
        D_STATE = 16
        D_CONV = 4
        DT_RANK = 128
        BATCH = 2
        SEQLEN = 256
        NXB = D_XB // D_STATE
        NC = D_INNER // D_STATE
        REP = NC // NXB
        DPG = D_INNER // NC

        def _mamba_fwd(hidden_states, W_in, W_dt, b_dt, conv_w, conv_b, A_log, D_param, W_out):
            b, l, _ = hidden_states.shape
            A = -jnp.exp(A_log)
            zxbcdt = hidden_states @ W_in.T
            splits = np.cumsum([D_INNER, D_XB, D_XB, D_INNER])
            z, x, Bm, Cm, dtl = jnp.split(zxbcdt, splits, axis=-1)
            dt_full = dtl @ W_dt.T + b_dt
            delta = jax.nn.softplus(dt_full + b_dt)
            x = x.transpose(0, 2, 1).reshape(b, NXB, D_STATE, l)
            x = jnp.repeat(x, REP, axis=1).reshape(b, D_INNER, l)
            x = jax.lax.conv_general_dilated(x, conv_w, (1,), [(D_CONV - 1, 0)], dimension_numbers=('NCH', 'OIH', 'NCH'), feature_group_count=D_INNER)
            x = jax.nn.silu(x + conv_b[None, :, None])
            Bg = jnp.repeat(Bm.reshape(b, l, NXB, D_STATE), REP, axis=2)
            Cg = Cm.reshape(b, l, NC, D_STATE)
            u_t = x.transpose(2, 0, 1)
            d_t = delta.transpose(1, 0, 2)
            B_t = Bg.transpose(1, 0, 2, 3)
            C_t = Cg.transpose(1, 0, 2, 3)
            A_g = A.reshape(NC, DPG, D_STATE)

            def step(state, inp):
                u, dlt, Bs, Cs = inp
                dA = jnp.exp(dlt.reshape(b, NC, DPG)[..., None] * A_g)
                du = (dlt * u).reshape(b, NC, DPG)
                state = dA * state + du[..., None] * Bs[:, :, None, :]
                y = jnp.einsum('bgdn,bgn->bgd', state, Cs).reshape(b, D_INNER)
                return (state, y)
            init = jnp.zeros((b, NC, DPG, D_STATE), jnp.float32)
            _, ys = jax.lax.scan(step, init, (u_t, d_t, B_t, C_t))
            y = ys.transpose(1, 0, 2)
            y = y + x.transpose(0, 2, 1) * D_param
            y = y * jax.nn.silu(z)
            return y @ W_out.T
        return _mamba_fwd(hidden_states, W_in, W_dt, b_dt, conv_w, conv_b, A_log, D_param, W_out)

    def _L0_ffn_ref(x, w_r, b_r, w1, b1, w2, b2):
        import jax, jax.numpy as jnp
        import numpy as np
        B, L, D = (4, 1024, 512)
        DF = 4 * D
        CAPACITY_RATIO = 0.5
        b, l, d = x.shape
        k = int(l * CAPACITY_RATIO)
        scores = jnp.einsum('bld,d->bl', x, w_r) + b_r
        _, idx = jax.lax.top_k(scores, k)
        x_sel = jnp.take_along_axis(x, idx[:, :, None], axis=1)
        h = jax.nn.gelu(jnp.einsum('bkd,df->bkf', x_sel, w1) + b1)
        out_sel = jnp.einsum('bkf,fd->bkd', h, w2) + b2
        batch_ix = jnp.arange(b)[:, None]
        out = jnp.zeros_like(x).at[batch_ix, idx].set(out_sel)
        return out

    def _L1_attn_ref(x, w_project, w_out):
        import jax, jax.numpy as jnp
        import numpy as np
        import math
        D_MODEL = 512
        NUM_HEAD = 16
        HEAD_DIM = D_MODEL // NUM_HEAD

        def _trunc_normal(key, shape, std):
            return jax.random.truncated_normal(key, -3.0, 3.0, shape, dtype=jnp.float32) * std
        b, s, d = x.shape
        qkv = jnp.einsum('bsd,od->bso', x, w_project)
        qkv = qkv.reshape(b, s, 3, NUM_HEAD, HEAD_DIM)
        qkv = jnp.transpose(qkv, (2, 0, 3, 1, 4))
        q, k, v = (qkv[0], qkv[1], qkv[2])
        att = jnp.einsum('bhqd,bhkd->bhqk', q, k) / math.sqrt(HEAD_DIM)
        causal = jnp.triu(jnp.ones((s, s), dtype=bool), k=1)
        att = jnp.where(causal[None, None, :, :], jnp.float32(-1000000000.0), att)
        att = jax.nn.softmax(att, axis=-1)
        out = jnp.einsum('bhqk,bhkd->bhqd', att, v)
        out = jnp.transpose(out, (0, 2, 1, 3)).reshape(b, s, d)
        return jnp.einsum('bsd,od->bso', out, w_out)

    def _L1_ffn_ref(x, centroids, gate_bias, wg_s, wu_s, wd_s, wg, wu, wd):
        import jax, jax.numpy as jnp
        import numpy as np
        B, S, H = (4, 256, 512)
        E = 16
        K = 2
        I = 256
        N_SHARED = 2
        I_SHARED = I * N_SHARED
        RATIO = 0.1
        EPS = 1e-09

        def _swiglu(x, wg, wu, wd):
            return jax.nn.silu(x @ wg) * (x @ wu) @ wd
        shared = _swiglu(x, wg_s, wu_s, wd_s) * RATIO
        affinity = jax.nn.sigmoid(jnp.einsum('bsh,eh->bse', x, centroids))
        biased = affinity + gate_bias
        _, top_idx = jax.lax.top_k(biased, K)
        top_aff = jnp.take_along_axis(affinity, top_idx, axis=-1)
        weights = top_aff / (top_aff.sum(-1, keepdims=True) + EPS)
        mask = (jax.nn.one_hot(top_idx, E, dtype=x.dtype) * weights[..., None]).sum(-2)
        routed = jnp.zeros_like(x)
        for e in range(E):
            routed = routed + mask[..., e:e + 1] * _swiglu(x, wg[e], wu[e], wd[e])
        return shared + routed
    x = L0_attn_hidden_states
    x = x + _L0_attn_ref(_layernorm(x, axis=-1), L0_attn_W_in, L0_attn_W_dt, L0_attn_b_dt, L0_attn_conv_w, L0_attn_conv_b, L0_attn_A_log, L0_attn_D_param, L0_attn_W_out)
    x = x + _L0_ffn_ref(_layernorm(x, axis=-1), L0_ffn_w_r, L0_ffn_b_r, L0_ffn_w1, L0_ffn_b1, L0_ffn_w2, L0_ffn_b2)
    x = x + _L1_attn_ref(_layernorm(x, axis=-1), L1_attn_w_project, L1_attn_w_out)
    x = x + _L1_ffn_ref(_layernorm(x, axis=-1), L1_ffn_centroids, L1_ffn_gate_bias, L1_ffn_wg_s, L1_ffn_wu_s, L1_ffn_wd_s, L1_ffn_wg, L1_ffn_wu, L1_ffn_wd)
    return x

_drawn_inputs = setup_inputs


def setup_inputs(seed=0):
    import zlib

    import numpy as np

    out = dict(_drawn_inputs(seed))
    spreads = {'L0_attn_conv_b': (0.0, 0.351),
     'L0_attn_D_param': (1.0, 0.6),
     'L0_ffn_b1': (0.0, 0.1),
     'L0_ffn_b2': (0.0, 0.1),
     'L1_ffn_gate_bias': (0.0, 2.0)}
    factors = {'L0_attn_W_dt': 8.0,
     'L0_attn_b_dt': 8.0,
     'L0_attn_A_log': 8.0,
     'L1_ffn_centroids': 22.736,
     'L1_ffn_wg_s': 8.0,
     'L1_ffn_wu_s': 8.0,
     'L1_ffn_wd_s': 8.0,
     'L1_ffn_wg': 8.0,
     'L1_ffn_wu': 7.975,
     'L1_ffn_wd': 7.945}
    for name, (base, spread) in spreads.items():
        noise = np.random.default_rng([zlib.crc32(name.encode()), seed]).standard_normal(out[name].shape)
        drawn = base * np.exp(spread * noise) if base else spread * noise
        out[name] = jnp.asarray(drawn.astype(out[name].dtype))
    for name, factor in factors.items():
        out[name] = (out[name] * factor).astype(out[name].dtype)
    return out
```

```python
from contextlib import ExitStack

import concourse.bass as bass
from concourse import mybir

F32 = mybir.dt.float32
BF16 = mybir.dt.bfloat16
I32 = mybir.dt.int32
U32 = mybir.dt.uint32
ALU = mybir.AluOpType
ACT = mybir.ActivationFunctionType
AX = mybir.AxisListType

P = 128
B, L, D = 2, 1024, 512
T = B * L
KD = D // P
CH = 512
NCH = L // CH
TT = CH // P
EPS = 1e-5
Z = 1

D_INNER, D_STATE, D_CONV = 1024, 16, 4
NC_T = D_INNER // P
GPT = P // D_STATE
M_IN = 3 * NC_T
HALO = D_CONV - 1
C_ROWS = 3 * 32
N_QUAD = D_STATE // 4

DF = 2048
KF = DF // P
K_SEL = L // 2

NH, HD = 16, 32
HG = P // HD
NHG = NH // HG
NQT = L // P
NEG = -1.0e9

E, TOPK, I_E = 16, 2, 256
I_SH = 512
RATIO = 0.1
RT_EPS = 1e-9
SLOT_TILE = 256
N_TILES = (T * TOPK) // SLOT_TILE + E - 1
TOK_TILES = T // P


class Scope:

    def __init__(self, nc, name):
        self.nc, self.name, self.stack, self.held = nc, name, ExitStack(), []
        self.at_zero = []

    def __enter__(self):
        self.stack.__enter__()
        return self

    def __exit__(self, *a):
        self.stack.__exit__(*a)
        self.nc.clear_and_free_semaphores(self.held)

    def sb(self, name, shape, dt=F32):
        return self.stack.enter_context(self.nc.sbuf_tensor(f"{self.name}_{name}", shape, dt))

    def ps(self, name, shape, dt=F32):
        return self.stack.enter_context(self.nc.psum_tensor(f"{self.name}_{name}", shape, dt))

    def sem(self, name):
        self.held.append(self.nc.alloc_semaphore(name=f"{self.name}_{name}"))
        return self.held[-1]

    def pool_dma_sem(self, name):
        self.at_zero.append(self.sem(name))
        return self.at_zero[-1]

    def sems(self, name, n):
        return [self.sem(f"{name}{i}") for i in range(n)]

    def block(self):
        self.passed = self.sem("passed")
        for sem in self.held:
            if sem not in self.at_zero:
                self.nc.gpsimd.sem_inc(sem, Z)
        self.nc.all_engine_barrier()
        return self.stack.enter_context(self.nc.Block())

    def hold(self, eng, sem, value):
        eng.wait_ge(sem, value)
        eng.sem_inc(self.passed, 1)


def rows(ap, start, n):
    return ap[bass.ds(start, n), :].rearrange("(t p) n -> p t n", p=P)


def cols(ap, start, n):
    return ap[:, :, bass.ds(start, n)].rearrange("c p t -> p c t")



def project_in(nc, a):
    M_Z, M_C, M_DT, M_X, M_B = 0, NC_T, 2 * NC_T, 2 * NC_T + 1, 2 * NC_T + 2
    NT, NV, NA = 2, 2, 4
    T_JOBS, V_JOBS, A_JOBS = KD, NC_T + 1, 2 + 3 * NC_T
    J_DT, J_XR, J_Z = 2, 2 + NC_T, 2 + 2 * NC_T
    N_CONST = 7
    with Scope(nc, "proj") as s:
        w_in = s.sb("w_in", [P, KD, (M_B + 1) * P])
        w_dt = s.sb("w_dt", [P, D_INNER])
        ident = s.sb("ident", [P, P])
        rep = s.sb("rep", [P, NC_T, P])
        bdt = s.sb("bdt", [P, NC_T])
        bdt2 = s.sb("bdt2", [P, NC_T])
        cw = s.sb("cw", [P, NC_T, D_CONV])
        cb = s.sb("cb", [P, NC_T])
        x = s.sb("x", [P, NCH, TT, D])
        stats = s.sb("stats", [P, NCH * TT, 6])
        mv = s.sb("mv", [P, NCH * TT, 2])
        std = s.sb("std", [P, NCH * TT])
        rstd = s.sb("rstd", [P, NCH * TT])
        xnT = s.sb("xnT", [P, KD, CH])
        dtl_x = s.sb("dtl_x", [P, 2, CH])
        xr = s.sb("xr", [P, NC_T, HALO + CH])
        conv = s.sb("conv", [P, 2, NC_T, CH])
        dt_x = s.sb("dt_x", [P, NC_T, CH])
        dt_e = s.sb("dt_e", [P, NC_T, CH])
        dt_l = s.sb("dt_l", [P, NC_T, CH])
        dt_d = s.sb("dt_d", [P, NC_T, CH])
        c_hi = s.sb("c_hi", [P, 2, CH], BF16)
        c_res = s.sb("c_res", [P, 2, CH])
        c_mid = s.sb("c_mid", [P, 2, CH], BF16)
        c_lo = s.sb("c_lo", [P, 2, CH], BF16)
        z = s.sb("z", [P, 2, CH])
        bT = s.sb("bT", [P, CH])

        ps_t = s.ps("ps_t", [P, NT, CH])
        ps_v = s.ps("ps_v", [P, NV, CH])
        ps_a = s.ps("ps_a", [P, NA, CH])

        consts, x_in, stats_ok, mv_ok, std_ok, rstd_ok, xn_ok = (s.sem(n) for n in (
            "consts", "x_in", "stats_ok", "mv_ok", "std_ok", "rstd_ok", "xn_ok"))
        t_full, t_read, v_full, v_read, a_full, a_read = (s.sem(n) for n in (
            "t_full", "t_read", "v_full", "v_read", "a_full", "a_read"))
        hi_ok, mid_ok, lo_ok = (s.sem(n) for n in ("hi_ok", "mid_ok", "lo_ok"))
        halo_ok, bdt2_ok, conv_step, u_ok = (s.sem(n) for n in ("halo_ok", "bdt2_ok", "conv_step", "u_ok"))
        abs_ok, exp_ok, ln_ok, sp_step, delta_ok, du_ok = (s.sem(n) for n in (
            "abs_ok", "exp_ok", "ln_ok", "sp_step", "delta_ok", "du_ok"))
        c_out, z_out = s.sems("c_out", 2), s.sems("z_out", 2)
        b_out, u_out, delta_out, du_out = (s.sem(n) for n in ("b_out", "u_out", "delta_out", "du_out"))
        block = s.block()
        SP_STEPS = 4

        @block.sync
        def _(sp):
            for dst, name in ((ident[:, :], "c_ident"), (w_dt[:, :], "w_dt"), (rep[:, :, :], "c_rep"),
                              (bdt[:, :], "b_dt"), (cw[:, :, :], "conv_w"), (cb[:, :], "conv_b")):
                sp.dma_start(dst, a[name]).then_inc(consts, 16)
            sp.dma_start(w_in[:, :, :], a["w_in"].rearrange("(k p) n -> p k n", p=P)).then_inc(consts, 16)
            with sp.Fori(0, B) as i:
                s.hold(sp, t_full, Z + i * NCH * T_JOBS)
                for ch in range(NCH):
                    sp.dma_start(x[:, ch, :, :], rows(a["x"], i * L + ch * CH, CH)).then_inc(x_in, 16)
                for ch in range(NCH):
                    g = i * NCH + ch
                    tok = i * L + ch * CH
                    s.hold(sp, v_read, Z + g * V_JOBS + NV + 1)
                    sp.dma_start(a["s_b"][:, bass.ds(tok, CH)], bT[:, :]).then_inc(b_out, 16)
                    for c in range(NC_T):
                        s.hold(sp, lo_ok, Z + g * NC_T + c + 1)
                        for n, part in enumerate((c_hi, c_mid, c_lo)):
                            sp.dma_start(a["s_c"][n, c, :, bass.ds(tok, CH)], part[:, c % 2, :]).then_inc(c_out[c % 2], 16)
                    for c in range(NC_T):
                        s.hold(sp, a_read, Z + g * A_JOBS + J_Z + c + NA + 1)
                        sp.dma_start(a["s_z"][c, :, bass.ds(tok, CH)], z[:, c % 2, :]).then_inc(z_out[c % 2], 16)
                    s.hold(sp, delta_ok, Z + g + 1)
                    sp.dma_start(cols(a["s_delta"], tok, CH), dt_l[:, :, :]).then_inc(delta_out, 16)
                    s.hold(sp, u_ok, Z + (g + 1) * NC_T)
                    sp.dma_start(cols(a["s_u"], tok, CH), conv[:, 1, :, :]).then_inc(u_out, 16)
                    s.hold(sp, du_ok, Z + g + 1)
                    sp.dma_start(cols(a["s_du"], tok, CH), dt_e[:, :, :]).then_inc(du_out, 16)
            for r in range(2):
                sp.wait_ge(c_out[r], Z + B * NCH * NC_T // 2 * 3 * 16)
                sp.wait_ge(z_out[r], Z + B * NCH * NC_T // 2 * 16)
            for done in (b_out, u_out, delta_out, du_out):
                sp.wait_ge(done, Z + B * NCH * 16)

        @block.gpsimd
        def _(pool):
            with pool.Fori(0, B) as i:
                for ch in range(NCH):
                    g = i * NCH + ch
                    for c in range(NC_T):
                        n = g * NC_T + c
                        s.hold(pool, v_read, Z + g * V_JOBS + c + NV + 2)
                        s.hold(pool, c_out[c % 2], Z + (g * (NC_T // 2) + c // 2) * 48)
                        nc.gpsimd.tensor_copy(c_mid[:, c % 2, :], c_res[:, c % 2, :]).then_inc(mid_ok, 1)
                        pool.wait_ge(mid_ok, Z + n + 1)
                        nc.gpsimd.tensor_tensor(c_lo[:, c % 2, :], c_res[:, c % 2, :], c_mid[:, c % 2, :],
                                                ALU.subtract).then_inc(lo_ok, 1)

        @block.tensor
        def _(pe):
            pe.wait_ge(consts, Z + 16 * N_CONST)
            with pe.Fori(0, B) as i:
                for ch in range(NCH):
                    g = i * NCH + ch

                    def project(dst, m):
                        for k in range(KD):
                            last = nc.tensor.matmul(dst, w_in[:, k, m * P:(m + 1) * P], xnT[:, k, :],
                                                    start=(k == 0), stop=(k == KD - 1))
                        return last

                    def slot_a(job):
                        pe.wait_ge(a_read, Z + g * A_JOBS + job + 1)
                        return ps_a[:, (ch * A_JOBS + job) % NA, :]

                    pe.wait_ge(xn_ok, Z + (g + 1) * TT)
                    for k in range(KD):
                        pe.wait_ge(t_read, Z + g * T_JOBS + k + 1)
                        for t in range(TT):
                            last = nc.tensor.transpose(ps_t[:, k % NT, t * P:(t + 1) * P],
                                                       x[:, ch, t, k * P:(k + 1) * P], ident[:, :])
                        last.then_inc(t_full, 1)
                    pe.wait_ge(t_read, Z + (g + 1) * T_JOBS + NT)
                    for job, m in enumerate((M_DT, M_X)):
                        project(slot_a(job), m).then_inc(a_full, 1)
                    for job in range(V_JOBS):
                        pe.wait_ge(v_read, Z + g * V_JOBS + job + 1)
                        project(ps_v[:, (ch * V_JOBS + job) % NV, :], M_C + job - 1 if job else M_B).then_inc(v_full, 1)
                    pe.wait_ge(a_read, Z + g * A_JOBS + NA + 1)
                    for c in range(NC_T):
                        nc.tensor.matmul(slot_a(J_DT + c), w_dt[:, c * P:(c + 1) * P], dtl_x[:, 0, :],
                                         start=True, stop=True).then_inc(a_full, 1)
                    pe.wait_ge(a_read, Z + g * A_JOBS + NA + 2)
                    for c in range(NC_T):
                        nc.tensor.matmul(slot_a(J_XR + c), rep[:, c, :], dtl_x[:, 1, :],
                                         start=True, stop=True).then_inc(a_full, 1)
                    for c in range(NC_T):
                        project(slot_a(J_Z + c), M_Z + c).then_inc(a_full, 1)

        @block.scalar
        def _(act):
            nc.scalar.nop().then_inc(a_read, NA)
            act.wait_ge(consts, Z + 16 * N_CONST)
            nc.scalar.mul(bdt2[:, :], bdt[:, :], 2.0).then_inc(bdt2_ok, 1)
            act.wait_ge(bdt2_ok, Z + 1)
            with act.Fori(0, B) as i:
                act.wait_ge(mv_ok, Z + (i + 1) * NCH * TT)
                nc.scalar.activation(std[:, :], mv[:, :, 1], ACT.Sqrt, bias=EPS).then_inc(std_ok, 1)
                for ch in range(NCH):
                    g = i * NCH + ch

                    def bank(job):
                        act.wait_ge(a_full, Z + g * A_JOBS + job + 1)
                        return ps_a[:, (ch * A_JOBS + job) % NA, :]

                    for job in range(2):
                        src = bank(job)
                        nc.scalar.copy(dtl_x[:, job, :], src).then_inc(a_read, 1)
                    for c in range(NC_T):
                        act.wait_ge(v_full, Z + g * V_JOBS + c + 2)
                        act.wait_ge(c_out[c % 2], Z + (g * (NC_T // 2) + c // 2) * 48)
                        nc.scalar.copy(c_hi[:, c % 2, :], ps_v[:, (ch * V_JOBS + c + 1) % NV, :]).then_inc(hi_ok, 1)
                    act.wait_ge(delta_ok, Z + g)
                    for c in range(NC_T):
                        src = bank(J_DT + c)
                        nc.scalar.activation(dt_x[:, c, :], src, ACT.Identity, bias=bdt2[:, c:c + 1]).then_inc(a_read, 1)
                    act.wait_ge(halo_ok, Z + g + 1)
                    for c in range(NC_T):
                        src = bank(J_XR + c)
                        nc.scalar.copy(xr[:, c, HALO:HALO + CH], src).then_inc(a_read, 1)
                    act.wait_ge(a_read, Z + g * A_JOBS + J_XR + NA)
                    act.wait_ge(du_out, Z + g * 16)
                    nc.scalar.activation(dt_e[:, :, :], dt_x[:, :, :], ACT.Abs).then_inc(abs_ok, 1)
                    act.wait_ge(abs_ok, Z + g + 1)
                    nc.scalar.activation(dt_e[:, :, :], dt_e[:, :, :], ACT.Exp, scale=-1.0).then_inc(exp_ok, 1)
                    act.wait_ge(exp_ok, Z + g + 1)
                    act.wait_ge(delta_out, Z + g * 16)
                    act.wait_ge(du_ok, Z + g)
                    nc.scalar.activation(dt_l[:, :, :], dt_e[:, :, :], ACT.Ln, bias=1.0).then_inc(ln_ok, 1)
                    for c in range(NC_T):
                        src = bank(J_Z + c)
                        act.wait_ge(z_out[c % 2], Z + (g * (NC_T // 2) + c // 2) * 16)
                        nc.scalar.activation(z[:, c % 2, :], src, ACT.Silu).then_inc(a_read, 1)
                    act.wait_ge(u_out, Z + g * 16)
                    act.wait_ge(du_ok, Z + g)
                    for c in range(NC_T):
                        act.wait_ge(conv_step, Z + (g * NC_T + c + 1) * D_CONV)
                        nc.scalar.activation(conv[:, 1, c, :], conv[:, 0, c, :], ACT.Silu, bias=cb[:, c:c + 1]).then_inc(u_ok, 1)

        @block.vector
        def _(dve):
            nc.vector.nop().then_inc(t_read, NT)
            nc.vector.nop().then_inc(v_read, NV)
            with dve.Fori(0, B) as i:
                dve.wait_ge(x_in, Z + (i + 1) * NCH * 16)
                for t in range(NCH * TT):
                    nc.vector.bn_stats(stats[:, t, :], x[:, t // TT, t % TT, :]).then_inc(stats_ok, 1)
                s.hold(dve, stats_ok, Z + (i + 1) * NCH * TT)
                for t in range(NCH * TT):
                    nc.vector.bn_aggr(mv[:, t, :], stats[:, t, :]).then_inc(mv_ok, 1)
                dve.wait_ge(std_ok, Z + i + 1)
                nc.vector.reciprocal(rstd[:, :], std[:, :]).then_inc(rstd_ok, 1)
                dve.wait_ge(rstd_ok, Z + i + 1)
                for t in range(NCH * TT):
                    xt = x[:, t // TT, t % TT, :]
                    nc.vector.tensor_scalar(xt, xt, mv[:, t, 0:1], rstd[:, t:t + 1], ALU.subtract, ALU.mult).then_inc(xn_ok, 1)
                for ch in range(NCH):
                    g = i * NCH + ch
                    dve.wait_ge(a_full, Z + g * A_JOBS)
                    dve.wait_ge(v_full, Z + g * V_JOBS)
                    for k in range(KD):
                        dve.wait_ge(t_full, Z + g * T_JOBS + k + 1)
                        nc.vector.tensor_copy(xnT[:, k, :], ps_t[:, k % NT, :]).then_inc(t_read, 1)
                    dve.wait_ge(conv_step, Z + g * NC_T * D_CONV)
                    if ch == 0:
                        nc.vector.memset(xr[:, :, 0:HALO], 0.0).then_inc(halo_ok, 1)
                    else:
                        nc.vector.tensor_copy(xr[:, :, 0:HALO], xr[:, :, CH:CH + HALO]).then_inc(halo_ok, 1)
                    dve.wait_ge(v_full, Z + g * V_JOBS + 1)
                    dve.wait_ge(b_out, Z + g * 16)
                    nc.vector.tensor_copy(bT[:, :], ps_v[:, (ch * V_JOBS) % NV, :]).then_inc(v_read, 1)
                    for c in range(NC_T):
                        dve.wait_ge(hi_ok, Z + g * NC_T + c + 1)
                        if c >= 2:
                            dve.wait_ge(lo_ok, Z + g * NC_T + c - 1)
                        nc.vector.tensor_tensor(c_res[:, c % 2, :], ps_v[:, (ch * V_JOBS + c + 1) % NV, :], c_hi[:, c % 2, :],
                                                ALU.subtract).then_inc(v_read, 1)
                    dve.wait_ge(u_ok, Z + g * NC_T)
                    for c in range(NC_T):
                        dve.wait_ge(a_read, Z + g * A_JOBS + J_XR + c + NA + 1)
                        for j in range(D_CONV):
                            step = (g * NC_T + c) * D_CONV + j
                            if j == 0:
                                nc.vector.tensor_scalar(conv[:, 0, c, :], xr[:, c, 0:CH], cw[:, c, 0:1], None,
                                                        ALU.mult).then_inc(conv_step, 1)
                            else:
                                dve.wait_ge(conv_step, Z + step)
                                nc.vector.scalar_tensor_tensor(out=conv[:, 0, c, :], in0=xr[:, c, j:j + CH], scalar=cw[:, c, j:j + 1],
                                                               in1=conv[:, 0, c, :], op0=ALU.mult, op1=ALU.add).then_inc(conv_step, 1)
                    dve.wait_ge(ln_ok, Z + g + 1)
                    dve.wait_ge(conv_step, Z + (g + 1) * NC_T * D_CONV)
                    nc.vector.tensor_scalar(dt_d[:, :, :], dt_e[:, :, :], 1.0, -1.0, ALU.add, ALU.add).then_inc(sp_step, 1)
                    dve.wait_ge(sp_step, Z + g * SP_STEPS + 1)
                    nc.vector.tensor_tensor(dt_d[:, :, :], dt_e[:, :, :], dt_d[:, :, :], ALU.subtract).then_inc(sp_step, 1)
                    dve.wait_ge(sp_step, Z + g * SP_STEPS + 2)
                    nc.vector.tensor_tensor(dt_l[:, :, :], dt_l[:, :, :], dt_d[:, :, :], ALU.add).then_inc(sp_step, 1)
                    dve.wait_ge(sp_step, Z + g * SP_STEPS + 3)
                    nc.vector.tensor_tensor(dt_l[:, :, :], dt_l[:, :, :], dt_e[:, :, :], ALU.min).then_inc(sp_step, 1)
                    dve.wait_ge(sp_step, Z + g * SP_STEPS + 4)
                    nc.vector.scalar_tensor_tensor(out=dt_l[:, :, :], in0=dt_x[:, :, :], scalar=0.0, in1=dt_l[:, :, :],
                                                   op0=ALU.max, op1=ALU.add).then_inc(delta_ok, 1)
                    dve.wait_ge(delta_ok, Z + g + 1)
                    dve.wait_ge(u_ok, Z + (g + 1) * NC_T)
                    nc.vector.tensor_tensor(dt_e[:, :, :], dt_l[:, :, :], conv[:, 1, :, :], ALU.mult).then_inc(du_ok, 1)


def selective_scan(nc, a):
    NB, R, NH_ = 8, 4, 2
    AHEAD = 4
    N = D_STATE
    with Scope(nc, "scan") as s:
        ident = s.sb("ident", [P, P])
        sel32 = s.sb("sel32", [C_ROWS, 4, P])
        sel = s.sb("sel", [C_ROWS, 4, P], BF16)
        a_exp = s.sb("a_exp", [P, NC_T * N])
        d_all = s.sb("d_all", [P, NC_T])
        a_cur = s.sb("a_cur", [P, B, N])
        d_cur = s.sb("d_cur", [P, B])
        delta = s.sb("delta", [P, B, L])
        du = s.sb("du", [P, B, L])
        u = s.sb("u", [P, B, L])
        sz = s.sb("sz", [P, B, L])
        cs = s.sb("cs", [C_ROWS, B, N_QUAD, L], BF16)
        b_bc = s.sb("b_bc", [P, NB, L])
        decay = s.sb("decay", [P, R, L])
        inp = s.sb("inp", [P, R, L])
        h = s.sb("h", [P, NH_, L])
        hc = s.sb("hc", [P, R, L])
        y = s.sb("y", [P, B, L])
        ps_c = s.ps("ps_c", [P, 2, L])
        ps_y = s.ps("ps_y", [P, B, L])

        consts, sel_ok, aexp_ok, cur_ok = (s.sem(n) for n in ("consts", "sel_ok", "aexp_ok", "cur_ok"))
        g_in = s.sems("g_in", B)
        b_in = s.sems("b_in", NB)
        exp_ok, inp_ok, scan_ok, hc_ok, c_full, sum_ok, skip_ok, fin_ok = (s.sem(n) for n in (
            "exp_ok", "inp_ok", "scan_ok", "hc_ok", "c_full", "sum_ok", "skip_ok", "fin_ok"))
        y_out = s.sems("y_out", B)
        block = s.block()
        G_LOADS = 4 + 3
        UNITS = B * N

        @block.sync
        def _(sp):
            def load_group(c, b):
                part = slice(b * L, (b + 1) * L)
                for dst, name in ((delta, "s_delta"), (du, "s_du"), (u, "s_u"), (sz, "s_z")):
                    sp.dma_start(dst[:, b, :], a[name][bass.ds(c, 1), :, part].rearrange("c p t -> (c p) t")).then_inc(g_in[b], 16)
                for n in range(3):
                    src = a["s_c"][n, bass.ds(c, 1), :, part].rearrange("c (q r) t -> (c r) q t", q=N_QUAD)
                    sp.dma_start(cs[32 * n:32 * n + 32, b, :, :], src).then_inc(g_in[b], 16)

            def load_b(c, b, n):
                k = (b * N + n) % NB
                row = a["s_b"][bass.ds(c * N + n, 1), b * L:(b + 1) * L]
                sp.dma_start(b_bc[:, k, :], row.to_broadcast([P, L])).then_inc(b_in[k], 16)

            for dst, name in ((ident[:, :], "c_ident"), (sel32[:, :, :], "c_sel"), (a_exp[:, :], "a_log"), (d_all[:, :], "d_param")):
                src = a[name].rearrange("p c n -> p (c n)") if name == "a_log" else a[name]
                sp.dma_start(dst, src).then_inc(consts, 16)
            load_group(0, 0)
            for n in range(AHEAD):
                load_b(0, 0, n)
            with sp.Fori(0, NC_T) as c:
                after = (c + 1) % NC_T
                for b in range(B):
                    g = c * B + b
                    for n in range(N):
                        m = b * N + n + AHEAD
                        s.hold(sp, inp_ok, Z + c * UNITS + m + 1)
                        load_b(c if m < UNITS else after, m % UNITS // N, m % N)
                        if n == 4:
                            s.hold(sp, fin_ok, Z + g)
                            load_group(c if b == 0 else after, 1 - b)
                        if n == 8 and b == 1:
                            sp.dma_start(a["s_y"][bass.ds(c, 1), :, 0:L].rearrange("c p t -> (c p) t"), y[:, 0, :]).then_inc(y_out[0], 16)
                s.hold(sp, fin_ok, Z + (c + 1) * B)
                sp.dma_start(a["s_y"][bass.ds(c, 1), :, L:2 * L].rearrange("c p t -> (c p) t"), y[:, 1, :]).then_inc(y_out[1], 16)
            for b in range(B):
                sp.wait_ge(y_out[b], Z + NC_T * 16)
            sp.wait_ge(g_in[0], Z + (NC_T + 1) * G_LOADS * 16)
            for k in range(AHEAD):
                sp.wait_ge(b_in[k], Z + (NC_T * UNITS // NB + 1) * 16)

        @block.scalar
        def _(act):
            act.wait_ge(consts, Z + 4 * 16)
            nc.scalar.activation(a_exp[:, :], a_exp[:, :], ACT.Exp).then_inc(aexp_ok, 1)
            nc.scalar.copy(sel[:, :, :], sel32[:, :, :]).then_inc(sel_ok, 1)
            act.wait_ge(aexp_ok, Z + 1)
            with act.Fori(0, NC_T) as c:
                for b in range(B):
                    g = c * B + b
                    if b == 0:
                        act.wait_ge(fin_ok, Z + c * B)
                        for bb in range(B):
                            nc.scalar.mul(a_cur[:, bb, :], a_exp[:, bass.ds(c * N, N)], -1.0).then_inc(cur_ok, 1)
                            nc.scalar.copy(d_cur[:, bb:bb + 1], d_all[:, bass.ds(c, 1)]).then_inc(cur_ok, 1)
                        act.wait_ge(cur_ok, Z + (c + 1) * 2 * B)
                    act.wait_ge(g_in[b], Z + (c + 1) * G_LOADS * 16)
                    for n in range(N):
                        act.wait_ge(scan_ok, Z + g * N + n + 1)
                        nc.scalar.activation(decay[:, n % R, :], delta[:, b, :], ACT.Exp, scale=a_cur[:, b, n:n + 1]).then_inc(exp_ok, 1)

        @block.gpsimd
        def _(pool):
            nc.gpsimd.nop().then_inc(inp_ok, NB)
            with pool.Fori(0, NC_T) as c:
                for b in range(B):
                    g = c * B + b
                    s.hold(pool, g_in[b], Z + (c + 1) * G_LOADS * 16)
                    for n in range(N):
                        k = (b * N + n) % NB
                        s.hold(pool, b_in[k], Z + (c * (UNITS // NB) + (b * N + n) // NB + 1) * 16)
                        s.hold(pool, scan_ok, Z + g * N + n + 1)
                        nc.gpsimd.tensor_tensor(inp[:, n % R, :], du[:, b, :], b_bc[:, k, :], ALU.mult).then_inc(inp_ok, 1)

        @block.vector
        def _(dve):
            nc.vector.nop().then_inc(scan_ok, R)
            nc.vector.nop().then_inc(hc_ok, NH_)
            with dve.Fori(0, NC_T) as c:
                for b in range(B):
                    g = c * B + b
                    for n in range(N):
                        U = g * N + n
                        dve.wait_ge(exp_ok, Z + U + 1)
                        dve.wait_ge(inp_ok, Z + U + NB + 1)
                        dve.wait_ge(hc_ok, Z + U + 1)
                        nc.vector.tensor_tensor_scan(h[:, n % NH_, :], decay[:, n % R, :], inp[:, n % R, :], 0.0,
                                                     ALU.mult, ALU.add).then_inc(scan_ok, 1)
                        dve.wait_ge(c_full, Z + U + 1)
                        dve.wait_ge(scan_ok, Z + U + R + 1)
                        dve.wait_ge(sum_ok, Z + U + 1)
                        nc.vector.tensor_tensor(hc[:, n % R, :], h[:, n % NH_, :], ps_c[:, n % 2, :], ALU.mult).then_inc(hc_ok, 1)
                    dve.wait_ge(sum_ok, Z + (g + 1) * N + R)
                    dve.wait_ge(y_out[b], Z + c * 16)
                    dve.wait_ge(cur_ok, Z + (c + 1) * 2 * B)
                    nc.vector.scalar_tensor_tensor(out=y[:, b, :], in0=u[:, b, :], scalar=d_cur[:, b:b + 1], in1=ps_y[:, b, :],
                                                   op0=ALU.mult, op1=ALU.add).then_inc(skip_ok, 1)
                    dve.wait_ge(skip_ok, Z + g + 1)
                    nc.vector.tensor_tensor(y[:, b, :], y[:, b, :], sz[:, b, :], ALU.mult).then_inc(fin_ok, 1)

        @block.tensor
        def _(pe):
            nc.tensor.nop().then_inc(sum_ok, R)
            pe.wait_ge(consts, Z + 4 * 16)
            pe.wait_ge(sel_ok, Z + 1)
            with pe.Fori(0, NC_T) as c:
                for b in range(B):
                    g = c * B + b

                    def spread(n):
                        pe.wait_ge(hc_ok, Z + g * N + n + 1)
                        for half in range(L // 512):
                            last = nc.tensor.matmul(ps_c[:, n % 2, half * 512:half * 512 + 512], sel[:, n % 4, :],
                                                    cs[:, b, n // 4, half * 512:half * 512 + 512], start=True, stop=True)
                        last.then_inc(c_full, 1)

                    pe.wait_ge(g_in[b], Z + (c + 1) * G_LOADS * 16)
                    spread(0)
                    pe.wait_ge(fin_ok, Z + c * B)
                    for n in range(N):
                        if n + 1 < N:
                            spread(n + 1)
                        pe.wait_ge(hc_ok, Z + g * N + n + NH_ + 1)
                        for half in range(L // 512):
                            last = nc.tensor.matmul(ps_y[:, b, half * 512:half * 512 + 512], ident[:, :],
                                                    hc[:, n % R, half * 512:half * 512 + 512], start=(n == 0), stop=(n == N - 1))
                        last.then_inc(sum_ok, 1)


def mix_out(nc, a):
    NP = 4
    KI = NC_T
    with Scope(nc, "mix") as s:
        w = s.sb("w", [P, KI, D])
        yT = s.sb("yT", [P, NCH, KI, CH])
        x = s.sb("x", [P, NCH, TT, D])
        xn = s.sb("xn", [P, NCH, TT, D])
        w_r = s.sb("w_r", [P, D])
        b_r = s.sb("b_r", [P, 1])
        stats = s.sb("stats", [P, NCH, TT, 6])
        mv = s.sb("mv", [P, NCH, TT, 2])
        std = s.sb("std", [P, NCH, TT])
        rstd = s.sb("rstd", [P, NCH, TT])
        prod = s.sb("prod", [P, TT, D])
        score = s.sb("score", [P, NCH, TT])
        ps = s.ps("ps", [P, NP, D])
        consts, full, read, stats_ok, mv_ok, std_ok, rstd_ok, xn_ok, dot_ok, score_ok = (s.sem(n) for n in (
            "consts", "full", "read", "stats_ok", "mv_ok", "std_ok", "rstd_ok", "xn_ok", "dot_ok", "score_ok"))
        y_in, x_in, x_out, xn_out, score_out = (s.sems(n, NCH) for n in ("y_in", "x_in", "x_out", "xn_out", "score_out"))
        block = s.block()

        @block.sync
        def _(sp):
            sp.dma_start(w[:, :, :], a["w_out"].rearrange("(k p) n -> p k n", p=P)).then_inc(consts, 16)
            sp.dma_start(w_r[:, :], a["w_r"].to_broadcast([P, D])).then_inc(consts, 16)
            sp.dma_start(b_r[:, :], a["b_r"].to_broadcast([P, 1])).then_inc(consts, 16)
            with sp.Fori(0, B) as i:
                for ch in range(NCH):
                    g = i * NCH + ch
                    s.hold(sp, full, Z + i * NCH * TT)
                    sp.dma_start(yT[:, ch, :, :], cols(a["s_y"], i * L + ch * CH, CH)).then_inc(y_in[ch], 16)
                    s.hold(sp, x_out[ch], Z + i * 16)
                    s.hold(sp, xn_ok, Z + i * NCH * TT)
                    sp.dma_start(x[:, ch, :, :], rows(a["x"], i * L + ch * CH, CH)).then_inc(x_in[ch], 16)
                for ch in range(NCH):
                    g = i * NCH + ch
                    tok = i * L + ch * CH
                    s.hold(sp, read, Z + (g + 1) * TT + NP)
                    sp.dma_start(rows(a["s_x1"], tok, CH), x[:, ch, :, :]).then_inc(x_out[ch], 16)
                    s.hold(sp, xn_ok, Z + (g + 1) * TT)
                    sp.dma_start(rows(a["s_n1"], tok, CH), xn[:, ch, :, :]).then_inc(xn_out[ch], 16)
                    s.hold(sp, score_ok, Z + g + 1)
                    sp.dma_start(a["s_score"][:, bass.ds(g * TT, TT)], score[:, ch, :]).then_inc(score_out[ch], 16)
            for ch in range(NCH):
                for done in (x_out, xn_out, score_out):
                    sp.wait_ge(done[ch], Z + B * 16)

        @block.tensor
        def _(pe):
            pe.wait_ge(consts, Z + 48)
            with pe.Fori(0, B) as i:
                for ch in range(NCH):
                    g = i * NCH + ch
                    pe.wait_ge(y_in[ch], Z + (i + 1) * 16)
                    for t in range(TT):
                        pe.wait_ge(read, Z + g * TT + t + 1)
                        for k in range(KI):
                            last = nc.tensor.matmul(ps[:, t, :], yT[:, ch, k, t * P:(t + 1) * P], w[:, k, :],
                                                    start=(k == 0), stop=(k == KI - 1))
                        last.then_inc(full, 1)

        @block.scalar
        def _(act):
            with act.Fori(0, B) as i:
                for ch in range(NCH):
                    act.wait_ge(mv_ok, Z + (i * NCH + ch + 1) * TT)
                    nc.scalar.activation(std[:, ch, :], mv[:, ch, :, 1], ACT.Sqrt, bias=EPS).then_inc(std_ok, 1)

        @block.vector
        def _(dve):
            nc.vector.nop().then_inc(read, NP)
            dve.wait_ge(consts, Z + 48)
            with dve.Fori(0, B) as i:
                for ch in range(NCH):
                    g = i * NCH + ch
                    dve.wait_ge(x_in[ch], Z + (i + 1) * 16)
                    for t in range(TT):
                        dve.wait_ge(full, Z + g * TT + t + 1)
                        nc.vector.tensor_tensor(x[:, ch, t, :], x[:, ch, t, :], ps[:, t, :], ALU.add).then_inc(read, 1)
                        dve.wait_ge(read, Z + g * TT + t + NP + 1)
                        nc.vector.bn_stats(stats[:, ch, t, :], x[:, ch, t, :]).then_inc(stats_ok, 1)
                    s.hold(dve, stats_ok, Z + (g + 1) * TT)
                    for t in range(TT):
                        nc.vector.bn_aggr(mv[:, ch, t, :], stats[:, ch, t, :]).then_inc(mv_ok, 1)
                    dve.wait_ge(std_ok, Z + g + 1)
                    nc.vector.reciprocal(rstd[:, ch, :], std[:, ch, :]).then_inc(rstd_ok, 1)
                    dve.wait_ge(rstd_ok, Z + g + 1)
                    dve.wait_ge(xn_out[ch], Z + i * 16)
                    for t in range(TT):
                        nc.vector.tensor_scalar(xn[:, ch, t, :], x[:, ch, t, :], mv[:, ch, t, 0:1], rstd[:, ch, t:t + 1],
                                                ALU.subtract, ALU.mult).then_inc(xn_ok, 1)
                    dve.wait_ge(score_out[ch], Z + i * 16)
                    dve.wait_ge(dot_ok, Z + g * TT)
                    for t in range(TT):
                        dve.wait_ge(xn_ok, Z + g * TT + t + 1)
                        nc.vector.tensor_tensor_reduce(prod[:, t, :], xn[:, ch, t, :], w_r[:, :], 1.0, 0.0,
                                                       ALU.mult, ALU.add, score[:, ch, t:t + 1]).then_inc(dot_ok, 1)
                    dve.wait_ge(dot_ok, Z + (g + 1) * TT)
                    nc.vector.tensor_scalar(score[:, ch, :], score[:, ch, :], b_r[:, 0:1], None, ALU.add).then_inc(score_ok, 1)


def rank_tokens(nc, a):
    with Scope(nc, "rank") as s:
        col = s.sb("col", [P, TOK_TILES])
        colT = s.sb("colT", [TOK_TILES, P])
        ident = s.sb("ident", [P, P])
        row = s.sb("row", [P, T])
        earlier = s.sb("earlier", [P, P])
        scratch = s.sb("scratch", [P, 3, TOK_TILES, L], BF16)
        cnt = s.sb("cnt", [P, 3, TOK_TILES])
        half = s.sb("half", [P, TOK_TILES])
        dest = s.sb("dest", [P, TOK_TILES])
        dest_i = s.sb("dest_i", [P, TOK_TILES], I32)
        xn = s.sb("xn", [P, TOK_TILES, D])
        zeros = s.sb("zeros", [P, TOK_TILES // 2, D])
        ps = s.ps("ps", [TOK_TILES, P])
        col_in, row_in, xn_in, zero_ok, zero_out, colT_ok, colT_sb, colT_out, cnt_zero, cnt_ok, step, dest_ok, dest_out = (s.sem(n) for n in (
            "col_in", "row_in", "xn_in", "zero_ok", "zero_out", "colT_ok", "colT_sb", "colT_out", "cnt_zero", "cnt_ok", "step", "dest_ok", "dest_out"))
        sent = s.pool_dma_sem("sent")
        block = s.block()
        N_CNT = 3 * TOK_TILES - B

        @block.sync
        def _(sp):
            sp.dma_start(col[:, :], a["s_score"]).then_inc(col_in, 16)
            sp.dma_start(ident[:, :], a["c_ident"]).then_inc(col_in, 16)
            sp.dma_start(earlier[:, :], a["c_earlier"]).then_inc(row_in, 16)
            sp.wait_ge(colT_sb, Z + 1)
            sp.dma_start(a["s_score_row"].rearrange("o (t p) -> (o t) p", p=P), colT[:, :]).then_inc(colT_out, 16)
            sp.dma_start(xn[:, :, :], rows(a["s_n1"], 0, T)).then_inc(xn_in, 16)
            sp.wait_ge(colT_out, Z + 16)
            sp.dma_start(row[:, :], a["s_score_row"].to_broadcast([P, T])).then_inc(row_in, 16)
            sp.wait_ge(zero_ok, Z + 1)
            sp.dma_start(rows(a["s_sel_out"], B * K_SEL, B * K_SEL), zeros[:, :, :]).then_inc(zero_out, 16)
            sp.wait_ge(dest_ok, Z + 1)
            sp.dma_start(a["s_dest"], dest_i[:, :]).then_inc(dest_out, 16)
            sp.wait_ge(dest_out, Z + 16)
            sp.wait_ge(zero_out, Z + 16)

        @block.tensor
        def _(pe):
            pe.wait_ge(col_in, Z + 32)
            nc.tensor.transpose(ps[:, :], col[:, :], ident[:, :]).then_inc(colT_ok, 1)

        @block.scalar
        def _(act):
            act.wait_ge(colT_ok, Z + 1)
            nc.scalar.copy(colT[:, :], ps[:, :]).then_inc(colT_sb, 1)

        @block.vector
        def _(dve):
            nc.vector.memset(cnt[:, :, :], 0.0).then_inc(cnt_zero, 1)
            dve.wait_ge(row_in, Z + 32)
            dve.wait_ge(col_in, Z + 32)
            dve.wait_ge(cnt_zero, Z + 1)
            for j in range(TOK_TILES):
                b, t = j // NQT, j % NQT
                seq = row[:, b * L:(b + 1) * L]
                me = col[:, j:j + 1]
                nc.vector.tensor_scalar(scratch[:, 0, j, 0:L - t * P], seq[:, t * P:L], me, 0.0, ALU.is_gt, ALU.add,
                                        accum_out=cnt[:, 0, j:j + 1]).then_inc(cnt_ok, 1)
                nc.vector.scalar_tensor_tensor(out=scratch[:, 1, j, 0:P], in0=seq[:, t * P:(t + 1) * P], scalar=me, in1=earlier[:, :],
                                               op0=ALU.is_equal, op1=ALU.mult, accum_out=cnt[:, 1, j:j + 1]).then_inc(cnt_ok, 1)
                if t:
                    nc.vector.tensor_scalar(scratch[:, 2, j, 0:t * P], seq[:, 0:t * P], me, 0.0, ALU.is_ge, ALU.add,
                                            accum_out=cnt[:, 2, j:j + 1]).then_inc(cnt_ok, 1)
            dve.wait_ge(cnt_ok, Z + N_CNT)
            nc.vector.tensor_tensor(cnt[:, 0, :], cnt[:, 0, :], cnt[:, 1, :], ALU.add).then_inc(step, 1)
            dve.wait_ge(step, Z + 1)
            nc.vector.tensor_tensor(cnt[:, 0, :], cnt[:, 0, :], cnt[:, 2, :], ALU.add).then_inc(step, 1)
            dve.wait_ge(step, Z + 2)
            nc.vector.tensor_scalar(half[:, :], cnt[:, 0, :], float(K_SEL), float(K_SEL), ALU.is_ge, ALU.mult).then_inc(step, 1)
            dve.wait_ge(step, Z + 3)
            nc.vector.tensor_tensor(dest[:, :], cnt[:, 0, :], half[:, :], ALU.add).then_inc(step, 1)
            dve.wait_ge(step, Z + 4)
            nc.vector.tensor_scalar(dest[:, NQT:], dest[:, NQT:], float(K_SEL), None, ALU.add).then_inc(step, 1)
            dve.wait_ge(step, Z + 5)
            nc.vector.tensor_copy(dest_i[:, :], dest[:, :]).then_inc(dest_ok, 1)

        @block.gpsimd
        def _(pool):
            nc.gpsimd.memset(zeros[:, :, :], 0.0).then_inc(zero_ok, 1)
            pool.wait_ge(dest_ok, Z + 1)
            pool.wait_ge(xn_in, Z + 16)
            for j in range(TOK_TILES):
                nc.gpsimd.indirect_dma_start(a["s_sel_in"], bass.IndirectOffsetOnAxis(ap=dest_i[:, j:j + 1].bitcast(U32), axis=0),
                                             xn[:, j, :], None).then_inc(sent, 16)
            pool.wait_ge(sent, 16 * TOK_TILES)


def select_ffn(nc, a):
    NT, NA, NV = 2, 4, 2
    with Scope(nc, "ffn") as s:
        w1 = s.sb("w1", [P, KD, DF])
        w2 = s.sb("w2", [P, KF, D])
        b1 = s.sb("b1", [P, KF])
        b2 = s.sb("b2", [P, D])
        ident = s.sb("ident", [P, P])
        xs = s.sb("xs", [P, TT, D])
        xT = s.sb("xT", [P, KD, CH])
        hT = s.sb("hT", [P, KF, CH])
        y = s.sb("y", [P, TT, D])
        ps_t = s.ps("ps_t", [P, NT, CH])
        ps_h = s.ps("ps_h", [P, NA, CH])
        ps_y = s.ps("ps_y", [P, NV, D])
        consts, x_in, t_full, t_read, h_full, h_read, y_full, y_read, y_out = (s.sem(n) for n in (
            "consts", "x_in", "t_full", "t_read", "h_full", "h_read", "y_full", "y_read", "y_out"))
        block = s.block()

        @block.sync
        def _(sp):
            sp.dma_start(ident[:, :], a["c_ident"]).then_inc(consts, 16)
            sp.dma_start(b1[:, :], a["b1"]).then_inc(consts, 16)
            sp.dma_start(w1[:, :, :], a["w1"].rearrange("(k p) n -> p k n", p=P)).then_inc(consts, 16)
            sp.dma_start(w2[:, :, :], a["w2"].rearrange("(k p) n -> p k n", p=P)).then_inc(consts, 16)
            sp.dma_start(b2[:, :], a["b2"].to_broadcast([P, D])).then_inc(consts, 16)
            sp.dma_start(xs[:, :, :], rows(a["s_sel_in"], 0, CH)).then_inc(x_in, 16)
            with sp.Fori(0, B) as b:
                s.hold(sp, t_full, Z + (b + 1) * KD)
                sp.dma_start(xs[:, :, :], rows(a["s_sel_in"], (B - 1) * CH, CH)).then_inc(x_in, 16)
                for t in range(TT):
                    s.hold(sp, y_read, Z + b * TT + t + NV + 1)
                    sp.dma_start(a["s_sel_out"][bass.ds(b * CH + t * P, P), :], y[:, t, :]).then_inc(y_out, 16)
            sp.wait_ge(y_out, Z + B * TT * 16)
            sp.wait_ge(x_in, Z + (B + 1) * 16)

        @block.tensor
        def _(pe):
            pe.wait_ge(consts, Z + 80)
            with pe.Fori(0, B) as b:
                pe.wait_ge(x_in, Z + (b + 1) * 16)
                for k in range(KD):
                    pe.wait_ge(t_read, Z + b * KD + k + 1)
                    for t in range(TT):
                        last = nc.tensor.transpose(ps_t[:, k % NT, t * P:(t + 1) * P], xs[:, t, k * P:(k + 1) * P], ident[:, :])
                    last.then_inc(t_full, 1)
                pe.wait_ge(t_read, Z + (b + 1) * KD + NT)
                for f in range(KF):
                    pe.wait_ge(h_read, Z + b * KF + f + 1)
                    for k in range(KD):
                        last = nc.tensor.matmul(ps_h[:, f % NA, :], w1[:, k, f * P:(f + 1) * P], xT[:, k, :],
                                                start=(k == 0), stop=(k == KD - 1))
                    last.then_inc(h_full, 1)
                pe.wait_ge(h_read, Z + (b + 1) * KF + NA)
                for t in range(TT):
                    pe.wait_ge(y_read, Z + b * TT + t + 1)
                    for f in range(KF):
                        last = nc.tensor.matmul(ps_y[:, t % NV, :], hT[:, f, t * P:(t + 1) * P], w2[:, f, :],
                                                start=(f == 0), stop=(f == KF - 1))
                    last.then_inc(y_full, 1)

        @block.scalar
        def _(act):
            nc.scalar.nop().then_inc(h_read, NA)
            act.wait_ge(consts, Z + 80)
            with act.Fori(0, B) as b:
                act.wait_ge(y_full, Z + b * TT)
                for f in range(KF):
                    act.wait_ge(h_full, Z + b * KF + f + 1)
                    nc.scalar.activation(hT[:, f, :], ps_h[:, f % NA, :], ACT.Gelu_apprx_tanh, bias=b1[:, f:f + 1]).then_inc(h_read, 1)

        @block.vector
        def _(dve):
            nc.vector.nop().then_inc(t_read, NT)
            nc.vector.nop().then_inc(y_read, NV)
            dve.wait_ge(consts, Z + 80)
            with dve.Fori(0, B) as b:
                dve.wait_ge(h_full, Z + b * KF)
                for k in range(KD):
                    dve.wait_ge(t_full, Z + b * KD + k + 1)
                    nc.vector.tensor_copy(xT[:, k, :], ps_t[:, k % NT, :]).then_inc(t_read, 1)
                dve.wait_ge(y_out, Z + b * TT * 16)
                for t in range(TT):
                    dve.wait_ge(y_full, Z + b * TT + t + 1)
                    nc.vector.tensor_tensor(y[:, t, :], ps_y[:, t % NV, :], b2[:, :], ALU.add).then_inc(y_read, 1)


def attend_in(nc, a):
    NT, NA, NV = 2, 4, 2
    QK_JOBS = 2 * NHG
    with Scope(nc, "qkv") as s:
        w = s.sb("w", [P, KD, 3 * D])
        ident = s.sb("ident", [P, P])
        dest = s.sb("dest", [P, TOK_TILES], I32)
        got = s.sb("got", [P, TOK_TILES, D])
        x = s.sb("x", [P, NCH, TT, D])
        xn = s.sb("xn", [P, NCH, TT, D])
        stats = s.sb("stats", [P, NCH, TT, 6])
        mv = s.sb("mv", [P, NCH, TT, 2])
        std = s.sb("std", [P, NCH, TT])
        rstd = s.sb("rstd", [P, NCH, TT])
        xT = s.sb("xT", [P, KD, CH])
        qk = s.sb("qk", [P, QK_JOBS, CH])
        v = s.sb("v", [P, TT, NH, HD + 1])
        ps_t = s.ps("ps_t", [P, NT, CH])
        ps_a = s.ps("ps_a", [P, NA, CH])
        ps_v = s.ps("ps_v", [P, NV, D])
        consts, dest_in, x2_ok, stats_ok, mv_ok, std_ok, rstd_ok, xn_ok = (s.sem(n) for n in (
            "consts", "dest_in", "x2_ok", "stats_ok", "mv_ok", "std_ok", "rstd_ok", "xn_ok"))
        t_full, t_read, a_full, a_read, v_full, v_read, qk_out, v_out = (s.sem(n) for n in (
            "t_full", "t_read", "a_full", "a_read", "v_full", "v_read", "qk_out", "v_out"))
        ones_ok = s.sem("ones_ok")
        got_in = s.pool_dma_sem("got_in")
        x_in, x_out = s.sems("x_in", NCH), s.sems("x_out", NCH)
        block = s.block()

        @block.sync
        def _(sp):
            sp.dma_start(dest[:, :], a["s_dest"]).then_inc(dest_in, 16)
            sp.dma_start(ident[:, :], a["c_ident"]).then_inc(consts, 16)
            sp.dma_start(w[:, :, :], a["w_qkv"].rearrange("(k p) n -> p k n", p=P)).then_inc(consts, 16)
            with sp.Fori(0, B) as i:
                for ch in range(NCH):
                    s.hold(sp, x_out[ch], Z + i * 16)
                    s.hold(sp, xn_ok, Z + i * NCH * TT)
                    sp.dma_start(x[:, ch, :, :], rows(a["s_x1"], i * L + ch * CH, CH)).then_inc(x_in[ch], 16)
                for ch in range(NCH):
                    g = i * NCH + ch
                    tok = i * L + ch * CH
                    s.hold(sp, x2_ok, Z + (g + 1) * TT)
                    sp.dma_start(rows(a["s_x2"], tok, CH), x[:, ch, :, :]).then_inc(x_out[ch], 16)
                    s.hold(sp, a_read, Z + (g + 1) * QK_JOBS + NA)
                    for n, name in enumerate(("s_q", "s_k")):
                        sp.dma_start(cols(a[name], tok, CH), qk[:, n * NHG:(n + 1) * NHG, :]).then_inc(qk_out, 16)
                    s.hold(sp, v_read, Z + (g + 1) * TT + NV)
                    sp.dma_start(rows(a["s_v"], tok, CH), v[:, :, :, :].rearrange("p t h d -> p t (h d)")).then_inc(v_out, 16)
            sp.wait_ge(qk_out, Z + B * NCH * 32)
            sp.wait_ge(v_out, Z + B * NCH * 16)
            for ch in range(NCH):
                sp.wait_ge(x_out[ch], Z + B * 16)

        @block.gpsimd
        def _(pool):
            pool.wait_ge(dest_in, Z + 16)
            for j in range(TOK_TILES):
                nc.gpsimd.indirect_dma_start(got[:, j, :], None, a["s_sel_out"],
                                             bass.IndirectOffsetOnAxis(ap=dest[:, j:j + 1].bitcast(U32), axis=0)).then_inc(got_in, 16)

        @block.tensor
        def _(pe):
            pe.wait_ge(consts, Z + 32)
            with pe.Fori(0, B) as i:
                for ch in range(NCH):
                    g = i * NCH + ch
                    pe.wait_ge(xn_ok, Z + (g + 1) * TT)
                    for k in range(KD):
                        pe.wait_ge(t_read, Z + g * KD + k + 1)
                        for t in range(TT):
                            last = nc.tensor.transpose(ps_t[:, k % NT, t * P:(t + 1) * P], xn[:, ch, t, k * P:(k + 1) * P], ident[:, :])
                        last.then_inc(t_full, 1)
                    pe.wait_ge(t_read, Z + (g + 1) * KD + NT)
                    for m in range(QK_JOBS):
                        pe.wait_ge(a_read, Z + g * QK_JOBS + m + 1)
                        for k in range(KD):
                            last = nc.tensor.matmul(ps_a[:, m % NA, :], w[:, k, m * P:(m + 1) * P], xT[:, k, :],
                                                    start=(k == 0), stop=(k == KD - 1))
                        last.then_inc(a_full, 1)
                    for t in range(TT):
                        pe.wait_ge(v_read, Z + g * TT + t + 1)
                        for k in range(KD):
                            last = nc.tensor.matmul(ps_v[:, t % NV, :], xT[:, k, t * P:(t + 1) * P], w[:, k, 2 * D:3 * D],
                                                    start=(k == 0), stop=(k == KD - 1))
                        last.then_inc(v_full, 1)

        @block.scalar
        def _(act):
            nc.scalar.nop().then_inc(a_read, NA)
            with act.Fori(0, B) as i:
                act.wait_ge(mv_ok, Z + (i + 1) * NCH * TT)
                nc.scalar.activation(std[:, :, :], mv[:, :, :, 1], ACT.Sqrt, bias=EPS).then_inc(std_ok, 1)
                for ch in range(NCH):
                    g = i * NCH + ch
                    act.wait_ge(qk_out, Z + g * 32)
                    for m in range(QK_JOBS):
                        act.wait_ge(a_full, Z + g * QK_JOBS + m + 1)
                        nc.scalar.copy(qk[:, m, :], ps_a[:, m % NA, :]).then_inc(a_read, 1)

        @block.vector
        def _(dve):
            nc.vector.nop().then_inc(t_read, NT)
            nc.vector.nop().then_inc(v_read, NV)
            nc.vector.memset(v[:, :, :, :], 1.0).then_inc(ones_ok, 1)
            dve.wait_ge(ones_ok, Z + 1)
            dve.wait_ge(got_in, 16 * TOK_TILES)
            with dve.Fori(0, B) as i:
                for ch in range(NCH):
                    g = i * NCH + ch
                    dve.wait_ge(x_in[ch], Z + (i + 1) * 16)
                    nc.vector.tensor_tensor(x[:, ch, :, :], x[:, ch, :, :], got[:, bass.ds(g * TT, TT), :], ALU.add).then_inc(x2_ok, TT)
                    dve.wait_ge(x2_ok, Z + (g + 1) * TT)
                    for t in range(TT):
                        nc.vector.bn_stats(stats[:, ch, t, :], x[:, ch, t, :]).then_inc(stats_ok, 1)
                    s.hold(dve, stats_ok, Z + (g + 1) * TT)
                    for t in range(TT):
                        nc.vector.bn_aggr(mv[:, ch, t, :], stats[:, ch, t, :]).then_inc(mv_ok, 1)
                dve.wait_ge(std_ok, Z + i + 1)
                nc.vector.reciprocal(rstd[:, :, :], std[:, :, :]).then_inc(rstd_ok, 1)
                dve.wait_ge(rstd_ok, Z + i + 1)
                dve.wait_ge(t_full, Z + i * NCH * KD)
                for t in range(NCH * TT):
                    n, m = t // TT, t % TT
                    nc.vector.tensor_scalar(xn[:, n, m, :], x[:, n, m, :], mv[:, n, m, 0:1], rstd[:, n, m:m + 1],
                                            ALU.subtract, ALU.mult).then_inc(xn_ok, 1)
                for ch in range(NCH):
                    g = i * NCH + ch
                    dve.wait_ge(v_full, Z + g * TT)
                    for k in range(KD):
                        dve.wait_ge(t_full, Z + g * KD + k + 1)
                        nc.vector.tensor_copy(xT[:, k, :], ps_t[:, k % NT, :]).then_inc(t_read, 1)
                    dve.wait_ge(v_out, Z + g * 16)
                    for t in range(TT):
                        dve.wait_ge(v_full, Z + g * TT + t + 1)
                        nc.vector.tensor_copy(v[:, t, :, 0:HD], ps_v[:, t % NV, :].rearrange("p (h d) -> p h d", d=HD)).then_inc(v_read, 1)


def attend(nc, a):
    R, NS = 4, 2
    UQ = HG
    UB = NQT * UQ
    U = B * UB
    LATE = NQT // 2 * UQ
    VW = HD + 1
    SCALE = 1.0 / float(HD) ** 0.5
    Z_ROWS = 2 * P
    with Scope(nc, "att") as s:
        ident = s.sb("ident", [P, P])
        mask = s.sb("mask", [P, L])
        q = s.sb("q", [P, B, HG, L])
        kT = s.sb("kT", [P, B, L])
        v = s.sb("v", [P, B, NQT, HG, VW])
        sm = s.sb("sm", [P, R, L])
        mx = s.sb("mx", [P, R])
        nb = s.sb("nb", [P, R])
        p = s.sb("p", [P, R, L])
        pT = s.sb("pT", [P, 2, NQT, P])
        rec = s.sb("rec", [P, 2, HG])
        o = s.sb("o", [P, B, NQT, HG, HD])
        zeros = s.sb("zeros", [P, Z_ROWS // P, D])
        ps_s = s.ps("ps_s", [P, NS, L])
        ps_t = s.ps("ps_t", [P, 2, 4, P])
        ps_o = s.ps("ps_o", [P, 2, 512])
        consts, q_zero, s_full, max_ok, nb_ok, exp_ok, t0_full, t1_full, e0_ok, e1_ok, pv_ok, rec_ok, norm_ok, z_ok = (s.sem(n) for n in (
            "consts", "q_zero", "s_full", "max_ok", "nb_ok", "exp_ok", "t0_full", "t1_full", "e0_ok", "e1_ok", "pv_ok", "rec_ok", "norm_ok", "z_ok"))
        z_out = s.pool_dma_sem("z_out")
        g_in, o_out = s.sems("g_in", B), s.sems("o_out", B)
        block = s.block()
        G_LOADS = HG + 2

        def unit(u):
            return u // UB, u % UB // UQ, u % UQ

        def late(i, u):
            return i * B * LATE + (u // UB) * LATE + (u % UB - LATE)

        @block.sync
        def _(sp):
            sp.dma_start(ident[:, :], a["c_ident"]).then_inc(consts, 16)
            sp.dma_start(mask[:, :], a["c_mask"]).then_inc(consts, 16)
            sp.wait_ge(q_zero, Z + 1)
            with sp.Fori(0, NHG) as i:
                for b in range(B):
                    s.hold(sp, norm_ok, Z + i * B * NQT + 2)
                    part = slice(b * L, (b + 1) * L)
                    for h in range(HG):
                        r = slice(h * HD, (h + 1) * HD)
                        sp.dma_start(q[r, b, h, :], a["s_q"][bass.ds(i, 1), r, part].rearrange("g p t -> (g p) t")).then_inc(g_in[b], 16)
                    sp.dma_start(kT[:, b, :], a["s_k"][bass.ds(i, 1), :, part].rearrange("g p t -> (g p) t")).then_inc(g_in[b], 16)
                    sp.dma_start(v[:, b, :, :, :].rearrange("p t h d -> p t (h d)"),
                                 a["s_v"][part, bass.ds(i * (HG * VW), HG * VW)].rearrange("(t p) n -> p t n", p=P)).then_inc(g_in[b], 16)
                for b in range(B):
                    s.hold(sp, norm_ok, Z + i * B * NQT + (b + 1) * NQT + 2)
                    sp.dma_start(a["s_o"][b * L:(b + 1) * L, bass.ds(i * P, P)].rearrange("(t p) n -> p t n", p=P),
                                 o[:, b, :, :, :].rearrange("p t h d -> p t (h d)")).then_inc(o_out[b], 16)
            for b in range(B):
                sp.wait_ge(o_out[b], Z + NHG * 16)

        @block.gpsimd
        def _(pool):
            nc.gpsimd.memset(q[:, :, :, :], 0.0).then_inc(q_zero, 1)
            nc.gpsimd.memset(zeros[:, :, :], 0.0).then_inc(z_ok, 1)
            pool.wait_ge(z_ok, Z + 1)
            with pool.Fori(0, N_TILES * SLOT_TILE // Z_ROWS) as i:
                nc.gpsimd.dma_start(rows(a["s_xs"], i * Z_ROWS, Z_ROWS), zeros[:, :, :]).then_inc(z_out, 16)
            pool.wait_ge(z_out, N_TILES * SLOT_TILE // Z_ROWS * 16)

        @block.tensor
        def _(pe):
            pe.wait_ge(consts, Z + 32)
            with pe.Fori(0, NHG) as i:

                def score(u):
                    b, t, h = unit(u)
                    if u % UB == 0:
                        pe.wait_ge(g_in[b], Z + (i + 1) * G_LOADS * 16)
                    pe.wait_ge(max_ok, Z + i * U + u + 1)
                    keys = (t + 1) * P
                    for k in range(0, keys, 512):
                        n = min(512, keys - k)
                        last = nc.tensor.matmul(ps_s[:, u % NS, k:k + n], q[:, b, h, t * P:(t + 1) * P], kT[:, b, k:k + n],
                                                start=True, stop=True)
                    last.then_inc(s_full, 1)

                def turn(u):
                    b, t, h = unit(u)
                    pe.wait_ge(exp_ok, Z + i * U + u + R + 1)
                    for half in range(t // 4 + 1):
                        if half == 0:
                            pe.wait_ge(e0_ok, Z + i * U + u)
                        else:
                            pe.wait_ge(e1_ok, Z + late(i, u))
                        for k in range(4 * half, min(4 * half + 4, t + 1)):
                            last = nc.tensor.transpose(ps_t[:, half, k % 4, :], p[:, u % R, k * P:(k + 1) * P], ident[:, :])
                        last.then_inc((t0_full, t1_full)[half], 1)

                def weigh(u):
                    b, t, h = unit(u)
                    if h == 0:
                        pe.wait_ge(norm_ok, Z + (i * B + b) * NQT + t + 1)
                    pe.wait_ge(e0_ok, Z + i * U + u + 1)
                    if t >= 4:
                        pe.wait_ge(e1_ok, Z + late(i, u) + 1)
                    for k in range(t + 1):
                        last = nc.tensor.matmul(ps_o[:, t % 2, h * VW:(h + 1) * VW], pT[:, u % 2, k, :], v[:, b, k, h, :],
                                                start=(k == 0), stop=(k == t))
                    last.then_inc(pv_ok, 1)

                score(0)
                score(1)
                for u in range(U):
                    if u + 2 < U:
                        score(u + 2)
                    turn(u)
                    if u:
                        weigh(u - 1)
                weigh(U - 1)

        @block.scalar
        def _(act):
            nc.scalar.nop().then_inc(exp_ok, R)
            with act.Fori(0, NHG) as i:

                def exponential(u):
                    b, t, h = unit(u)
                    keys = (t + 1) * P
                    act.wait_ge(nb_ok, Z + i * U + u + 1)
                    act.wait_ge(pv_ok, Z + i * U + u + 1)
                    nc.scalar.activation(p[:, u % R, 0:keys], sm[:, u % R, 0:keys], ACT.Exp, bias=nb[:, u % R:u % R + 1],
                                         scale=SCALE).then_inc(exp_ok, 1)

                exponential(0)
                for u in range(U):
                    if u + 1 < U:
                        exponential(u + 1)
                    b, t, h = unit(u)
                    if t >= 4:
                        act.wait_ge(t1_full, Z + late(i, u) + 1)
                        act.wait_ge(pv_ok, Z + i * U + u + R - 1)
                        nc.scalar.copy(pT[:, u % 2, 4:t + 1, :], ps_t[:, 1, 0:t - 3, :]).then_inc(e1_ok, 1)

        @block.vector
        def _(dve):
            nc.vector.nop().then_inc(max_ok, NS)
            nc.vector.nop().then_inc(norm_ok, 2)
            nc.vector.nop().then_inc(pv_ok, R)
            dve.wait_ge(consts, Z + 32)
            with dve.Fori(0, NHG) as i:

                def maximum(u):
                    b, t, h = unit(u)
                    keys = (t + 1) * P
                    dve.wait_ge(s_full, Z + i * U + u + 1)
                    s.hold(dve, exp_ok, Z + i * U + u + 1)
                    nc.vector.tensor_tensor_reduce(sm[:, u % R, 0:keys], ps_s[:, u % NS, 0:keys], mask[:, L - keys:L], 1.0, 3 * NEG,
                                                   ALU.add, ALU.max, mx[:, u % R:u % R + 1]).then_inc(max_ok, 1)
                    dve.wait_ge(max_ok, Z + i * U + u + NS + 1)
                    nc.vector.tensor_scalar(nb[:, u % R:u % R + 1], mx[:, u % R:u % R + 1], -SCALE, None, ALU.mult).then_inc(nb_ok, 1)

                def normalise(n):
                    b, t = n // NQT, n % NQT
                    g = i * B * NQT + n
                    dve.wait_ge(pv_ok, Z + i * U + (n + 1) * UQ + R)
                    out = ps_o[:, t % 2, 0:HG * VW].rearrange("p (h d) -> p h d", d=VW)
                    dve.wait_ge(norm_ok, Z + g + 1)
                    nc.vector.reciprocal(rec[:, t % 2, :], out[:, :, HD]).then_inc(rec_ok, 1)
                    dve.wait_ge(rec_ok, Z + g + 1)
                    if t == 0:
                        dve.wait_ge(o_out[b], Z + i * 16)
                    nc.vector.tensor_tensor(o[:, b, t, :, :], out[:, :, 0:HD], rec[:, t % 2, :].unsqueeze(2).to_broadcast([P, HG, HD]),
                                            ALU.mult).then_inc(norm_ok, 1)

                maximum(0)
                for u in range(U):
                    if u + 1 < U:
                        maximum(u + 1)
                    b, t, h = unit(u)
                    n = min(t + 1, 4)
                    dve.wait_ge(t0_full, Z + i * U + u + 1)
                    dve.wait_ge(pv_ok, Z + i * U + u + R - 1)
                    nc.vector.tensor_copy(pT[:, u % 2, 0:n, :], ps_t[:, 0, 0:n, :]).then_inc(e0_ok, 1)
                    if u >= UQ and u % UQ == 1:
                        normalise(u // UQ - 1)
                normalise(U // UQ - 1)


def attend_out(nc, a):
    NT, NP = 2, 4
    with Scope(nc, "att_out") as s:
        w = s.sb("w", [P, KD, D])
        ident = s.sb("ident", [P, P])
        o = s.sb("o", [P, NCH, TT, D])
        oT = s.sb("oT", [P, KD, CH])
        x = s.sb("x", [P, NCH, TT, D])
        xn = s.sb("xn", [P, NCH, TT, D])
        stats = s.sb("stats", [P, NCH, TT, 6])
        mv = s.sb("mv", [P, NCH, TT, 2])
        std = s.sb("std", [P, NCH, TT])
        rstd = s.sb("rstd", [P, NCH, TT])
        ps_t = s.ps("ps_t", [P, NT, CH])
        ps = s.ps("ps", [P, NP, D])
        consts, t_full, t_read, full, read, stats_ok, mv_ok, std_ok, rstd_ok, xn_ok = (s.sem(n) for n in (
            "consts", "t_full", "t_read", "full", "read", "stats_ok", "mv_ok", "std_ok", "rstd_ok", "xn_ok"))
        o_in, x_in, x_out, xn_out = (s.sems(n, NCH) for n in ("o_in", "x_in", "x_out", "xn_out"))
        block = s.block()

        @block.sync
        def _(sp):
            sp.dma_start(ident[:, :], a["c_ident"]).then_inc(consts, 16)
            sp.dma_start(w[:, :, :], a["w_o"].rearrange("(k p) n -> p k n", p=P)).then_inc(consts, 16)
            with sp.Fori(0, B) as i:
                for ch in range(NCH):
                    s.hold(sp, t_full, Z + i * NCH * KD)
                    sp.dma_start(o[:, ch, :, :], rows(a["s_o"], i * L + ch * CH, CH)).then_inc(o_in[ch], 16)
                    s.hold(sp, x_out[ch], Z + i * 16)
                    s.hold(sp, xn_ok, Z + i * NCH * TT)
                    sp.dma_start(x[:, ch, :, :], rows(a["s_x2"], i * L + ch * CH, CH)).then_inc(x_in[ch], 16)
                for ch in range(NCH):
                    g = i * NCH + ch
                    tok = i * L + ch * CH
                    s.hold(sp, read, Z + (g + 1) * TT + NP)
                    sp.dma_start(rows(a["s_x3"], tok, CH), x[:, ch, :, :]).then_inc(x_out[ch], 16)
                    s.hold(sp, xn_ok, Z + (g + 1) * TT)
                    sp.dma_start(rows(a["s_n3"], tok, CH), xn[:, ch, :, :]).then_inc(xn_out[ch], 16)
            for ch in range(NCH):
                sp.wait_ge(x_out[ch], Z + B * 16)
                sp.wait_ge(xn_out[ch], Z + B * 16)

        @block.tensor
        def _(pe):
            pe.wait_ge(consts, Z + 32)
            with pe.Fori(0, B) as i:
                for ch in range(NCH):
                    g = i * NCH + ch
                    pe.wait_ge(o_in[ch], Z + (i + 1) * 16)
                    for k in range(KD):
                        pe.wait_ge(t_read, Z + g * KD + k + 1)
                        for t in range(TT):
                            last = nc.tensor.transpose(ps_t[:, k % NT, t * P:(t + 1) * P], o[:, ch, t, k * P:(k + 1) * P], ident[:, :])
                        last.then_inc(t_full, 1)
                    pe.wait_ge(t_read, Z + (g + 1) * KD + NT)
                    for t in range(TT):
                        pe.wait_ge(read, Z + g * TT + t + 1)
                        for k in range(KD):
                            last = nc.tensor.matmul(ps[:, t, :], oT[:, k, t * P:(t + 1) * P], w[:, k, :],
                                                    start=(k == 0), stop=(k == KD - 1))
                        last.then_inc(full, 1)

        @block.scalar
        def _(act):
            nc.scalar.nop().then_inc(t_read, NT)
            with act.Fori(0, B) as i:
                for ch in range(NCH):
                    g = i * NCH + ch
                    act.wait_ge(full, Z + g * TT)
                    for k in range(KD):
                        act.wait_ge(t_full, Z + g * KD + k + 1)
                        nc.scalar.copy(oT[:, k, :], ps_t[:, k % NT, :]).then_inc(t_read, 1)
                    act.wait_ge(mv_ok, Z + (g + 1) * TT)
                    nc.scalar.activation(std[:, ch, :], mv[:, ch, :, 1], ACT.Sqrt, bias=EPS).then_inc(std_ok, 1)

        @block.vector
        def _(dve):
            nc.vector.nop().then_inc(read, NP)
            with dve.Fori(0, B) as i:
                for ch in range(NCH):
                    g = i * NCH + ch
                    dve.wait_ge(x_in[ch], Z + (i + 1) * 16)
                    for t in range(TT):
                        dve.wait_ge(full, Z + g * TT + t + 1)
                        nc.vector.tensor_tensor(x[:, ch, t, :], x[:, ch, t, :], ps[:, t, :], ALU.add).then_inc(read, 1)
                        dve.wait_ge(read, Z + g * TT + t + NP + 1)
                        nc.vector.bn_stats(stats[:, ch, t, :], x[:, ch, t, :]).then_inc(stats_ok, 1)
                    s.hold(dve, stats_ok, Z + (g + 1) * TT)
                    for t in range(TT):
                        nc.vector.bn_aggr(mv[:, ch, t, :], stats[:, ch, t, :]).then_inc(mv_ok, 1)
                    dve.wait_ge(std_ok, Z + g + 1)
                    nc.vector.reciprocal(rstd[:, ch, :], std[:, ch, :]).then_inc(rstd_ok, 1)
                    dve.wait_ge(rstd_ok, Z + g + 1)
                    dve.wait_ge(xn_out[ch], Z + i * 16)
                    for t in range(TT):
                        nc.vector.tensor_scalar(xn[:, ch, t, :], x[:, ch, t, :], mv[:, ch, t, 0:1], rstd[:, ch, t:t + 1],
                                                ALU.subtract, ALU.mult).then_inc(xn_ok, 1)


def shared_ffn(nc, a):
    NT, NG, NV = 2, 4, 2
    KS = I_SH // P
    with Scope(nc, "shr") as s:
        wg = s.sb("wg", [P, KD, I_SH])
        wu = s.sb("wu", [P, KD, I_SH])
        wd = s.sb("wd", [P, KS, D])
        cent = s.sb("cent", [P, KD, E])
        ident = s.sb("ident", [P, P])
        xn = s.sb("xn", [P, NCH, TT, D])
        x = s.sb("x", [P, NCH, TT, D])
        xT = s.sb("xT", [P, KD, CH])
        sg = s.sb("sg", [P, 2, CH])
        hT = s.sb("hT", [P, KS, CH])
        lg = s.sb("lg", [P, NCH, TT, E])
        ps_t = s.ps("ps_t", [P, NT, CH])
        ps_g = s.ps("ps_g", [P, NG, CH])
        ps_v = s.ps("ps_v", [P, NV, D])
        consts, t_full, t_read, g_full, silu_ok, h_ok, v_full, v_read = (s.sem(n) for n in (
            "consts", "t_full", "t_read", "g_full", "silu_ok", "h_ok", "v_full", "v_read"))
        xn_in, x_in, x_out, lg_out = (s.sems(n, NCH) for n in ("xn_in", "x_in", "x_out", "lg_out"))
        block = s.block()
        V_JOBS = 2 + TT

        @block.sync
        def _(sp):
            sp.dma_start(ident[:, :], a["c_ident"]).then_inc(consts, 16)
            sp.dma_start(cent[:, :, :], a["cent"].rearrange("(k p) n -> p k n", p=P)).then_inc(consts, 16)
            for dst, name in ((wg, "wg_s"), (wu, "wu_s"), (wd, "wd_s")):
                sp.dma_start(dst[:, :, :], a[name].rearrange("(k p) n -> p k n", p=P)).then_inc(consts, 16)
            with sp.Fori(0, B) as i:
                for ch in range(NCH):
                    s.hold(sp, t_full, Z + i * NCH * KD)
                    sp.dma_start(xn[:, ch, :, :], rows(a["s_n3"], i * L + ch * CH, CH)).then_inc(xn_in[ch], 16)
                    s.hold(sp, x_out[ch], Z + i * 16)
                    sp.dma_start(x[:, ch, :, :], rows(a["s_x3"], i * L + ch * CH, CH)).then_inc(x_in[ch], 16)
                for ch in range(NCH):
                    g = i * NCH + ch
                    s.hold(sp, v_read, Z + g * V_JOBS + NV + 2)
                    sp.dma_start(a["s_lg"][:, bass.ds(g * (TT * E), TT * E)], lg[:, ch, :, :].rearrange("p t e -> p (t e)")).then_inc(lg_out[ch], 16)
                    s.hold(sp, v_read, Z + (g + 1) * V_JOBS + NV)
                    sp.dma_start(rows(a["s_x4"], i * L + ch * CH, CH), x[:, ch, :, :]).then_inc(x_out[ch], 16)
            for ch in range(NCH):
                sp.wait_ge(x_out[ch], Z + B * 16)
                sp.wait_ge(lg_out[ch], Z + B * 16)

        @block.tensor
        def _(pe):
            pe.wait_ge(consts, Z + 80)
            with pe.Fori(0, B) as i:
                for ch in range(NCH):
                    g = i * NCH + ch
                    pe.wait_ge(xn_in[ch], Z + (i + 1) * 16)
                    for k in range(KD):
                        pe.wait_ge(t_read, Z + g * KD + k + 1)
                        for t in range(TT):
                            last = nc.tensor.transpose(ps_t[:, k % NT, t * P:(t + 1) * P], xn[:, ch, t, k * P:(k + 1) * P], ident[:, :])
                        last.then_inc(t_full, 1)
                    pe.wait_ge(t_read, Z + (g + 1) * KD + NT)
                    for t in range(TT):
                        if t % 2 == 0:
                            pe.wait_ge(v_read, Z + g * V_JOBS + t // 2 + 1)
                        for k in range(KD):
                            last = nc.tensor.matmul(ps_v[:, t // 2, (t % 2) * E:(t % 2 + 1) * E], xT[:, k, t * P:(t + 1) * P], cent[:, k, :],
                                                    start=(k == 0), stop=(k == KD - 1))
                        if t % 2:
                            last.then_inc(v_full, 1)
                    for m in range(KS):
                        for n, wt in enumerate((wg, wu)):
                            if n == 0:
                                pe.wait_ge(h_ok, Z + g * KS + m + 1)
                            for k in range(KD):
                                last = nc.tensor.matmul(ps_g[:, (2 * m + n) % NG, :], wt[:, k, m * P:(m + 1) * P], xT[:, k, :],
                                                        start=(k == 0), stop=(k == KD - 1))
                            last.then_inc(g_full, 1)
                    pe.wait_ge(h_ok, Z + (g + 1) * KS + 2)
                    for t in range(TT):
                        pe.wait_ge(v_read, Z + g * V_JOBS + 2 + t + 1)
                        for k in range(KS):
                            last = nc.tensor.matmul(ps_v[:, t % NV, :], hT[:, k, t * P:(t + 1) * P], wd[:, k, :],
                                                    start=(k == 0), stop=(k == KS - 1))
                        last.then_inc(v_full, 1)

        @block.scalar
        def _(act):
            with act.Fori(0, B) as i:
                for ch in range(NCH):
                    g = i * NCH + ch
                    for m in range(KS):
                        act.wait_ge(g_full, Z + g * 2 * KS + 2 * m + 1)
                        act.wait_ge(h_ok, Z + g * KS + m + 1)
                        nc.scalar.activation(sg[:, m % 2, :], ps_g[:, 2 * m % NG, :], ACT.Silu).then_inc(silu_ok, 1)

        @block.vector
        def _(dve):
            nc.vector.nop().then_inc(t_read, NT)
            nc.vector.nop().then_inc(h_ok, 2)
            nc.vector.nop().then_inc(v_read, NV)
            with dve.Fori(0, B) as i:
                for ch in range(NCH):
                    g = i * NCH + ch
                    dve.wait_ge(g_full, Z + g * 2 * KS)
                    for k in range(KD):
                        dve.wait_ge(t_full, Z + g * KD + k + 1)
                        nc.vector.tensor_copy(xT[:, k, :], ps_t[:, k % NT, :]).then_inc(t_read, 1)
                    dve.wait_ge(lg_out[ch], Z + i * 16)
                    for t in range(2):
                        dve.wait_ge(v_full, Z + g * V_JOBS + t + 1)
                        nc.vector.tensor_copy(lg[:, ch, 2 * t:2 * t + 2, :].rearrange("p t e -> p (t e)"), ps_v[:, t, 0:2 * E]).then_inc(v_read, 1)
                    dve.wait_ge(v_full, Z + g * V_JOBS)
                    for m in range(KS):
                        dve.wait_ge(silu_ok, Z + g * KS + m + 1)
                        dve.wait_ge(g_full, Z + g * 2 * KS + 2 * m + 2)
                        nc.vector.tensor_tensor(hT[:, m, :], sg[:, m % 2, :], ps_g[:, (2 * m + 1) % NG, :], ALU.mult).then_inc(h_ok, 1)
                    dve.wait_ge(x_in[ch], Z + (i + 1) * 16)
                    for t in range(TT):
                        dve.wait_ge(v_full, Z + g * V_JOBS + 2 + t + 1)
                        nc.vector.scalar_tensor_tensor(out=x[:, ch, t, :], in0=ps_v[:, t % NV, :], scalar=RATIO, in1=x[:, ch, t, :],
                                                       op0=ALU.mult, op1=ALU.add).then_inc(v_read, 1)


def route_tokens(nc, a):
    NTE = TOK_TILES * E
    K256 = T // SLOT_TILE
    with Scope(nc, "route") as s:
        lg = s.sb("lg", [P, TOK_TILES, E])
        gb = s.sb("gb", [P, E])
        rev = s.sb("rev", [P, E])
        full_at = s.sb("full_at", [P, K256])
        tile_no = s.sb("tile_no", [P, N_TILES])
        earlier = s.sb("earlier", [P, P])
        ones = s.sb("ones", [P, P])
        aff = s.sb("aff", [P, TOK_TILES, E])
        cand = s.sb("cand", [P, TOK_TILES, E])
        tmp = s.sb("tmp", [P, TOK_TILES, E])
        one = s.sb("one", [P, TOPK, TOK_TILES, E])
        both = s.sb("both", [P, TOK_TILES, E])
        top = s.sb("top", [P, TOK_TILES])
        ta = s.sb("ta", [P, TOPK, TOK_TILES])
        wsum = s.sb("wsum", [P, TOK_TILES])
        wt = s.sb("wt", [P, TOPK, TOK_TILES])
        run = s.sb("run", [P, 2, TOK_TILES, E])
        pos = s.sb("pos", [P, TOK_TILES, E])
        cmp = s.sb("cmp", [P, E, K256])
        tiles = s.sb("tiles", [P, E])
        cum = s.sb("cum", [P, 2, E])
        base = s.sb("base", [P, E])
        cmp_t = s.sb("cmp_t", [P, N_TILES, E])
        ex_f = s.sb("ex_f", [P, N_TILES])
        ex_i = s.sb("ex_i", [P, N_TILES], I32)
        slot = s.sb("slot", [P, TOPK, TOK_TILES])
        slot_i = s.sb("slot_i", [P, TOPK, TOK_TILES], I32)
        xn = s.sb("xn", [P, TOK_TILES, D])
        ps_w = s.ps("ps_w", [P, 512])
        ps_n = s.ps("ps_n", [P, 512])
        loads, xn_in, clamp_ok, exp_ok, both_ok, pref_ok, st, out_ok, outs = (s.sem(n) for n in (
            "loads", "xn_in", "clamp_ok", "exp_ok", "both_ok", "pref_ok", "st", "out_ok", "outs"))
        sent = s.pool_dma_sem("sent")
        block = s.block()

        @block.sync
        def _(sp):
            sp.dma_start(lg[:, :, :].rearrange("p t e -> p (t e)"), a["s_lg"]).then_inc(loads, 16)
            sp.dma_start(gb[:, :], a["gate_b"].to_broadcast([P, E])).then_inc(loads, 16)
            sp.dma_start(rev[:, :], a["c_rev"].to_broadcast([P, E])).then_inc(loads, 16)
            sp.dma_start(full_at[:, :], a["c_full_at"].to_broadcast([P, K256])).then_inc(loads, 16)
            sp.dma_start(tile_no[:, :], a["c_tile_no"].to_broadcast([P, N_TILES])).then_inc(loads, 16)
            sp.dma_start(earlier[:, :], a["c_before"]).then_inc(loads, 16)
            sp.dma_start(ones[:, :], a["c_ones"]).then_inc(loads, 16)
            sp.dma_start(xn[:, :, :], rows(a["s_n3"], 0, T)).then_inc(xn_in, 16)
            sp.wait_ge(out_ok, Z + 2)
            sp.dma_start(a["s_expert"], ex_i[0:1, :]).then_inc(outs, 16)
            sp.dma_start(a["s_slot"], slot_i[:, :, :].rearrange("p k t -> p (k t)")).then_inc(outs, 16)
            sp.dma_start(a["s_wt"], wt[:, :, :].rearrange("p k t -> p (k t)")).then_inc(outs, 16)
            sp.wait_ge(outs, Z + 48)

        @block.scalar
        def _(act):
            act.wait_ge(clamp_ok, Z + 1)
            nc.scalar.activation(aff[:, :, :], lg[:, :, :], ACT.Exp, scale=-1.0).then_inc(exp_ok, 1)

        @block.tensor
        def _(pe):
            pe.wait_ge(loads, Z + 7 * 16)
            pe.wait_ge(both_ok, Z + 1)
            m = both[:, :, :].rearrange("p t e -> p (t e)")
            nc.tensor.matmul(ps_w[:, 0:NTE], earlier[:, :], m, start=True, stop=True)
            nc.tensor.matmul(ps_n[:, 0:NTE], ones[:, :], m, start=True, stop=True).then_inc(pref_ok, 1)

        @block.vector
        def _(dve):
            steps = [0]

            def after(ins):
                steps[0] += 1
                ins.then_inc(st, 1)
                dve.wait_ge(st, Z + steps[0])

            v = nc.vector
            shape = [P, TOK_TILES, E]
            per_token = lambda x: x.unsqueeze(2).to_broadcast(shape)
            per_expert = lambda x: x.unsqueeze(1).to_broadcast(shape)
            dve.wait_ge(loads, Z + 7 * 16)
            v.tensor_scalar(lg[:, :, :], lg[:, :, :], -87.0, None, ALU.max).then_inc(clamp_ok, 1)
            dve.wait_ge(exp_ok, Z + 1)
            after(v.tensor_scalar(aff[:, :, :], aff[:, :, :], 1.0, None, ALU.add))
            after(v.reciprocal(aff[:, :, :], aff[:, :, :]))
            after(v.tensor_tensor(cand[:, :, :], aff[:, :, :], per_expert(gb[:, :]), ALU.add))
            for k in range(TOPK):
                after(v.tensor_reduce(top[:, :], cand[:, :, :], AX.X, ALU.max))
                after(v.tensor_tensor(tmp[:, :, :], cand[:, :, :], per_token(top[:, :]), ALU.is_equal))
                after(v.tensor_tensor(tmp[:, :, :], tmp[:, :, :], per_expert(rev[:, :]), ALU.mult))
                after(v.tensor_reduce(top[:, :], tmp[:, :, :], AX.X, ALU.max))
                after(v.tensor_tensor(one[:, k, :, :], per_expert(rev[:, :]), per_token(top[:, :]), ALU.is_equal))
                after(v.tensor_tensor(tmp[:, :, :], one[:, k, :, :], aff[:, :, :], ALU.mult))
                after(v.tensor_reduce(ta[:, k, :], tmp[:, :, :], AX.X, ALU.add))
                if k == 0:
                    after(v.scalar_tensor_tensor(out=cand[:, :, :], in0=one[:, 0, :, :], scalar=-3.0e38, in1=cand[:, :, :],
                                                 op0=ALU.mult, op1=ALU.add))
            v.tensor_tensor(both[:, :, :], one[:, 0, :, :], one[:, 1, :, :], ALU.add).then_inc(both_ok, 1)
            after(v.tensor_tensor(wsum[:, :], ta[:, 0, :], ta[:, 1, :], ALU.add))
            after(v.tensor_scalar(wsum[:, :], wsum[:, :], RT_EPS, None, ALU.add))
            after(v.reciprocal(wsum[:, :], wsum[:, :]))
            after(v.tensor_tensor(wt[:, :, :], ta[:, :, :], wsum[:, :].unsqueeze(1).to_broadcast([P, TOPK, TOK_TILES]), ALU.mult))
            dve.wait_ge(pref_ok, Z + 1)
            after(v.tensor_copy(run[:, 0, :, :].rearrange("p t e -> p (t e)"), ps_n[:, 0:NTE]))
            src, width = 0, 1
            while width < TOK_TILES:
                after(v.tensor_copy(run[:, 1 - src, 0:width, :], run[:, src, 0:width, :]))
                after(v.tensor_tensor(run[:, 1 - src, width:, :], run[:, src, width:, :], run[:, src, 0:TOK_TILES - width, :], ALU.add))
                src, width = 1 - src, 2 * width
            total = run[:, src, TOK_TILES - 1, :]
            after(v.tensor_tensor(cmp[:, :, :], total.unsqueeze(2).to_broadcast([P, E, K256]),
                                  full_at[:, :].unsqueeze(1).to_broadcast([P, E, K256]), ALU.is_gt))
            after(v.tensor_reduce(tiles[:, :], cmp[:, :, :], AX.X, ALU.add))
            after(v.tensor_copy(cum[:, 0, :], tiles[:, :]))
            cs, width = 0, 1
            while width < E:
                after(v.tensor_copy(cum[:, 1 - cs, 0:width], cum[:, cs, 0:width]))
                after(v.tensor_tensor(cum[:, 1 - cs, width:], cum[:, cs, width:], cum[:, cs, 0:E - width], ALU.add))
                cs, width = 1 - cs, 2 * width
            after(v.tensor_tensor(base[:, :], cum[:, cs, :], tiles[:, :], ALU.subtract))
            after(v.tensor_scalar(base[:, :], base[:, :], float(SLOT_TILE), None, ALU.mult))
            after(v.tensor_tensor(pos[:, :, :].rearrange("p t e -> p (t e)"), ps_w[:, 0:NTE],
                                  run[:, src, :, :].rearrange("p t e -> p (t e)"), ALU.add))
            after(v.tensor_tensor(pos[:, :, :].rearrange("p t e -> p (t e)"), pos[:, :, :].rearrange("p t e -> p (t e)"),
                                  ps_n[:, 0:NTE], ALU.subtract))
            after(v.tensor_tensor(pos[:, :, :], pos[:, :, :], per_expert(base[:, :]), ALU.add))
            for k in range(TOPK):
                after(v.tensor_tensor(tmp[:, :, :], one[:, k, :, :], pos[:, :, :], ALU.mult))
                after(v.tensor_reduce(slot[:, k, :], tmp[:, :, :], AX.X, ALU.add))
            v.tensor_copy(slot_i[:, :, :], slot[:, :, :]).then_inc(out_ok, 1)
            after(v.tensor_tensor(cmp_t[:, :, :], cum[:, cs, :].unsqueeze(1).to_broadcast([P, N_TILES, E]),
                                  tile_no[:, :].unsqueeze(2).to_broadcast([P, N_TILES, E]), ALU.is_le))
            after(v.tensor_reduce(ex_f[:, :], cmp_t[:, :, :], AX.X, ALU.add))
            after(v.tensor_scalar(ex_f[:, :], ex_f[:, :], float(E - 1), None, ALU.min))
            v.tensor_copy(ex_i[:, :], ex_f[:, :]).then_inc(out_ok, 1)

        @block.gpsimd
        def _(pool):
            pool.wait_ge(xn_in, Z + 16)
            pool.wait_ge(out_ok, Z + 1)
            for k in range(TOPK):
                for j in range(TOK_TILES):
                    nc.gpsimd.indirect_dma_start(a["s_xs"], bass.IndirectOffsetOnAxis(ap=slot_i[:, k, j:j + 1].bitcast(U32), axis=0),
                                                 xn[:, j, :], None).then_inc(sent, 16)
            pool.wait_ge(sent, 16 * TOPK * TOK_TILES)


def experts(nc, a):
    ST = SLOT_TILE // P
    KI = I_E // P
    W = 2
    with Scope(nc, "moe") as s:
        ex = s.sb("ex", [1, N_TILES], I32)
        ident = s.sb("ident", [P, P])
        wg = s.sb("wg", [P, W, KD, I_E])
        wu = s.sb("wu", [P, W, KD, I_E])
        wd = s.sb("wd", [P, W, KI, D])
        xs = s.sb("xs", [P, W, ST, D])
        xT = s.sb("xT", [P, W, KD, SLOT_TILE])
        sg = s.sb("sg", [P, W, KI * SLOT_TILE])
        hT = s.sb("hT", [P, W, KI, SLOT_TILE])
        y = s.sb("y", [P, W, ST, D])
        ps_t = s.ps("ps_t", [P, 2, 2, SLOT_TILE])
        ps_g = s.ps("ps_g", [P, 2, KI * SLOT_TILE])
        ps_u = s.ps("ps_u", [P, 2, KI * SLOT_TILE])
        ps_y = s.ps("ps_y", [P, ST, D])
        consts, ex_in, t_full, t_read, g_full, u_full, silu_ok, h_ok, y_full, y_read = (s.sem(n) for n in (
            "consts", "ex_in", "t_full", "t_read", "g_full", "u_full", "silu_ok", "h_ok", "y_full", "y_read"))
        w_in, x_in, y_out = (s.sems(n, W) for n in ("w_in", "x_in", "y_out"))
        block = s.block()
        PAIRS = N_TILES // W

        @block.sync
        def _(sp):
            def load_x(j, w):
                sp.dma_start(xs[:, w, :, :], rows(a["s_xs"], j * SLOT_TILE, SLOT_TILE)).then_inc(x_in[w], 16)

            def load_w(j, w):
                e = sp.value_load(ex[0:1, bass.ds(j, 1)], min_val=0, max_val=E - 1)
                for dst, name in ((wg, "wg"), (wu, "wu"), (wd, "wd")):
                    sp.dma_start(dst[:, w, :, :], a[name][bass.ds(e, 1), :, :].rearrange("e (k p) n -> p (e k) n", p=P)).then_inc(w_in[w], 16)

            def store(j, w):
                s.hold(sp, y_read, Z + (j + 1) * ST + ST)
                sp.dma_start(rows(a["s_ys"], j * SLOT_TILE, SLOT_TILE), y[:, w, :, :]).then_inc(y_out[w], 16)

            def load_after(j, w):
                s.hold(sp, t_full, Z + (j + 1) * 2)
                load_x(j + W, w)
                s.hold(sp, y_full, Z + (j + 1) * ST)
                load_w(j + W, w)

            sp.dma_start(ident[:, :], a["c_ident"]).then_inc(consts, 16)
            sp.dma_start(ex[:, :], a["s_expert"]).then_inc(ex_in, 16)
            for w in range(W):
                load_x(w, w)
            sp.wait_ge(ex_in, Z + 16)
            for w in range(W):
                load_w(w, w)
            with sp.Fori(0, PAIRS - 1) as i:
                for w in range(W):
                    load_after(i * W + w, w)
                    store(i * W + w, w)
            for j in range((PAIRS - 1) * W, N_TILES):
                if j + W < N_TILES:
                    load_after(j, j % W)
                store(j, j % W)
            for w in range(W):
                sp.wait_ge(y_out[w], Z + (N_TILES - w + 1) // W * 16)

        @block.tensor
        def _(pe):
            def turn(j, w, n):
                pe.wait_ge(x_in[w], Z + (n + 1) * 16)
                for kk in range(2):
                    pe.wait_ge(t_read, Z + j * 2 + kk + 1)
                    for k in range(2):
                        for t in range(ST):
                            last = nc.tensor.transpose(ps_t[:, kk, k, t * P:(t + 1) * P],
                                                       xs[:, w, t, (2 * kk + k) * P:(2 * kk + k + 1) * P], ident[:, :])
                    last.then_inc(t_full, 1)

            def step(j, w, n, more):
                pe.wait_ge(t_read, Z + (j + 1) * 2 + 2)
                pe.wait_ge(w_in[w], Z + (n + 1) * 48)
                pe.wait_ge(h_ok, Z + j + 1)
                for ps, wt, done in ((ps_g, wg, g_full), (ps_u, wu, u_full)):
                    for m in range(KI):
                        for k in range(KD):
                            last = nc.tensor.matmul(ps[:, w, m * SLOT_TILE:(m + 1) * SLOT_TILE], wt[:, w, k, m * P:(m + 1) * P],
                                                    xT[:, w, k, :], start=(k == 0), stop=(k == KD - 1))
                    last.then_inc(done, 1)
                if more:
                    turn(j + 1, 1 - w, n + w)
                pe.wait_ge(h_ok, Z + j + 1 + W)
                for t in range(ST):
                    pe.wait_ge(y_read, Z + j * ST + t + 1)
                    for m in range(KI):
                        last = nc.tensor.matmul(ps_y[:, t, :], hT[:, w, m, t * P:(t + 1) * P], wd[:, w, m, :],
                                                start=(m == 0), stop=(m == KI - 1))
                    last.then_inc(y_full, 1)

            pe.wait_ge(consts, Z + 16)
            turn(0, 0, 0)
            with pe.Fori(0, PAIRS) as i:
                for w in range(W):
                    step(i * W + w, w, i, True)
            step(N_TILES - 1, 0, PAIRS, False)

        @block.scalar
        def _(act):
            def step(j, w, n):
                act.wait_ge(g_full, Z + j + 1)
                act.wait_ge(h_ok, Z + j + 1)
                nc.scalar.activation(sg[:, w, :], ps_g[:, w, :], ACT.Silu).then_inc(silu_ok, 1)
                act.wait_ge(y_out[w], Z + n * 16)
                for t in range(ST):
                    act.wait_ge(y_full, Z + j * ST + t + 1)
                    nc.scalar.copy(y[:, w, t, :], ps_y[:, t, :]).then_inc(y_read, 1)

            nc.scalar.nop().then_inc(y_read, ST)
            with act.Fori(0, PAIRS) as i:
                for w in range(W):
                    step(i * W + w, w, i)
            step(N_TILES - 1, 0, PAIRS)

        @block.vector
        def _(dve):
            def turned(j, w):
                if not isinstance(j, int) or j >= 1:
                    dve.wait_ge(u_full, Z + j - 1)
                for kk in range(2):
                    dve.wait_ge(t_full, Z + j * 2 + kk + 1)
                    nc.vector.tensor_copy(xT[:, w, 2 * kk:2 * kk + 2, :], ps_t[:, kk, :, :]).then_inc(t_read, 1)

            def step(j, w, more):
                dve.wait_ge(silu_ok, Z + j + 1)
                dve.wait_ge(u_full, Z + j + 1)
                nc.vector.tensor_tensor(hT[:, w, :, :].rearrange("p m t -> p (m t)"), sg[:, w, :], ps_u[:, w, :],
                                        ALU.mult).then_inc(h_ok, 1)
                if more:
                    turned(j + 1, 1 - w)

            nc.vector.nop().then_inc(t_read, 2)
            nc.vector.nop().then_inc(h_ok, W)
            turned(0, 0)
            with dve.Fori(0, PAIRS) as i:
                for w in range(W):
                    step(i * W + w, w, True)
            step(N_TILES - 1, 0, False)


def combine(nc, a):
    with Scope(nc, "end") as s:
        slot = s.sb("slot", [P, TOPK, TOK_TILES], I32)
        wt = s.sb("wt", [P, TOPK, TOK_TILES])
        got = s.sb("got", [P, TOPK, TOK_TILES, D])
        x = s.sb("x", [P, TOK_TILES, D])
        slot_in, wt_in, add_ok, out_sent = (s.sem(n) for n in ("slot_in", "wt_in", "add_ok", "out_sent"))
        x_in = s.sems("x_in", NCH * B)
        got_in = [s.pool_dma_sem(f"got_in{j}") for j in range(TOK_TILES)]
        block = s.block()

        @block.sync
        def _(sp):
            sp.dma_start(slot[:, :, :].rearrange("p k t -> p (k t)"), a["s_slot"]).then_inc(slot_in, 16)
            sp.dma_start(wt[:, :, :].rearrange("p k t -> p (k t)"), a["s_wt"]).then_inc(wt_in, 16)
            for g in range(NCH * B):
                sp.dma_start(x[:, g * TT:(g + 1) * TT, :], rows(a["s_x4"], g * CH, CH)).then_inc(x_in[g], 16)
            for g in range(NCH * B):
                sp.wait_ge(add_ok, Z + (g + 1) * TT * TOPK)
                sp.dma_start(rows(a["out"], g * CH, CH), x[:, g * TT:(g + 1) * TT, :]).then_inc(out_sent, 16)
            sp.wait_ge(out_sent, Z + NCH * B * 16)

        @block.gpsimd
        def _(pool):
            pool.wait_ge(slot_in, Z + 16)
            for j in range(TOK_TILES):
                for k in range(TOPK):
                    nc.gpsimd.indirect_dma_start(got[:, k, j, :], None, a["s_ys"],
                                                 bass.IndirectOffsetOnAxis(ap=slot[:, k, j:j + 1].bitcast(U32), axis=0)).then_inc(got_in[j], 16)

        @block.vector
        def _(dve):
            dve.wait_ge(wt_in, Z + 16)
            for j in range(TOK_TILES):
                if j % TT == 0:
                    dve.wait_ge(x_in[j // TT], Z + 16)
                dve.wait_ge(got_in[j], TOPK * 16)
                for k in range(TOPK):
                    if k:
                        dve.wait_ge(add_ok, Z + j * TOPK + k)
                    nc.vector.scalar_tensor_tensor(out=x[:, j, :], in0=got[:, k, j, :], scalar=wt[:, k, j:j + 1], in1=x[:, j, :],
                                                   op0=ALU.mult, op1=ALU.add).then_inc(add_ok, 1)


SCRATCH = {
    "s_b": ((P, T), F32), "s_c": ((3, NC_T, P, T), BF16),
    "s_delta": ((NC_T, P, T), F32), "s_du": ((NC_T, P, T), F32),
    "s_x1": ((T, D), F32), "s_n1": ((T, D), F32), "s_x2": ((T, D), F32),
    "s_score": ((P, TOK_TILES), F32), "s_score_row": ((1, T), F32), "s_dest": ((P, TOK_TILES), I32),
    "s_sel_in": ((T, D), F32), "s_sel_out": ((T, D), F32),
    "s_q": ((NHG, P, T), F32), "s_k": ((NHG, P, T), F32), "s_v": ((T, NH * (HD + 1)), F32),
    "s_xs": ((N_TILES * SLOT_TILE, D), F32), "s_ys": ((N_TILES * SLOT_TILE, D), F32),
    "s_o": ((T, D), F32), "s_x3": ((T, D), F32), "s_n3": ((T, D), F32), "s_x4": ((T, D), F32),
    "s_expert": ((1, N_TILES), I32), "s_slot": ((P, TOPK * TOK_TILES), I32), "s_wt": ((P, TOPK * TOK_TILES), F32),
    "s_lg": ((P, TOK_TILES * E), F32),
    "s_y": ((NC_T, P, T), F32),
    "s_u": ((NC_T, P, T), F32), "s_z": ((NC_T, P, T), F32),
}
PHASES = [project_in, selective_scan, mix_out, rank_tokens, select_ffn, attend_in,
          attend, attend_out, shared_ffn,
          route_tokens, experts, combine]


def build(nc, a):
    for phase in PHASES:
        phase(nc, a)


def layout(inputs):
    import numpy as np

    v = {k: np.asarray(x) for k, x in inputs.items()}
    per_channel = lambda x: np.ascontiguousarray(x.reshape(NC_T, P, *x.shape[1:]).swapaxes(0, 1))
    w = v["L0_attn_W_in"]
    z, x, bm, cm, dtl = np.split(w, np.cumsum([D_INNER, P, P, D_INNER]), axis=0)
    cm = cm.reshape(NC_T, GPT, N_QUAD, 4, D).transpose(0, 2, 3, 1, 4).reshape(D_INNER, D)
    out = {
        "x": v["L0_attn_hidden_states"].reshape(T, D),
        "w_in": np.ascontiguousarray(np.concatenate([z, cm, dtl, x, bm]).T),
        "w_dt": np.ascontiguousarray(v["L0_attn_W_dt"].T),
        "b_dt": per_channel(v["L0_attn_b_dt"]),
        "conv_w": per_channel(v["L0_attn_conv_w"][:, 0, :]),
        "conv_b": per_channel(v["L0_attn_conv_b"]),
        "a_log": per_channel(v["L0_attn_A_log"]),
        "d_param": per_channel(v["L0_attn_D_param"]),
        "w_out": np.ascontiguousarray(v["L0_attn_W_out"].T),
        "w_r": v["L0_ffn_w_r"].reshape(1, D),
        "b_r": v["L0_ffn_b_r"].reshape(1, 1),
        "w1": v["L0_ffn_w1"],
        "b1": np.ascontiguousarray(v["L0_ffn_b1"].reshape(KF, P).T),
        "w2": v["L0_ffn_w2"],
        "b2": v["L0_ffn_b2"].reshape(1, D),
        "w_qkv": np.ascontiguousarray(v["L1_attn_w_project"].T),
        "w_o": np.ascontiguousarray(v["L1_attn_w_out"].T),
        "cent": np.ascontiguousarray(v["L1_ffn_centroids"].T),
        "gate_b": v["L1_ffn_gate_bias"].reshape(1, E),
        "wg_s": v["L1_ffn_wg_s"], "wu_s": v["L1_ffn_wu_s"], "wd_s": v["L1_ffn_wd_s"],
        "wg": v["L1_ffn_wg"], "wu": v["L1_ffn_wu"], "wd": v["L1_ffn_wd"],
    }
    p = np.arange(P)
    out["c_ident"] = np.eye(P, dtype=np.float32)
    rep = np.zeros((P, NC_T, P), np.float32)
    for c in range(NC_T):
        rep[16 * c + p % 16, c, p] = 1
    out["c_rep"] = rep
    sel = np.zeros((3, 4, GPT, 4, P), np.float32)
    for n in range(4):
        for g in range(GPT):
            sel[:, n, g, n, 16 * g:16 * g + 16] = 1
    out["c_sel"] = sel.reshape(C_ROWS, 4, P)
    mask = np.zeros((P, L), np.float32)
    mask[:, L - P:] = np.where(p[None, :] > p[:, None], np.float32(NEG), np.float32(0))
    out["c_mask"] = mask
    out["c_earlier"] = (p[None, :] < p[:, None]).astype(np.float32)
    out["c_before"] = (p[:, None] < p[None, :]).astype(np.float32)
    out["c_rev"] = (E - np.arange(E, dtype=np.float32)).reshape(1, E)
    out["c_full_at"] = (SLOT_TILE * np.arange(T // SLOT_TILE, dtype=np.float32)).reshape(1, -1)
    out["c_tile_no"] = np.arange(N_TILES, dtype=np.float32).reshape(1, -1)
    out["c_ones"] = np.ones((P, P), np.float32)
    return out


def kernel(**inputs):
    import numpy as _np
    import concourse.bacc as _bacc
    from concourse import mybir as _mybir
    from concourse.bass_utils import run_bass_kernel_spmd as _run

    nc = _bacc.Bacc("TRN2", target_bir_lowering=False, num_devices=1)
    arrays, args = {}, {}
    for name, arr in layout(inputs).items():
        arrays[f"in_{name}"] = arr
        args[name] = nc.dram_tensor(f"in_{name}", arr.shape, _mybir.dt.from_np(arr.dtype), kind="ExternalInput").ap()
    for name, (shape, dt) in SCRATCH.items():
        args[name] = nc.dram_tensor(name, shape, dt).ap()
    args["out"] = nc.dram_tensor("out_0_dram", (T, D), F32, kind="ExternalOutput").ap()
    build(nc, args)
    r = _run(nc, [arrays], core_ids=[0])
    return r.results[0]["out_0_dram"].reshape(B, L, D)
```

```python
from contextlib import ExitStack

import concourse.bass as bass
from concourse import mybir

F32 = mybir.dt.float32
F32R = mybir.dt.float32r
BF16 = mybir.dt.bfloat16
I32 = mybir.dt.int32
U32 = mybir.dt.uint32
ALU = mybir.AluOpType
ACT = mybir.ActivationFunctionType
AX = mybir.AxisListType

P = 128
B, L, D = 2, 1024, 512
T = B * L
KD = D // P
CH = 512
NCH = L // CH
TT = CH // P
EPS = 1e-5
Z = 1

D_INNER, D_STATE, D_CONV = 1024, 16, 4
NC_T = D_INNER // P
GPT = P // D_STATE
M_IN = 3 * NC_T
HALO = D_CONV - 1
C_ROWS = 3 * 32
N_QUAD = D_STATE // 4

DF = 2048
KF = DF // P
K_SEL = L // 2

NH, HD = 16, 32
HG = P // HD
NHG = NH // HG
NQT = L // P
NEG = -1.0e9

E, TOPK, I_E = 16, 2, 256
I_SH = 512
RATIO = 0.1
RT_EPS = 1e-9
SLOT_TILE = 256
N_TILES = (T * TOPK) // SLOT_TILE + E - 1
TOK_TILES = T // P


class Scope:

    def __init__(self, nc, name):
        self.nc, self.name, self.stack, self.held = nc, name, ExitStack(), []
        self.at_zero = []

    def __enter__(self):
        self.stack.__enter__()
        return self

    def __exit__(self, *a):
        self.stack.__exit__(*a)
        self.nc.clear_and_free_semaphores(self.held)

    def sb(self, name, shape, dt=F32):
        return self.stack.enter_context(self.nc.sbuf_tensor(f"{self.name}_{name}", shape, dt))

    def ps(self, name, shape, dt=F32):
        return self.stack.enter_context(self.nc.psum_tensor(f"{self.name}_{name}", shape, dt))

    def sem(self, name):
        self.held.append(self.nc.alloc_semaphore(name=f"{self.name}_{name}"))
        return self.held[-1]

    def pool_dma_sem(self, name):
        self.at_zero.append(self.sem(name))
        return self.at_zero[-1]

    def sems(self, name, n):
        return [self.sem(f"{name}{i}") for i in range(n)]

    def block(self):
        self.passed = self.sem("passed")
        for sem in self.held:
            if sem not in self.at_zero:
                self.nc.gpsimd.sem_inc(sem, Z)
        self.nc.all_engine_barrier()
        return self.stack.enter_context(self.nc.Block())

    def hold(self, eng, sem, value):
        eng.wait_ge(sem, value)
        eng.sem_inc(self.passed, 1)


def rows(ap, start, n):
    return ap[bass.ds(start, n), :].rearrange("(t p) n -> p t n", p=P)


def cols(ap, start, n):
    return ap[:, :, bass.ds(start, n)].rearrange("c p t -> p c t")



def exact_product(nc, dst, lhs, rhs):
    parts = [(l[m].bitcast(F32R), r[n].bitcast(F32R)) for l, r in zip(lhs, rhs) for m, n in ((0, 0), (0, 1), (1, 0))]
    for i, (l, r) in enumerate(parts):
        last = nc.tensor.matmul(dst, l, r, start=(i == 0), stop=(i == len(parts) - 1))
    return last


def project_in(nc, a):
    M_Z, M_C, M_DT, M_X, M_B = 0, NC_T, 2 * NC_T, 2 * NC_T + 1, 2 * NC_T + 2
    NT, NV, NA = 2, 2, 4
    T_JOBS, V_JOBS, A_JOBS = KD, NC_T + 1, 2 + 3 * NC_T
    J_DT, J_XR, J_Z = 2, 2 + NC_T, 2 + 2 * NC_T
    N_CONST = 6
    with Scope(nc, "proj") as s:
        w_in = s.sb("w_in", [P, KD, (M_B + 1) * P])
        w_dt = s.sb("w_dt", [P, D_INNER])
        ident = s.sb("ident", [P, P])
        rep = s.sb("rep", [P, NC_T, P])
        bdt = s.sb("bdt", [P, NC_T])
        bdt2 = s.sb("bdt2", [P, NC_T])
        cw = s.sb("cw", [P, NC_T, D_CONV])
        cb = s.sb("cb", [P, NC_T])
        x = s.sb("x", [P, NCH, TT, D])
        stats = s.sb("stats", [P, NCH, TT, 6])
        mv = s.sb("mv", [P, NCH, TT, 2])
        std = s.sb("std", [P, NCH, TT])
        rstd = s.sb("rstd", [P, NCH, TT])
        xnT = s.sb("xnT", [P, NCH, KD, CH])
        dtl_x = s.sb("dtl_x", [P, 2, CH])
        xr = s.sb("xr", [P, NC_T, HALO + CH])
        conv = s.sb("conv", [P, NC_T, CH])
        dt_x = s.sb("dt_x", [P, NC_T, CH])
        dt_e = s.sb("dt_e", [P, NC_T, CH])
        dt_l = s.sb("dt_l", [P, NC_T, CH])
        dt_d = s.sb("dt_d", [P, NC_T, CH])
        c_hi = s.sb("c_hi", [P, 2, CH], BF16)
        c_res = s.sb("c_res", [P, 2, CH])
        c_mid = s.sb("c_mid", [P, 2, CH], BF16)
        c_lo = s.sb("c_lo", [P, 2, CH], BF16)
        z = s.sb("z", [P, 2, CH])
        bT = s.sb("bT", [P, CH])

        ps_t = s.ps("ps_t", [P, NT, CH])
        ps_v = s.ps("ps_v", [P, NV, CH])
        ps_a = s.ps("ps_a", [P, NA, CH])

        consts, stats_ok, mv_ok, std_ok, rstd_ok, xn_ok = (s.sem(n) for n in (
            "consts", "stats_ok", "mv_ok", "std_ok", "rstd_ok", "xn_ok"))
        x_in = s.sems("x_in", NCH)
        t_full, t_read, v_full, v_read, a_full, a_read = (s.sem(n) for n in (
            "t_full", "t_read", "v_full", "v_read", "a_full", "a_read"))
        hi_ok, mid_ok, lo_ok = (s.sem(n) for n in ("hi_ok", "mid_ok", "lo_ok"))
        halo_ok, bdt2_ok, conv_step, u_ok = (s.sem(n) for n in ("halo_ok", "bdt2_ok", "conv_step", "u_ok"))
        abs_ok, exp_ok, ln_ok, sp_step, delta_ok, du_ok = (s.sem(n) for n in (
            "abs_ok", "exp_ok", "ln_ok", "sp_step", "delta_ok", "du_ok"))
        c_out, z_out = s.sems("c_out", 2), s.sems("z_out", 2)
        w_ok = s.sems("w_ok", 3)
        b_out, u_out, delta_out, du_out = (s.sem(n) for n in ("b_out", "u_out", "delta_out", "du_out"))
        block = s.block()
        SP_STEPS = 4

        @block.sync
        def _(sp):
            sp.dma_start(x[:, 0, :, :], rows(a["x"], 0, CH)).then_inc(x_in[0], 16)
            for dst, name in ((ident[:, :], "c_ident"), (w_dt[:, :], "w_dt"), (rep[:, :, :], "c_rep"),
                              (bdt[:, :], "b_dt"), (cw[:, :, :], "conv_w"), (cb[:, :], "conv_b")):
                sp.dma_start(dst, a[name]).then_inc(consts, 16)
            for n, m in enumerate(((M_DT, M_B + 1), (M_C, M_DT), (M_Z, M_C))):
                c = slice(m[0] * P, m[1] * P)
                sp.dma_start(w_in[:, :, c], a["w_in"][:, c].rearrange("(k p) n -> p k n", p=P)).then_inc(w_ok[n], 16)
            with sp.Fori(0, B) as i:
                for ch in range(NCH):
                    g = i * NCH + ch
                    tok = i * L + ch * CH
                    s.hold(sp, t_full, Z + g * T_JOBS)
                    after = (i + ch) % B * L + (ch + 1) % NCH * CH
                    sp.dma_start(x[:, (ch + 1) % NCH, :, :], rows(a["x"], after, CH)).then_inc(x_in[(ch + 1) % NCH], 16)
                    s.hold(sp, v_read, Z + g * V_JOBS + NV + 1)
                    sp.dma_start(a["s_b"][:, bass.ds(tok, CH)], bT[:, :]).then_inc(b_out, 16)
                    for c in range(NC_T):
                        s.hold(sp, lo_ok, Z + g * NC_T + c + 1)
                        for n, part in enumerate((c_hi, c_mid, c_lo)):
                            sp.dma_start(a["s_c"][n, c, :, bass.ds(tok, CH)], part[:, c % 2, :]).then_inc(c_out[c % 2], 16)
                    s.hold(sp, u_ok, Z + (g + 1) * NC_T)
                    sp.dma_start(cols(a["s_u"], tok, CH), conv[:, :, :]).then_inc(u_out, 16)
                    for c in range(NC_T):
                        s.hold(sp, a_read, Z + g * A_JOBS + J_Z + c + NA + 1)
                        sp.dma_start(a["s_z"][c, :, bass.ds(tok, CH)], z[:, c % 2, :]).then_inc(z_out[c % 2], 16)
                    s.hold(sp, delta_ok, Z + g + 1)
                    sp.dma_start(cols(a["s_delta"], tok, CH), dt_l[:, :, :]).then_inc(delta_out, 16)
                    s.hold(sp, du_ok, Z + g + 1)
                    sp.dma_start(cols(a["s_du"], tok, CH), dt_e[:, :, :]).then_inc(du_out, 16)
            sp.wait_ge(x_in[0], Z + (B + 1) * 16)
            for r in range(2):
                sp.wait_ge(c_out[r], Z + B * NCH * NC_T // 2 * 3 * 16)
                sp.wait_ge(z_out[r], Z + B * NCH * NC_T // 2 * 16)
            for done in (b_out, u_out, delta_out, du_out):
                sp.wait_ge(done, Z + B * NCH * 16)

        @block.gpsimd
        def _(pool):
            with pool.Fori(0, B) as i:
                for ch in range(NCH):
                    g = i * NCH + ch
                    for c in range(NC_T):
                        n = g * NC_T + c
                        s.hold(pool, v_read, Z + g * V_JOBS + c + NV + 2)
                        s.hold(pool, c_out[c % 2], Z + (g * (NC_T // 2) + c // 2) * 48)
                        nc.gpsimd.tensor_copy(c_mid[:, c % 2, :], c_res[:, c % 2, :]).then_inc(mid_ok, 1)
                        pool.wait_ge(mid_ok, Z + n + 1)
                        nc.gpsimd.tensor_tensor(c_lo[:, c % 2, :], c_res[:, c % 2, :], c_mid[:, c % 2, :],
                                                ALU.subtract).then_inc(lo_ok, 1)

        @block.tensor
        def _(pe):
            def turn(j, slot):
                pe.wait_ge(xn_ok, Z + (j + 1) * TT)
                for k in range(KD):
                    pe.wait_ge(t_read, Z + j * T_JOBS + k + 1)
                    for t in range(TT):
                        last = nc.tensor.transpose(ps_t[:, k % NT, t * P:(t + 1) * P],
                                                   x[:, slot, t, k * P:(k + 1) * P], ident[:, :])
                    last.then_inc(t_full, 1)

            pe.wait_ge(consts, Z + 16 * N_CONST)
            turn(0, 0)
            pe.wait_ge(w_ok[0], Z + 16)
            with pe.Fori(0, B) as i:
                for ch in range(NCH):
                    g = i * NCH + ch

                    def project(dst, m):
                        for k in range(KD):
                            last = nc.tensor.matmul(dst, w_in[:, k, m * P:(m + 1) * P], xnT[:, ch, k, :],
                                                    start=(k == 0), stop=(k == KD - 1))
                        return last

                    def slot_a(job):
                        pe.wait_ge(a_read, Z + g * A_JOBS + job + 1)
                        return ps_a[:, (ch * A_JOBS + job) % NA, :]

                    pe.wait_ge(t_read, Z + (g + 1) * T_JOBS + NT)
                    for job, m in enumerate((M_DT, M_X)):
                        project(slot_a(job), m).then_inc(a_full, 1)
                    pe.wait_ge(v_read, Z + g * V_JOBS + 1)
                    project(ps_v[:, (ch * V_JOBS) % NV, :], M_B).then_inc(v_full, 1)
                    pe.wait_ge(a_read, Z + g * A_JOBS + NA + 1)
                    for c in range(NC_T):
                        nc.tensor.matmul(slot_a(J_DT + c), w_dt[:, c * P:(c + 1) * P], dtl_x[:, 0, :],
                                         start=True, stop=True).then_inc(a_full, 1)
                    pe.wait_ge(a_read, Z + g * A_JOBS + NA + 2)
                    for c in range(NC_T):
                        nc.tensor.matmul(slot_a(J_XR + c), rep[:, c, :], dtl_x[:, 1, :],
                                         start=True, stop=True).then_inc(a_full, 1)
                    pe.wait_ge(w_ok[1], Z + 16)
                    for c in range(NC_T):
                        pe.wait_ge(v_read, Z + g * V_JOBS + c + 2)
                        project(ps_v[:, (ch * V_JOBS + c + 1) % NV, :], M_C + c).then_inc(v_full, 1)
                    pe.wait_ge(w_ok[2], Z + 16)
                    for c in range(NC_T):
                        project(slot_a(J_Z + c), M_Z + c).then_inc(a_full, 1)
                        if c == NC_T // 2:
                            turn(g + 1, (ch + 1) % NCH)

        @block.scalar
        def _(act):
            def deviation(j, slot):
                act.wait_ge(mv_ok, Z + (j + 1) * TT)
                nc.scalar.activation(std[:, slot, :], mv[:, slot, :, 1], ACT.Sqrt, bias=EPS).then_inc(std_ok, 1)

            nc.scalar.nop().then_inc(a_read, NA)
            deviation(0, 0)
            act.wait_ge(consts, Z + 16 * N_CONST)
            nc.scalar.mul(bdt2[:, :], bdt[:, :], 2.0).then_inc(bdt2_ok, 1)
            act.wait_ge(bdt2_ok, Z + 1)
            with act.Fori(0, B) as i:
                for ch in range(NCH):
                    g = i * NCH + ch

                    def bank(job):
                        act.wait_ge(a_full, Z + g * A_JOBS + job + 1)
                        return ps_a[:, (ch * A_JOBS + job) % NA, :]

                    for job in range(2):
                        src = bank(job)
                        nc.scalar.copy(dtl_x[:, job, :], src).then_inc(a_read, 1)
                    act.wait_ge(delta_ok, Z + g)
                    for c in range(NC_T):
                        src = bank(J_DT + c)
                        nc.scalar.activation(dt_x[:, c, :], src, ACT.Identity, bias=bdt2[:, c:c + 1]).then_inc(a_read, 1)
                    act.wait_ge(halo_ok, Z + g + 1)
                    for c in range(NC_T):
                        src = bank(J_XR + c)
                        nc.scalar.copy(xr[:, c, HALO:HALO + CH], src).then_inc(a_read, 1)
                    act.wait_ge(a_read, Z + g * A_JOBS + J_XR + NA)
                    act.wait_ge(du_out, Z + g * 16)
                    nc.scalar.activation(dt_e[:, :, :], dt_x[:, :, :], ACT.Abs).then_inc(abs_ok, 1)
                    act.wait_ge(abs_ok, Z + g + 1)
                    nc.scalar.activation(dt_e[:, :, :], dt_e[:, :, :], ACT.Exp, scale=-1.0).then_inc(exp_ok, 1)
                    act.wait_ge(exp_ok, Z + g + 1)
                    act.wait_ge(delta_out, Z + g * 16)
                    act.wait_ge(du_ok, Z + g)
                    nc.scalar.activation(dt_l[:, :, :], dt_e[:, :, :], ACT.Ln, bias=1.0).then_inc(ln_ok, 1)
                    for c in range(NC_T):
                        act.wait_ge(v_full, Z + g * V_JOBS + c + 2)
                        act.wait_ge(c_out[c % 2], Z + (g * (NC_T // 2) + c // 2) * 48)
                        nc.scalar.copy(c_hi[:, c % 2, :], ps_v[:, (ch * V_JOBS + c + 1) % NV, :]).then_inc(hi_ok, 1)
                    for c in range(NC_T):
                        act.wait_ge(conv_step, Z + (g * NC_T + c + 1) * D_CONV)
                        nc.scalar.activation(conv[:, c, :], conv[:, c, :], ACT.Silu, bias=cb[:, c:c + 1]).then_inc(u_ok, 1)
                    for c in range(NC_T):
                        if c == NC_T // 4:
                            deviation(g + 1, (ch + 1) % NCH)
                        src = bank(J_Z + c)
                        act.wait_ge(z_out[c % 2], Z + (g * (NC_T // 2) + c // 2) * 16)
                        nc.scalar.activation(z[:, c % 2, :], src, ACT.Silu).then_inc(a_read, 1)

        @block.vector
        def _(dve):
            def statistics(j, slot, loads):
                dve.wait_ge(x_in[slot], Z + loads * 16)
                for t in range(TT):
                    nc.vector.bn_stats(stats[:, slot, t, :], x[:, slot, t, :]).then_inc(stats_ok, 1)
                s.hold(dve, stats_ok, Z + (j + 1) * TT)
                for t in range(TT):
                    nc.vector.bn_aggr(mv[:, slot, t, :], stats[:, slot, t, :]).then_inc(mv_ok, 1)

            def normalise(j, slot):
                dve.wait_ge(std_ok, Z + j + 1)
                nc.vector.reciprocal(rstd[:, slot, :], std[:, slot, :]).then_inc(rstd_ok, 1)
                dve.wait_ge(rstd_ok, Z + j + 1)
                for t in range(TT):
                    xt = x[:, slot, t, :]
                    nc.vector.tensor_scalar(xt, xt, mv[:, slot, t, 0:1], rstd[:, slot, t:t + 1], ALU.subtract, ALU.mult).then_inc(xn_ok, 1)

            def read_turned(j, slot):
                for k in range(KD):
                    dve.wait_ge(t_full, Z + j * T_JOBS + k + 1)
                    nc.vector.tensor_copy(xnT[:, slot, k, :], ps_t[:, k % NT, :]).then_inc(t_read, 1)

            nc.vector.nop().then_inc(t_read, NT)
            nc.vector.nop().then_inc(v_read, NV)
            statistics(0, 0, 1)
            normalise(0, 0)
            read_turned(0, 0)
            with dve.Fori(0, B) as i:
                for ch in range(NCH):
                    g = i * NCH + ch
                    dve.wait_ge(conv_step, Z + g * NC_T * D_CONV)
                    if ch == 0:
                        nc.vector.memset(xr[:, :, 0:HALO], 0.0).then_inc(halo_ok, 1)
                    else:
                        nc.vector.tensor_copy(xr[:, :, 0:HALO], xr[:, :, CH:CH + HALO]).then_inc(halo_ok, 1)
                    dve.wait_ge(v_full, Z + g * V_JOBS + 1)
                    dve.wait_ge(b_out, Z + g * 16)
                    nc.vector.tensor_copy(bT[:, :], ps_v[:, (ch * V_JOBS) % NV, :]).then_inc(v_read, 1)
                    dve.wait_ge(u_out, Z + g * 16)
                    for c in range(NC_T):
                        dve.wait_ge(a_read, Z + g * A_JOBS + J_XR + c + NA + 1)
                        for j in range(D_CONV):
                            step = (g * NC_T + c) * D_CONV + j
                            if j == 0:
                                nc.vector.tensor_scalar(conv[:, c, :], xr[:, c, 0:CH], cw[:, c, 0:1], None,
                                                        ALU.mult).then_inc(conv_step, 1)
                            else:
                                dve.wait_ge(conv_step, Z + step)
                                nc.vector.scalar_tensor_tensor(out=conv[:, c, :], in0=xr[:, c, j:j + CH], scalar=cw[:, c, j:j + 1],
                                                               in1=conv[:, c, :], op0=ALU.mult, op1=ALU.add).then_inc(conv_step, 1)
                        dve.wait_ge(hi_ok, Z + g * NC_T + c + 1)
                        if c >= 2:
                            dve.wait_ge(lo_ok, Z + g * NC_T + c - 1)
                        nc.vector.tensor_tensor(c_res[:, c % 2, :], ps_v[:, (ch * V_JOBS + c + 1) % NV, :], c_hi[:, c % 2, :],
                                                ALU.subtract).then_inc(v_read, 1)
                    statistics(g + 1, (ch + 1) % NCH, i + ch + 1)
                    dve.wait_ge(ln_ok, Z + g + 1)
                    nc.vector.tensor_scalar(dt_d[:, :, :], dt_e[:, :, :], 1.0, -1.0, ALU.add, ALU.add).then_inc(sp_step, 1)
                    normalise(g + 1, (ch + 1) % NCH)
                    dve.wait_ge(sp_step, Z + g * SP_STEPS + 1)
                    nc.vector.tensor_tensor(dt_d[:, :, :], dt_e[:, :, :], dt_d[:, :, :], ALU.subtract).then_inc(sp_step, 1)
                    read_turned(g + 1, (ch + 1) % NCH)
                    dve.wait_ge(sp_step, Z + g * SP_STEPS + 2)
                    nc.vector.tensor_tensor(dt_l[:, :, :], dt_l[:, :, :], dt_d[:, :, :], ALU.add).then_inc(sp_step, 1)
                    dve.wait_ge(sp_step, Z + g * SP_STEPS + 3)
                    nc.vector.tensor_tensor(dt_l[:, :, :], dt_l[:, :, :], dt_e[:, :, :], ALU.min).then_inc(sp_step, 1)
                    dve.wait_ge(sp_step, Z + g * SP_STEPS + 4)
                    nc.vector.scalar_tensor_tensor(out=dt_l[:, :, :], in0=dt_x[:, :, :], scalar=0.0, in1=dt_l[:, :, :],
                                                   op0=ALU.max, op1=ALU.add).then_inc(delta_ok, 1)
                    dve.wait_ge(delta_ok, Z + g + 1)
                    dve.wait_ge(u_ok, Z + (g + 1) * NC_T)
                    nc.vector.tensor_tensor(dt_e[:, :, :], dt_l[:, :, :], conv[:, :, :], ALU.mult).then_inc(du_ok, 1)


def selective_scan(nc, a):
    NB, R, NH_ = 8, 4, 2
    AHEAD = 4
    N = D_STATE
    with Scope(nc, "scan") as s:
        ident = s.sb("ident", [P, P])
        sel32 = s.sb("sel32", [C_ROWS, 4, P])
        sel = s.sb("sel", [C_ROWS, 4, P], BF16)
        a_exp = s.sb("a_exp", [P, NC_T * N])
        d_all = s.sb("d_all", [P, NC_T])
        a_cur = s.sb("a_cur", [P, B, N])
        d_cur = s.sb("d_cur", [P, B])
        delta = s.sb("delta", [P, B, L])
        du = s.sb("du", [P, B, L])
        u = s.sb("u", [P, B, L])
        sz = s.sb("sz", [P, B, L])
        cs = s.sb("cs", [C_ROWS, B, N_QUAD, L], BF16)
        b_bc = s.sb("b_bc", [P, NB, L])
        decay = s.sb("decay", [P, R, L])
        inp = s.sb("inp", [P, R, L])
        h = s.sb("h", [P, NH_, L])
        hc = s.sb("hc", [P, R, L])
        y = s.sb("y", [P, B, L])
        ps_c = s.ps("ps_c", [P, 2, L])
        ps_y = s.ps("ps_y", [P, B, L])

        consts, sel_ok, aexp_ok, cur_ok = (s.sem(n) for n in ("consts", "sel_ok", "aexp_ok", "cur_ok"))
        g_in = s.sems("g_in", B)
        b_in = s.sems("b_in", NB)
        exp_ok, inp_ok, scan_ok, hc_ok, c_full, sum_ok, skip_ok, fin_ok = (s.sem(n) for n in (
            "exp_ok", "inp_ok", "scan_ok", "hc_ok", "c_full", "sum_ok", "skip_ok", "fin_ok"))
        y_out = s.sems("y_out", B)
        block = s.block()
        G_LOADS = 4 + 3
        LOAD_AT = (4, 5, 7, 8, 10, 11, 13)
        UNITS = B * N
        FIN = 1

        def over_groups(eng, group):
            group(0, 0, None, (0, 1))
            with eng.Fori(0, NC_T - 1) as c:
                group(c, 1, (c, 0), (c + 1, 0))
                group(c + 1, 0, (c, 1), (c + 1, 1))
            group(NC_T - 1, 1, (NC_T - 1, 0), None)

        @block.sync
        def _(sp):
            def load_group(c, b, i):
                part = slice(b * L, (b + 1) * L)
                if i < 4:
                    dst, name = ((delta, "s_delta"), (du, "s_du"), (u, "s_u"), (sz, "s_z"))[i]
                    dst, src = dst[:, b, :], a[name][bass.ds(c, 1), :, part].rearrange("c p t -> (c p) t")
                else:
                    n = i - 4
                    dst = cs[32 * n:32 * n + 32, b, :, :]
                    src = a["s_c"][n, bass.ds(c, 1), :, part].rearrange("c (q r) t -> (c r) q t", q=N_QUAD)
                sp.dma_start(dst, src).then_inc(g_in[b], 16)

            def load_b(c, b, n):
                k = (b * N + n) % NB
                row = a["s_b"][bass.ds(c * N + n, 1), b * L:(b + 1) * L]
                sp.dma_start(b_bc[:, k, :], row.to_broadcast([P, L])).then_inc(b_in[k], 16)

            def finished(c, b):
                s.hold(sp, fin_ok, Z + c * B + b + FIN + 1)
                sp.dma_start(a["s_y"][bass.ds(c, 1), :, b * L:(b + 1) * L].rearrange("c p t -> (c p) t"), y[:, b, :]).then_inc(y_out[b], 16)

            def group(c, b, before, after):
                for n in range(N):
                    if n + AHEAD < N or after:
                        s.hold(sp, inp_ok, Z + (c * B + b) * N + n + AHEAD + 1)
                        load_b(*((c, b) if n + AHEAD < N else after), (n + AHEAD) % N)
                    if n == LOAD_AT[0] and before:
                        finished(*before)
                    if n in LOAD_AT and after:
                        load_group(*after, LOAD_AT.index(n))

            for i in range(G_LOADS):
                load_group(0, 0, i)
            for dst, name in ((a_exp[:, :], "a_log"), (ident[:, :], "c_ident"), (sel32[:, :, :], "c_sel"), (d_all[:, :], "d_param")):
                src = a[name].rearrange("p c n -> p (c n)") if name == "a_log" else a[name]
                sp.dma_start(dst, src).then_inc(consts, 16)
            for n in range(AHEAD):
                load_b(0, 0, n)
            over_groups(sp, group)
            finished(NC_T - 1, 1)
            for b in range(B):
                sp.wait_ge(y_out[b], Z + NC_T * 16)

        @block.scalar
        def _(act):
            act.wait_ge(consts, Z + 4 * 16)
            nc.scalar.activation(a_exp[:, :], a_exp[:, :], ACT.Exp).then_inc(aexp_ok, 1)
            nc.scalar.copy(sel[:, :, :], sel32[:, :, :]).then_inc(sel_ok, 1)
            act.wait_ge(aexp_ok, Z + 1)

            def group(c, b, before, after):
                g = c * B + b
                act.wait_ge(fin_ok, Z + g - 1 + FIN)
                nc.scalar.mul(a_cur[:, b, :], a_exp[:, bass.ds(c * N, N)], -1.0).then_inc(cur_ok, 1)
                nc.scalar.copy(d_cur[:, b:b + 1], d_all[:, bass.ds(c, 1)]).then_inc(cur_ok, 1)
                act.wait_ge(cur_ok, Z + (g + 1) * 2)
                act.wait_ge(g_in[b], Z + (c + 1) * G_LOADS * 16)
                for n in range(N):
                    act.wait_ge(scan_ok, Z + g * N + n + 1)
                    nc.scalar.activation(decay[:, n % R, :], delta[:, b, :], ACT.Exp, scale=a_cur[:, b, n:n + 1]).then_inc(exp_ok, 1)

            over_groups(act, group)

        @block.gpsimd
        def _(pool):
            nc.gpsimd.nop().then_inc(inp_ok, NB)

            def group(c, b, before, after):
                s.hold(pool, g_in[b], Z + (c + 1) * G_LOADS * 16)
                for n in range(N):
                    k = (b * N + n) % NB
                    s.hold(pool, b_in[k], Z + (c * (UNITS // NB) + (b * N + n) // NB + 1) * 16)
                    s.hold(pool, scan_ok, Z + (c * B + b) * N + n + 1)
                    nc.gpsimd.tensor_tensor(inp[:, n % R, :], du[:, b, :], b_bc[:, k, :], ALU.mult).then_inc(inp_ok, 1)

            over_groups(pool, group)

        @block.vector
        def _(dve):
            nc.vector.nop().then_inc(scan_ok, R)
            nc.vector.nop().then_inc(hc_ok, NH_)
            nc.vector.nop().then_inc(fin_ok, FIN)

            def scan(U, n):
                dve.wait_ge(exp_ok, Z + U + 1)
                dve.wait_ge(inp_ok, Z + U + NB + 1)
                dve.wait_ge(hc_ok, Z + U + 1)
                nc.vector.tensor_tensor_scan(h[:, n % NH_, :], decay[:, n % R, :], inp[:, n % R, :], 0.0,
                                             ALU.mult, ALU.add).then_inc(scan_ok, 1)

            def finish(c, b):
                g = c * B + b
                dve.wait_ge(sum_ok, Z + (g + 1) * N + R)
                dve.wait_ge(y_out[b], Z + c * 16)
                dve.wait_ge(cur_ok, Z + (g + 1) * 2)
                nc.vector.scalar_tensor_tensor(out=y[:, b, :], in0=u[:, b, :], scalar=d_cur[:, b:b + 1], in1=ps_y[:, b, :],
                                               op0=ALU.mult, op1=ALU.add).then_inc(skip_ok, 1)
                dve.wait_ge(skip_ok, Z + g + 1)
                nc.vector.tensor_tensor(y[:, b, :], y[:, b, :], sz[:, b, :], ALU.mult).then_inc(fin_ok, 1)

            def group(c, b, before, after):
                scan((c * B + b) * N, 0)
                for n in range(N):
                    U = (c * B + b) * N + n
                    if n + 1 < N:
                        scan(U + 1, n + 1)
                    dve.wait_ge(c_full, Z + U + 1)
                    dve.wait_ge(scan_ok, Z + U + R + 1)
                    dve.wait_ge(sum_ok, Z + U + 1)
                    nc.vector.tensor_tensor(hc[:, n % R, :], h[:, n % NH_, :], ps_c[:, n % 2, :], ALU.mult).then_inc(hc_ok, 1)
                    if n == 1 and before:
                        finish(*before)

            over_groups(dve, group)
            finish(NC_T - 1, 1)

        @block.tensor
        def _(pe):
            nc.tensor.nop().then_inc(sum_ok, R)
            pe.wait_ge(consts, Z + 4 * 16)
            pe.wait_ge(sel_ok, Z + 1)

            def spread(c, b, n):
                if n == 0:
                    pe.wait_ge(g_in[b], Z + (c + 1) * G_LOADS * 16)
                pe.wait_ge(hc_ok, Z + (c * B + b) * N + n + 1)
                for half in range(L // 512):
                    last = nc.tensor.matmul(ps_c[:, n % 2, half * 512:half * 512 + 512], sel[:, n % 4, :],
                                            cs[:, b, n // 4, half * 512:half * 512 + 512], start=True, stop=True)
                last.then_inc(c_full, 1)

            def group(c, b, before, after):
                g = c * B + b
                if not before:
                    spread(c, b, 0)
                pe.wait_ge(fin_ok, Z + g - 1 + FIN)
                for n in range(N):
                    if n + 1 < N:
                        spread(c, b, n + 1)
                    elif after:
                        spread(*after, 0)
                    pe.wait_ge(hc_ok, Z + g * N + n + NH_ + 1)
                    for half in range(L // 512):
                        last = nc.tensor.matmul(ps_y[:, b, half * 512:half * 512 + 512], ident[:, :],
                                                hc[:, n % R, half * 512:half * 512 + 512], start=(n == 0), stop=(n == N - 1))
                    last.then_inc(sum_ok, 1)

            over_groups(pe, group)


def mix_out(nc, a):
    NP = 4
    KI = NC_T
    with Scope(nc, "mix") as s:
        w = s.sb("w", [P, KI, D])
        yT = s.sb("yT", [P, NCH, KI, CH])
        x = s.sb("x", [P, NCH, TT, D])
        xn = s.sb("xn", [P, NCH, TT, D])
        w_r = s.sb("w_r", [P, D])
        b_r = s.sb("b_r", [P, 1])
        stats = s.sb("stats", [P, NCH, TT, 6])
        mv = s.sb("mv", [P, NCH, TT, 2])
        std = s.sb("std", [P, NCH, TT])
        rstd = s.sb("rstd", [P, NCH, TT])
        prod = s.sb("prod", [P, TT, D])
        score = s.sb("score", [P, NCH, TT])
        ps = s.ps("ps", [P, NP, D])
        consts, full, read, stats_ok, mv_ok, std_ok, rstd_ok, xn_ok, dot_ok, score_ok = (s.sem(n) for n in (
            "consts", "full", "read", "stats_ok", "mv_ok", "std_ok", "rstd_ok", "xn_ok", "dot_ok", "score_ok"))
        y_in, x_in, x_out, xn_out, score_out = (s.sems(n, NCH) for n in ("y_in", "x_in", "x_out", "xn_out", "score_out"))
        block = s.block()

        @block.sync
        def _(sp):
            sp.dma_start(w[:, :, :], a["w_out"].rearrange("(k p) n -> p k n", p=P)).then_inc(consts, 16)
            sp.dma_start(w_r[:, :], a["w_r"].to_broadcast([P, D])).then_inc(consts, 16)
            sp.dma_start(b_r[:, :], a["b_r"].to_broadcast([P, 1])).then_inc(consts, 16)
            with sp.Fori(0, B) as i:
                for ch in range(NCH):
                    g = i * NCH + ch
                    s.hold(sp, full, Z + i * NCH * TT)
                    sp.dma_start(yT[:, ch, :, :], cols(a["s_y"], i * L + ch * CH, CH)).then_inc(y_in[ch], 16)
                    s.hold(sp, x_out[ch], Z + i * 16)
                    s.hold(sp, xn_ok, Z + i * NCH * TT)
                    sp.dma_start(x[:, ch, :, :], rows(a["x"], i * L + ch * CH, CH)).then_inc(x_in[ch], 16)
                for ch in range(NCH):
                    g = i * NCH + ch
                    tok = i * L + ch * CH
                    s.hold(sp, read, Z + (g + 1) * TT + NP)
                    sp.dma_start(rows(a["s_x1"], tok, CH), x[:, ch, :, :]).then_inc(x_out[ch], 16)
                    s.hold(sp, xn_ok, Z + (g + 1) * TT)
                    sp.dma_start(rows(a["s_n1"], tok, CH), xn[:, ch, :, :]).then_inc(xn_out[ch], 16)
                    s.hold(sp, score_ok, Z + g + 1)
                    sp.dma_start(a["s_score"][:, bass.ds(g * TT, TT)], score[:, ch, :]).then_inc(score_out[ch], 16)
            for ch in range(NCH):
                for done in (x_out, xn_out, score_out):
                    sp.wait_ge(done[ch], Z + B * 16)

        @block.tensor
        def _(pe):
            pe.wait_ge(consts, Z + 48)
            with pe.Fori(0, B) as i:
                for ch in range(NCH):
                    g = i * NCH + ch
                    pe.wait_ge(y_in[ch], Z + (i + 1) * 16)
                    for t in range(TT):
                        pe.wait_ge(read, Z + g * TT + t + 1)
                        for k in range(KI):
                            last = nc.tensor.matmul(ps[:, t, :], yT[:, ch, k, t * P:(t + 1) * P], w[:, k, :],
                                                    start=(k == 0), stop=(k == KI - 1))
                        last.then_inc(full, 1)

        @block.scalar
        def _(act):
            with act.Fori(0, B) as i:
                for ch in range(NCH):
                    act.wait_ge(mv_ok, Z + (i * NCH + ch + 1) * TT)
                    nc.scalar.activation(std[:, ch, :], mv[:, ch, :, 1], ACT.Sqrt, bias=EPS).then_inc(std_ok, 1)

        @block.vector
        def _(dve):
            nc.vector.nop().then_inc(read, NP)
            dve.wait_ge(consts, Z + 48)
            with dve.Fori(0, B) as i:
                for ch in range(NCH):
                    g = i * NCH + ch
                    dve.wait_ge(x_in[ch], Z + (i + 1) * 16)
                    for t in range(TT):
                        dve.wait_ge(full, Z + g * TT + t + 1)
                        nc.vector.tensor_tensor(x[:, ch, t, :], x[:, ch, t, :], ps[:, t, :], ALU.add).then_inc(read, 1)
                        dve.wait_ge(read, Z + g * TT + t + NP + 1)
                        nc.vector.bn_stats(stats[:, ch, t, :], x[:, ch, t, :]).then_inc(stats_ok, 1)
                    s.hold(dve, stats_ok, Z + (g + 1) * TT)
                    for t in range(TT):
                        nc.vector.bn_aggr(mv[:, ch, t, :], stats[:, ch, t, :]).then_inc(mv_ok, 1)
                    dve.wait_ge(std_ok, Z + g + 1)
                    nc.vector.reciprocal(rstd[:, ch, :], std[:, ch, :]).then_inc(rstd_ok, 1)
                    dve.wait_ge(rstd_ok, Z + g + 1)
                    dve.wait_ge(xn_out[ch], Z + i * 16)
                    for t in range(TT):
                        nc.vector.tensor_scalar(xn[:, ch, t, :], x[:, ch, t, :], mv[:, ch, t, 0:1], rstd[:, ch, t:t + 1],
                                                ALU.subtract, ALU.mult).then_inc(xn_ok, 1)
                    dve.wait_ge(score_out[ch], Z + i * 16)
                    dve.wait_ge(dot_ok, Z + g * TT)
                    for t in range(TT):
                        dve.wait_ge(xn_ok, Z + g * TT + t + 1)
                        nc.vector.tensor_tensor_reduce(prod[:, t, :], xn[:, ch, t, :], w_r[:, :], 1.0, 0.0,
                                                       ALU.mult, ALU.add, score[:, ch, t:t + 1]).then_inc(dot_ok, 1)
                    dve.wait_ge(dot_ok, Z + (g + 1) * TT)
                    nc.vector.tensor_scalar(score[:, ch, :], score[:, ch, :], b_r[:, 0:1], None, ALU.add).then_inc(score_ok, 1)


def rank_tokens(nc, a):
    with Scope(nc, "rank") as s:
        col = s.sb("col", [P, TOK_TILES])
        colT = s.sb("colT", [TOK_TILES, P])
        ident = s.sb("ident", [P, P])
        row = s.sb("row", [P, T])
        earlier = s.sb("earlier", [P, P])
        scratch = s.sb("scratch", [P, 3, TOK_TILES, L], BF16)
        cnt = s.sb("cnt", [P, 3, TOK_TILES])
        half = s.sb("half", [P, TOK_TILES])
        dest = s.sb("dest", [P, TOK_TILES])
        dest_i = s.sb("dest_i", [P, TOK_TILES], I32)
        xn = s.sb("xn", [P, TOK_TILES, D])
        zeros = s.sb("zeros", [P, TOK_TILES // 2, D])
        ps = s.ps("ps", [TOK_TILES, P])
        col_in, row_in, xn_in, zero_ok, zero_out, colT_ok, colT_sb, colT_out, cnt_zero, cnt_ok, step, dest_ok, dest_out = (s.sem(n) for n in (
            "col_in", "row_in", "xn_in", "zero_ok", "zero_out", "colT_ok", "colT_sb", "colT_out", "cnt_zero", "cnt_ok", "step", "dest_ok", "dest_out"))
        sent = s.pool_dma_sem("sent")
        block = s.block()
        N_CNT = 3 * TOK_TILES - B

        @block.sync
        def _(sp):
            sp.dma_start(col[:, :], a["s_score"]).then_inc(col_in, 16)
            sp.dma_start(ident[:, :], a["c_ident"]).then_inc(col_in, 16)
            sp.dma_start(earlier[:, :], a["c_earlier"]).then_inc(row_in, 16)
            sp.wait_ge(colT_sb, Z + 1)
            sp.dma_start(a["s_score_row"].rearrange("o (t p) -> (o t) p", p=P), colT[:, :]).then_inc(colT_out, 16)
            sp.dma_start(xn[:, :, :], rows(a["s_n1"], 0, T)).then_inc(xn_in, 16)
            sp.wait_ge(colT_out, Z + 16)
            sp.dma_start(row[:, :], a["s_score_row"].to_broadcast([P, T])).then_inc(row_in, 16)
            sp.wait_ge(zero_ok, Z + 1)
            sp.dma_start(rows(a["s_sel_out"], B * K_SEL, B * K_SEL), zeros[:, :, :]).then_inc(zero_out, 16)
            sp.wait_ge(dest_ok, Z + 1)
            sp.dma_start(a["s_dest"], dest_i[:, :]).then_inc(dest_out, 16)
            sp.wait_ge(dest_out, Z + 16)
            sp.wait_ge(zero_out, Z + 16)

        @block.tensor
        def _(pe):
            pe.wait_ge(col_in, Z + 32)
            nc.tensor.transpose(ps[:, :], col[:, :], ident[:, :]).then_inc(colT_ok, 1)

        @block.scalar
        def _(act):
            act.wait_ge(colT_ok, Z + 1)
            nc.scalar.copy(colT[:, :], ps[:, :]).then_inc(colT_sb, 1)

        @block.vector
        def _(dve):
            nc.vector.memset(cnt[:, :, :], 0.0).then_inc(cnt_zero, 1)
            dve.wait_ge(row_in, Z + 32)
            dve.wait_ge(col_in, Z + 32)
            dve.wait_ge(cnt_zero, Z + 1)
            for j in range(TOK_TILES):
                b, t = j // NQT, j % NQT
                seq = row[:, b * L:(b + 1) * L]
                me = col[:, j:j + 1]
                nc.vector.tensor_scalar(scratch[:, 0, j, 0:L - t * P], seq[:, t * P:L], me, 0.0, ALU.is_gt, ALU.add,
                                        accum_out=cnt[:, 0, j:j + 1]).then_inc(cnt_ok, 1)
                nc.vector.scalar_tensor_tensor(out=scratch[:, 1, j, 0:P], in0=seq[:, t * P:(t + 1) * P], scalar=me, in1=earlier[:, :],
                                               op0=ALU.is_equal, op1=ALU.mult, accum_out=cnt[:, 1, j:j + 1]).then_inc(cnt_ok, 1)
                if t:
                    nc.vector.tensor_scalar(scratch[:, 2, j, 0:t * P], seq[:, 0:t * P], me, 0.0, ALU.is_ge, ALU.add,
                                            accum_out=cnt[:, 2, j:j + 1]).then_inc(cnt_ok, 1)
            dve.wait_ge(cnt_ok, Z + N_CNT)
            nc.vector.tensor_tensor(cnt[:, 0, :], cnt[:, 0, :], cnt[:, 1, :], ALU.add).then_inc(step, 1)
            dve.wait_ge(step, Z + 1)
            nc.vector.tensor_tensor(cnt[:, 0, :], cnt[:, 0, :], cnt[:, 2, :], ALU.add).then_inc(step, 1)
            dve.wait_ge(step, Z + 2)
            nc.vector.tensor_scalar(half[:, :], cnt[:, 0, :], float(K_SEL), float(K_SEL), ALU.is_ge, ALU.mult).then_inc(step, 1)
            dve.wait_ge(step, Z + 3)
            nc.vector.tensor_tensor(dest[:, :], cnt[:, 0, :], half[:, :], ALU.add).then_inc(step, 1)
            dve.wait_ge(step, Z + 4)
            nc.vector.tensor_scalar(dest[:, NQT:], dest[:, NQT:], float(K_SEL), None, ALU.add).then_inc(step, 1)
            dve.wait_ge(step, Z + 5)
            nc.vector.tensor_copy(dest_i[:, :], dest[:, :]).then_inc(dest_ok, 1)

        @block.gpsimd
        def _(pool):
            nc.gpsimd.memset(zeros[:, :, :], 0.0).then_inc(zero_ok, 1)
            pool.wait_ge(dest_ok, Z + 1)
            pool.wait_ge(xn_in, Z + 16)
            for j in range(TOK_TILES):
                nc.gpsimd.indirect_dma_start(a["s_sel_in"], bass.IndirectOffsetOnAxis(ap=dest_i[:, j:j + 1].bitcast(U32), axis=0),
                                             xn[:, j, :], None).then_inc(sent, 16)
            pool.wait_ge(sent, 16 * TOK_TILES)


def select_ffn(nc, a):
    NT, NA, NV = 2, 4, 2
    with Scope(nc, "ffn") as s:
        w1 = s.sb("w1", [P, KD, DF])
        w2 = s.sb("w2", [P, KF, D])
        b1 = s.sb("b1", [P, KF])
        b2 = s.sb("b2", [P, D])
        ident = s.sb("ident", [P, P])
        xs = s.sb("xs", [P, TT, D])
        xT = s.sb("xT", [P, KD, CH])
        hT = s.sb("hT", [P, KF, CH])
        y = s.sb("y", [P, TT, D])
        ps_t = s.ps("ps_t", [P, NT, CH])
        ps_h = s.ps("ps_h", [P, NA, CH])
        ps_y = s.ps("ps_y", [P, NV, D])
        consts, x_in, t_full, t_read, h_full, h_read, y_full, y_read, y_out = (s.sem(n) for n in (
            "consts", "x_in", "t_full", "t_read", "h_full", "h_read", "y_full", "y_read", "y_out"))
        block = s.block()

        @block.sync
        def _(sp):
            sp.dma_start(ident[:, :], a["c_ident"]).then_inc(consts, 16)
            sp.dma_start(b1[:, :], a["b1"]).then_inc(consts, 16)
            sp.dma_start(w1[:, :, :], a["w1"].rearrange("(k p) n -> p k n", p=P)).then_inc(consts, 16)
            sp.dma_start(w2[:, :, :], a["w2"].rearrange("(k p) n -> p k n", p=P)).then_inc(consts, 16)
            sp.dma_start(b2[:, :], a["b2"].to_broadcast([P, D])).then_inc(consts, 16)
            sp.dma_start(xs[:, :, :], rows(a["s_sel_in"], 0, CH)).then_inc(x_in, 16)
            with sp.Fori(0, B) as b:
                s.hold(sp, t_full, Z + (b + 1) * KD)
                sp.dma_start(xs[:, :, :], rows(a["s_sel_in"], (B - 1) * CH, CH)).then_inc(x_in, 16)
                for t in range(TT):
                    s.hold(sp, y_read, Z + b * TT + t + NV + 1)
                    sp.dma_start(a["s_sel_out"][bass.ds(b * CH + t * P, P), :], y[:, t, :]).then_inc(y_out, 16)
            sp.wait_ge(y_out, Z + B * TT * 16)
            sp.wait_ge(x_in, Z + (B + 1) * 16)

        @block.tensor
        def _(pe):
            pe.wait_ge(consts, Z + 80)
            with pe.Fori(0, B) as b:
                pe.wait_ge(x_in, Z + (b + 1) * 16)
                for k in range(KD):
                    pe.wait_ge(t_read, Z + b * KD + k + 1)
                    for t in range(TT):
                        last = nc.tensor.transpose(ps_t[:, k % NT, t * P:(t + 1) * P], xs[:, t, k * P:(k + 1) * P], ident[:, :])
                    last.then_inc(t_full, 1)
                pe.wait_ge(t_read, Z + (b + 1) * KD + NT)
                for f in range(KF):
                    pe.wait_ge(h_read, Z + b * KF + f + 1)
                    for k in range(KD):
                        last = nc.tensor.matmul(ps_h[:, f % NA, :], w1[:, k, f * P:(f + 1) * P], xT[:, k, :],
                                                start=(k == 0), stop=(k == KD - 1))
                    last.then_inc(h_full, 1)
                pe.wait_ge(h_read, Z + (b + 1) * KF + NA)
                for t in range(TT):
                    pe.wait_ge(y_read, Z + b * TT + t + 1)
                    for f in range(KF):
                        last = nc.tensor.matmul(ps_y[:, t % NV, :], hT[:, f, t * P:(t + 1) * P], w2[:, f, :],
                                                start=(f == 0), stop=(f == KF - 1))
                    last.then_inc(y_full, 1)

        @block.scalar
        def _(act):
            nc.scalar.nop().then_inc(h_read, NA)
            act.wait_ge(consts, Z + 80)
            with act.Fori(0, B) as b:
                act.wait_ge(y_full, Z + b * TT)
                for f in range(KF):
                    act.wait_ge(h_full, Z + b * KF + f + 1)
                    nc.scalar.activation(hT[:, f, :], ps_h[:, f % NA, :], ACT.Gelu_apprx_tanh, bias=b1[:, f:f + 1]).then_inc(h_read, 1)

        @block.vector
        def _(dve):
            nc.vector.nop().then_inc(t_read, NT)
            nc.vector.nop().then_inc(y_read, NV)
            dve.wait_ge(consts, Z + 80)
            with dve.Fori(0, B) as b:
                dve.wait_ge(h_full, Z + b * KF)
                for k in range(KD):
                    dve.wait_ge(t_full, Z + b * KD + k + 1)
                    nc.vector.tensor_copy(xT[:, k, :], ps_t[:, k % NT, :]).then_inc(t_read, 1)
                dve.wait_ge(y_out, Z + b * TT * 16)
                for t in range(TT):
                    dve.wait_ge(y_full, Z + b * TT + t + 1)
                    nc.vector.tensor_tensor(y[:, t, :], ps_y[:, t % NV, :], b2[:, :], ALU.add).then_inc(y_read, 1)


def attend_in(nc, a):
    NT, NA, NV = 2, 4, 2
    QK_JOBS = 2 * NHG
    with Scope(nc, "qkv") as s:
        w = s.sb("w", [P, KD, 3 * D])
        ident = s.sb("ident", [P, P])
        dest = s.sb("dest", [P, TOK_TILES], I32)
        got = s.sb("got", [P, TOK_TILES, D])
        x = s.sb("x", [P, NCH, TT, D])
        xn = s.sb("xn", [P, NCH, TT, D])
        stats = s.sb("stats", [P, NCH, TT, 6])
        mv = s.sb("mv", [P, NCH, TT, 2])
        std = s.sb("std", [P, NCH, TT])
        rstd = s.sb("rstd", [P, NCH, TT])
        xT = s.sb("xT", [P, KD, CH])
        qk_hi = s.sb("qk_hi", [P, QK_JOBS, CH])
        qk_lo = s.sb("qk_lo", [P, QK_JOBS, CH])
        v = s.sb("v", [P, TT, D])
        ps_t = s.ps("ps_t", [P, NT, CH])
        ps_a = s.ps("ps_a", [P, NA, CH])
        ps_v = s.ps("ps_v", [P, NV, D])
        consts, dest_in, x2_ok, stats_ok, mv_ok, std_ok, rstd_ok, xn_ok = (s.sem(n) for n in (
            "consts", "dest_in", "x2_ok", "stats_ok", "mv_ok", "std_ok", "rstd_ok", "xn_ok"))
        t_full, t_read, a_full, a_read, v_full, v_read, qk_out, v_out = (s.sem(n) for n in (
            "t_full", "t_read", "a_full", "a_read", "v_full", "v_read", "qk_out", "v_out"))
        qk_hi_ok = s.sem("qk_hi_ok")
        got_in = s.pool_dma_sem("got_in")
        x_in, x_out = s.sems("x_in", NCH), s.sems("x_out", NCH)
        block = s.block()

        @block.sync
        def _(sp):
            sp.dma_start(dest[:, :], a["s_dest"]).then_inc(dest_in, 16)
            sp.dma_start(ident[:, :], a["c_ident"]).then_inc(consts, 16)
            sp.dma_start(w[:, :, :], a["w_qkv"].rearrange("(k p) n -> p k n", p=P)).then_inc(consts, 16)
            with sp.Fori(0, B) as i:
                for ch in range(NCH):
                    s.hold(sp, x_out[ch], Z + i * 16)
                    s.hold(sp, xn_ok, Z + i * NCH * TT)
                    sp.dma_start(x[:, ch, :, :], rows(a["s_x1"], i * L + ch * CH, CH)).then_inc(x_in[ch], 16)
                for ch in range(NCH):
                    g = i * NCH + ch
                    tok = i * L + ch * CH
                    s.hold(sp, x2_ok, Z + (g + 1) * TT)
                    sp.dma_start(rows(a["s_x2"], tok, CH), x[:, ch, :, :]).then_inc(x_out[ch], 16)
                    s.hold(sp, a_read, Z + (g + 1) * QK_JOBS + NA)
                    for n, name in enumerate(("s_q", "s_k")):
                        for part, src in enumerate((qk_hi, qk_lo)):
                            sp.dma_start(cols(a[name][:, part, :, :], tok, CH), src[:, n * NHG:(n + 1) * NHG, :]).then_inc(qk_out, 16)
                    s.hold(sp, v_read, Z + (g + 1) * TT + NV)
                    sp.dma_start(rows(a["s_v"], tok, CH), v[:, :, :]).then_inc(v_out, 16)
            sp.wait_ge(qk_out, Z + B * NCH * 64)
            sp.wait_ge(v_out, Z + B * NCH * 16)
            for ch in range(NCH):
                sp.wait_ge(x_out[ch], Z + B * 16)

        @block.gpsimd
        def _(pool):
            pool.wait_ge(dest_in, Z + 16)
            for j in range(TOK_TILES):
                nc.gpsimd.indirect_dma_start(got[:, j, :], None, a["s_sel_out"],
                                             bass.IndirectOffsetOnAxis(ap=dest[:, j:j + 1].bitcast(U32), axis=0)).then_inc(got_in, 16)

        @block.tensor
        def _(pe):
            pe.wait_ge(consts, Z + 32)
            with pe.Fori(0, B) as i:
                for ch in range(NCH):
                    g = i * NCH + ch
                    pe.wait_ge(xn_ok, Z + (g + 1) * TT)
                    for k in range(KD):
                        pe.wait_ge(t_read, Z + g * KD + k + 1)
                        for t in range(TT):
                            last = nc.tensor.transpose(ps_t[:, k % NT, t * P:(t + 1) * P], xn[:, ch, t, k * P:(k + 1) * P], ident[:, :])
                        last.then_inc(t_full, 1)
                    pe.wait_ge(t_read, Z + (g + 1) * KD + NT)
                    for m in range(QK_JOBS):
                        pe.wait_ge(a_read, Z + g * QK_JOBS + m + 1)
                        for k in range(KD):
                            last = nc.tensor.matmul(ps_a[:, m % NA, :], w[:, k, m * P:(m + 1) * P], xT[:, k, :],
                                                    start=(k == 0), stop=(k == KD - 1))
                        last.then_inc(a_full, 1)
                    for t in range(TT):
                        pe.wait_ge(v_read, Z + g * TT + t + 1)
                        for k in range(KD):
                            last = nc.tensor.matmul(ps_v[:, t % NV, :], xT[:, k, t * P:(t + 1) * P], w[:, k, 2 * D:3 * D],
                                                    start=(k == 0), stop=(k == KD - 1))
                        last.then_inc(v_full, 1)

        @block.scalar
        def _(act):
            with act.Fori(0, B) as i:
                act.wait_ge(mv_ok, Z + (i + 1) * NCH * TT)
                nc.scalar.activation(std[:, :, :], mv[:, :, :, 1], ACT.Sqrt, bias=EPS).then_inc(std_ok, 1)
                for ch in range(NCH):
                    g = i * NCH + ch
                    act.wait_ge(qk_out, Z + g * 64)
                    for m in range(QK_JOBS):
                        act.wait_ge(a_full, Z + g * QK_JOBS + m + 1)
                        nc.scalar.copy(qk_hi[:, m, :].bitcast(F32R), ps_a[:, m % NA, :]).then_inc(qk_hi_ok, 1)

        @block.vector
        def _(dve):
            nc.vector.nop().then_inc(t_read, NT)
            nc.vector.nop().then_inc(v_read, NV)
            nc.vector.nop().then_inc(a_read, NA)
            dve.wait_ge(got_in, 16 * TOK_TILES)
            with dve.Fori(0, B) as i:
                for ch in range(NCH):
                    g = i * NCH + ch
                    dve.wait_ge(x_in[ch], Z + (i + 1) * 16)
                    nc.vector.tensor_tensor(x[:, ch, :, :], x[:, ch, :, :], got[:, bass.ds(g * TT, TT), :], ALU.add).then_inc(x2_ok, TT)
                    dve.wait_ge(x2_ok, Z + (g + 1) * TT)
                    for t in range(TT):
                        nc.vector.bn_stats(stats[:, ch, t, :], x[:, ch, t, :]).then_inc(stats_ok, 1)
                    s.hold(dve, stats_ok, Z + (g + 1) * TT)
                    for t in range(TT):
                        nc.vector.bn_aggr(mv[:, ch, t, :], stats[:, ch, t, :]).then_inc(mv_ok, 1)
                dve.wait_ge(std_ok, Z + i + 1)
                nc.vector.reciprocal(rstd[:, :, :], std[:, :, :]).then_inc(rstd_ok, 1)
                dve.wait_ge(rstd_ok, Z + i + 1)
                dve.wait_ge(t_full, Z + i * NCH * KD)
                for t in range(NCH * TT):
                    n, m = t // TT, t % TT
                    nc.vector.tensor_scalar(xn[:, n, m, :], x[:, n, m, :], mv[:, n, m, 0:1], rstd[:, n, m:m + 1],
                                            ALU.subtract, ALU.mult).then_inc(xn_ok, 1)
                for ch in range(NCH):
                    g = i * NCH + ch
                    dve.wait_ge(v_full, Z + g * TT)
                    for k in range(KD):
                        dve.wait_ge(t_full, Z + g * KD + k + 1)
                        nc.vector.tensor_copy(xT[:, k, :], ps_t[:, k % NT, :]).then_inc(t_read, 1)
                    dve.wait_ge(qk_out, Z + g * 64)
                    for m in range(QK_JOBS):
                        dve.wait_ge(qk_hi_ok, Z + g * QK_JOBS + m + 1)
                        nc.vector.tensor_tensor(qk_lo[:, m, :].bitcast(F32R), ps_a[:, m % NA, :], qk_hi[:, m, :],
                                                ALU.subtract).then_inc(a_read, 1)
                    dve.wait_ge(v_out, Z + g * 16)
                    for t in range(TT):
                        dve.wait_ge(v_full, Z + g * TT + t + 1)
                        nc.vector.tensor_copy(v[:, t, :], ps_v[:, t % NV, :]).then_inc(v_read, 1)


def attend(nc, a):
    R, NS, AHEAD = 4, 2, 2
    UQ = HG
    UB = NQT * UQ
    U = B * UB
    LATE = NQT // 2 * UQ
    NORM = 4
    SCALE = 1.0 / float(HD) ** 0.5
    HIGH = 3.0e38
    Z_ROWS = 2 * P
    with Scope(nc, "att") as s:
        ident = s.sb("ident", [P, P])
        mask = s.sb("mask", [P, L])
        q = s.sb("q", [P, B, HG, L])
        kT = s.sb("kT", [P, B, HG, L])
        v_rows = s.sb("v_rows", [P, B, NQT, P])
        v = s.sb("v", [P, B, NQT, HG, P])
        sm = s.sb("sm", [P, R, L])
        low = s.sb("low", [P, R])
        p = s.sb("p", [P, R, L])
        pT = s.sb("pT", [P, 2, NQT, P])
        total = s.sb("total", [P, NORM, HG])
        oT = s.sb("oT", [P, 2, P])
        rec = s.sb("rec", [P, 2, HG])
        o = s.sb("o", [P, B, NQT, HG, HD])
        zeros = s.sb("zeros", [P, Z_ROWS // P, D])
        ps_s = s.ps("ps_s", [P, NS, L])
        ps_t = s.ps("ps_t", [P, 2, 4, P])
        ps_o = s.ps("ps_o", [P, 2, 512])
        v_zero, v_ok, oT_ok, o_full = (s.sem(n) for n in ("v_zero", "v_ok", "oT_ok", "o_full"))
        consts, s_full, low_ok, exp_ok, t0_full, t1_full, e0_ok, e1_ok, pv_ok, rec_ok, norm_ok, z_ok = (s.sem(n) for n in (
            "consts", "s_full", "low_ok", "exp_ok", "t0_full", "t1_full", "e0_ok", "e1_ok", "pv_ok", "rec_ok", "norm_ok", "z_ok"))
        z_out = s.pool_dma_sem("z_out")
        g_in, o_out = s.sems("g_in", B), s.sems("o_out", B)
        block = s.block()
        G_LOADS = 2 * P // HD + 1

        def unit(u):
            return u // UB, u % UB // UQ, u % UQ

        def late(i, u):
            return i * B * LATE + (u // UB) * LATE + (u % UB - LATE)

        @block.sync
        def _(sp):
            sp.dma_start(ident[:, :], a["c_ident"]).then_inc(consts, 16)
            sp.dma_start(mask[:, :], a["c_mask"]).then_inc(consts, 16)

            def load(group, b):
                part = slice(b * L, (b + 1) * L)
                for n in range(P // HD):
                    r = slice(n * HD, (n + 1) * HD)
                    for dst, name, which in ((q, "s_q", n // 2), (kT, "s_k", n % 2)):
                        sp.dma_start(dst[r, b, :, :], a[name][bass.ds(group, 1), which, :, part].rearrange(
                            "g (h d) t -> d (g h) t", d=HD)).then_inc(g_in[b], 16)
                sp.dma_start(v_rows[:, b, :, :],
                             a["s_v"][part, bass.ds(group * P, P)].rearrange("(t p) n -> p t n", p=P)).then_inc(g_in[b], 16)

            def store(group, b):
                s.hold(sp, norm_ok, Z + (group * B + b + 1) * NQT + NORM)
                sp.dma_start(a["s_o"][b * L:(b + 1) * L, bass.ds(group * P, P)].rearrange("(t p) n -> p t n", p=P),
                             o[:, b, :, :, :].rearrange("p t h d -> p t (h d)")).then_inc(o_out[b], 16)

            for b in range(B):
                load(0, b)
            with sp.Fori(0, NHG - 1) as i:
                for b in range(B):
                    store(i, b)
                    load(i + 1, b)
            for b in range(B):
                store(NHG - 1, b)
            for b in range(B):
                sp.wait_ge(o_out[b], Z + NHG * 16)

        @block.gpsimd
        def _(pool):
            nc.gpsimd.memset(v[:, :, :, :, :], 0.0).then_inc(v_zero, 1)
            nc.gpsimd.memset(zeros[:, :, :], 0.0).then_inc(z_ok, 1)
            pool.wait_ge(z_ok, Z + 1)
            with pool.Fori(0, N_TILES * SLOT_TILE // Z_ROWS) as i:
                nc.gpsimd.dma_start(rows(a["s_xs"], i * Z_ROWS, Z_ROWS), zeros[:, :, :]).then_inc(z_out, 16)
            pool.wait_ge(v_zero, Z + 1)

            def place(group, b):
                s.hold(pool, g_in[b], Z + (group + 1) * G_LOADS * 16)
                for h in range(HG):
                    c = slice(h * HD, (h + 1) * HD)
                    nc.gpsimd.tensor_copy(v[:, b, :, h, c], v_rows[:, b, :, c]).then_inc(v_ok, 1)

            with pool.Fori(0, NHG) as i:
                for b in range(B):
                    place(i, b)
            pool.wait_ge(z_out, N_TILES * SLOT_TILE // Z_ROWS * 16)

        @block.tensor
        def _(pe):
            pe.wait_ge(consts, Z + 32)
            with pe.Fori(0, NHG) as i:

                def score(u):
                    b, t, h = unit(u)
                    if u % UB == 0:
                        pe.wait_ge(g_in[b], Z + (i + 1) * G_LOADS * 16)
                    pe.wait_ge(low_ok, Z + i * U + u + 1)
                    keys = (t + 1) * P
                    for k in range(0, keys, 512):
                        n = min(512, keys - k)
                        last = nc.tensor.matmul(ps_s[:, u % NS, k:k + n], q[:, b, h, t * P:(t + 1) * P].bitcast(F32R),
                                                kT[:, b, h, k:k + n].bitcast(F32R), start=True, stop=True)
                    last.then_inc(s_full, 1)

                def turn(u):
                    b, t, h = unit(u)
                    pe.wait_ge(exp_ok, Z + i * U + u + R + 1)
                    for half in range(t // 4 + 1):
                        if half == 0:
                            pe.wait_ge(e0_ok, Z + i * U + u)
                        else:
                            pe.wait_ge(e1_ok, Z + late(i, u))
                        for k in range(4 * half, min(4 * half + 4, t + 1)):
                            last = nc.tensor.transpose(ps_t[:, half, k % 4, :], p[:, u % R, k * P:(k + 1) * P], ident[:, :])
                        last.then_inc((t0_full, t1_full)[half], 1)

                def weigh(u):
                    b, t, h = unit(u)
                    if h == 0:
                        pe.wait_ge(norm_ok, Z + (i * B + b) * NQT + t + NORM - 1)
                        if t == 0:
                            pe.wait_ge(v_ok, Z + (i * B + b + 1) * HG)
                    pe.wait_ge(e0_ok, Z + i * U + u + 1)
                    if t >= 4:
                        pe.wait_ge(e1_ok, Z + late(i, u) + 1)
                    for k in range(t + 1):
                        last = nc.tensor.matmul(ps_o[:, t % 2, 0:P], v[:, b, k, h, :], pT[:, u % 2, k, :],
                                                start=(h == 0 and k == 0), stop=(h == HG - 1 and k == t))
                    last.then_inc(pv_ok, 1)

                def turn_back(n):
                    pe.wait_ge(oT_ok, Z + i * B * NQT + n + 1)
                    nc.tensor.transpose(ps_o[:, n % 2, P:2 * P], oT[:, n % 2, :], ident[:, :]).then_inc(o_full, 1)

                for u in range(AHEAD + 1):
                    score(u)
                for u in range(U):
                    if u + AHEAD + 1 < U:
                        score(u + AHEAD + 1)
                    turn(u)
                    if u:
                        weigh(u - 1)
                    if u >= UQ and u % UQ == 2:
                        turn_back(u // UQ - 1)
                weigh(U - 1)
                turn_back(U // UQ - 1)

        @block.scalar
        def _(act):
            nc.scalar.nop().then_inc(exp_ok, R)
            with act.Fori(0, NHG) as i:

                def exponential(u):
                    b, t, h = unit(u)
                    keys = (t + 1) * P
                    if h == 0:
                        act.wait_ge(norm_ok, Z + (i * B + b) * NQT + t + 1)
                    act.wait_ge(low_ok, Z + i * U + u + NS + 1)
                    act.wait_ge(pv_ok, Z + i * U + u + 1)
                    nc.scalar.activation(p[:, u % R, 0:keys], sm[:, u % R, 0:keys], ACT.Exp, bias=low[:, u % R:u % R + 1],
                                         scale=-1.0, accum_out=total[:, t % NORM, h:h + 1]).then_inc(exp_ok, 1)

                def read_out(n):
                    act.wait_ge(pv_ok, Z + i * U + (n + 1) * UQ + R)
                    nc.scalar.copy(oT[:, n % 2, :], ps_o[:, n % 2, 0:P]).then_inc(oT_ok, 1)

                for u in range(AHEAD):
                    exponential(u)
                for u in range(U):
                    if u + AHEAD < U:
                        exponential(u + AHEAD)
                    b, t, h = unit(u)
                    if t >= 4:
                        act.wait_ge(t1_full, Z + late(i, u) + 1)
                        act.wait_ge(pv_ok, Z + i * U + u + R - 1)
                        nc.scalar.copy(pT[:, u % 2, 4:t + 1, :], ps_t[:, 1, 0:t - 3, :]).then_inc(e1_ok, 1)
                    if u >= UQ and u % UQ == 1:
                        read_out(u // UQ - 1)
                read_out(U // UQ - 1)

        @block.vector
        def _(dve):
            nc.vector.nop().then_inc(low_ok, NS)
            nc.vector.nop().then_inc(norm_ok, NORM)
            nc.vector.nop().then_inc(pv_ok, R)
            dve.wait_ge(consts, Z + 32)
            with dve.Fori(0, NHG) as i:

                def bound(u):
                    b, t, h = unit(u)
                    keys = (t + 1) * P
                    dve.wait_ge(s_full, Z + i * U + u + 1)
                    s.hold(dve, exp_ok, Z + i * U + u + 1)
                    nc.vector.tensor_tensor_reduce(sm[:, u % R, 0:keys], ps_s[:, u % NS, 0:keys], mask[:, L - keys:L], -SCALE, HIGH,
                                                   ALU.add, ALU.min, low[:, u % R:u % R + 1]).then_inc(low_ok, 1)

                def normalise(n):
                    b, t = n // NQT, n % NQT
                    g = i * B * NQT + n
                    s.hold(dve, exp_ok, Z + i * U + (n + 1) * UQ + R)
                    dve.wait_ge(norm_ok, Z + g + NORM - 1)
                    nc.vector.reciprocal(rec[:, t % 2, :], total[:, t % NORM, :]).then_inc(rec_ok, 1)
                    s.hold(dve, o_full, Z + g + 1)
                    dve.wait_ge(rec_ok, Z + g + 1)
                    if t == 0:
                        dve.wait_ge(o_out[b], Z + i * 16)
                    nc.vector.tensor_tensor(o[:, b, t, :, :], ps_o[:, t % 2, P:2 * P].rearrange("p (h d) -> p h d", d=HD), rec[:, t % 2, :].unsqueeze(2).to_broadcast([P, HG, HD]),
                                            ALU.mult).then_inc(norm_ok, 1)

                for u in range(AHEAD):
                    bound(u)
                for u in range(U):
                    if u + AHEAD < U:
                        bound(u + AHEAD)
                    b, t, h = unit(u)
                    n = min(t + 1, 4)
                    dve.wait_ge(t0_full, Z + i * U + u + 1)
                    dve.wait_ge(pv_ok, Z + i * U + u + R - 1)
                    nc.vector.tensor_copy(pT[:, u % 2, 0:n, :], ps_t[:, 0, 0:n, :]).then_inc(e0_ok, 1)
                    if u >= UQ and u % UQ == 3:
                        normalise(u // UQ - 1)
                normalise(U // UQ - 1)


def attend_out(nc, a):
    NT, NP = 2, 4
    with Scope(nc, "att_out") as s:
        w = s.sb("w", [P, KD, D])
        ident = s.sb("ident", [P, P])
        o = s.sb("o", [P, NCH, TT, D])
        oT = s.sb("oT", [P, KD, CH])
        x = s.sb("x", [P, NCH, TT, D])
        xn = s.sb("xn", [P, NCH, TT, D])
        stats = s.sb("stats", [P, NCH, TT, 6])
        mv = s.sb("mv", [P, NCH, TT, 2])
        std = s.sb("std", [P, NCH, TT])
        rstd = s.sb("rstd", [P, NCH, TT])
        ps_t = s.ps("ps_t", [P, NT, CH])
        ps = s.ps("ps", [P, NP, D])
        consts, t_full, t_read, full, read, stats_ok, mv_ok, std_ok, rstd_ok, xn_ok = (s.sem(n) for n in (
            "consts", "t_full", "t_read", "full", "read", "stats_ok", "mv_ok", "std_ok", "rstd_ok", "xn_ok"))
        o_in, x_in, x_out, xn_out = (s.sems(n, NCH) for n in ("o_in", "x_in", "x_out", "xn_out"))
        block = s.block()

        @block.sync
        def _(sp):
            sp.dma_start(ident[:, :], a["c_ident"]).then_inc(consts, 16)
            sp.dma_start(w[:, :, :], a["w_o"].rearrange("(k p) n -> p k n", p=P)).then_inc(consts, 16)
            with sp.Fori(0, B) as i:
                for ch in range(NCH):
                    s.hold(sp, t_full, Z + i * NCH * KD)
                    sp.dma_start(o[:, ch, :, :], rows(a["s_o"], i * L + ch * CH, CH)).then_inc(o_in[ch], 16)
                    s.hold(sp, x_out[ch], Z + i * 16)
                    s.hold(sp, xn_ok, Z + i * NCH * TT)
                    sp.dma_start(x[:, ch, :, :], rows(a["s_x2"], i * L + ch * CH, CH)).then_inc(x_in[ch], 16)
                for ch in range(NCH):
                    g = i * NCH + ch
                    tok = i * L + ch * CH
                    s.hold(sp, read, Z + (g + 1) * TT + NP)
                    sp.dma_start(rows(a["s_x3"], tok, CH), x[:, ch, :, :]).then_inc(x_out[ch], 16)
                    s.hold(sp, xn_ok, Z + (g + 1) * TT)
                    sp.dma_start(rows(a["s_n3"], tok, CH), xn[:, ch, :, :]).then_inc(xn_out[ch], 16)
            for ch in range(NCH):
                sp.wait_ge(x_out[ch], Z + B * 16)
                sp.wait_ge(xn_out[ch], Z + B * 16)

        @block.tensor
        def _(pe):
            pe.wait_ge(consts, Z + 32)
            with pe.Fori(0, B) as i:
                for ch in range(NCH):
                    g = i * NCH + ch
                    pe.wait_ge(o_in[ch], Z + (i + 1) * 16)
                    for k in range(KD):
                        pe.wait_ge(t_read, Z + g * KD + k + 1)
                        for t in range(TT):
                            last = nc.tensor.transpose(ps_t[:, k % NT, t * P:(t + 1) * P], o[:, ch, t, k * P:(k + 1) * P], ident[:, :])
                        last.then_inc(t_full, 1)
                    pe.wait_ge(t_read, Z + (g + 1) * KD + NT)
                    for t in range(TT):
                        pe.wait_ge(read, Z + g * TT + t + 1)
                        for k in range(KD):
                            last = nc.tensor.matmul(ps[:, t, :], oT[:, k, t * P:(t + 1) * P], w[:, k, :],
                                                    start=(k == 0), stop=(k == KD - 1))
                        last.then_inc(full, 1)

        @block.scalar
        def _(act):
            nc.scalar.nop().then_inc(t_read, NT)
            with act.Fori(0, B) as i:
                for ch in range(NCH):
                    g = i * NCH + ch
                    act.wait_ge(full, Z + g * TT)
                    for k in range(KD):
                        act.wait_ge(t_full, Z + g * KD + k + 1)
                        nc.scalar.copy(oT[:, k, :], ps_t[:, k % NT, :]).then_inc(t_read, 1)
                    act.wait_ge(mv_ok, Z + (g + 1) * TT)
                    nc.scalar.activation(std[:, ch, :], mv[:, ch, :, 1], ACT.Sqrt, bias=EPS).then_inc(std_ok, 1)

        @block.vector
        def _(dve):
            nc.vector.nop().then_inc(read, NP)
            with dve.Fori(0, B) as i:
                for ch in range(NCH):
                    g = i * NCH + ch
                    dve.wait_ge(x_in[ch], Z + (i + 1) * 16)
                    for t in range(TT):
                        dve.wait_ge(full, Z + g * TT + t + 1)
                        nc.vector.tensor_tensor(x[:, ch, t, :], x[:, ch, t, :], ps[:, t, :], ALU.add).then_inc(read, 1)
                        dve.wait_ge(read, Z + g * TT + t + NP + 1)
                        nc.vector.bn_stats(stats[:, ch, t, :], x[:, ch, t, :]).then_inc(stats_ok, 1)
                    s.hold(dve, stats_ok, Z + (g + 1) * TT)
                    for t in range(TT):
                        nc.vector.bn_aggr(mv[:, ch, t, :], stats[:, ch, t, :]).then_inc(mv_ok, 1)
                    dve.wait_ge(std_ok, Z + g + 1)
                    nc.vector.reciprocal(rstd[:, ch, :], std[:, ch, :]).then_inc(rstd_ok, 1)
                    dve.wait_ge(rstd_ok, Z + g + 1)
                    dve.wait_ge(xn_out[ch], Z + i * 16)
                    for t in range(TT):
                        nc.vector.tensor_scalar(xn[:, ch, t, :], x[:, ch, t, :], mv[:, ch, t, 0:1], rstd[:, ch, t:t + 1],
                                                ALU.subtract, ALU.mult).then_inc(xn_ok, 1)


def shared_ffn(nc, a):
    NT, NG, NV = 2, 4, 2
    KS = I_SH // P
    with Scope(nc, "shr") as s:
        wg = s.sb("wg", [P, KD, I_SH])
        wu = s.sb("wu", [P, KD, I_SH])
        wd = s.sb("wd", [P, KS, D])
        cent = s.sb("cent", [P, KD, E])
        ident = s.sb("ident", [P, P])
        xn = s.sb("xn", [P, NCH, TT, D])
        x = s.sb("x", [P, NCH, TT, D])
        xT = s.sb("xT", [P, KD, CH])
        sg = s.sb("sg", [P, 2, CH])
        hT = s.sb("hT", [P, KS, CH])
        lg = s.sb("lg", [P, NCH, TT, E])
        ps_t = s.ps("ps_t", [P, NT, CH])
        ps_g = s.ps("ps_g", [P, NG, CH])
        ps_v = s.ps("ps_v", [P, NV, D])
        consts, t_full, t_read, g_full, silu_ok, h_ok, v_full, v_read = (s.sem(n) for n in (
            "consts", "t_full", "t_read", "g_full", "silu_ok", "h_ok", "v_full", "v_read"))
        xn_in, x_in, x_out, lg_out = (s.sems(n, NCH) for n in ("xn_in", "x_in", "x_out", "lg_out"))
        block = s.block()
        V_JOBS = 2 + TT

        @block.sync
        def _(sp):
            sp.dma_start(ident[:, :], a["c_ident"]).then_inc(consts, 16)
            sp.dma_start(cent[:, :, :], a["cent"].rearrange("(k p) n -> p k n", p=P)).then_inc(consts, 16)
            for dst, name in ((wg, "wg_s"), (wu, "wu_s"), (wd, "wd_s")):
                sp.dma_start(dst[:, :, :], a[name].rearrange("(k p) n -> p k n", p=P)).then_inc(consts, 16)
            with sp.Fori(0, B) as i:
                for ch in range(NCH):
                    s.hold(sp, t_full, Z + i * NCH * KD)
                    sp.dma_start(xn[:, ch, :, :], rows(a["s_n3"], i * L + ch * CH, CH)).then_inc(xn_in[ch], 16)
                    s.hold(sp, x_out[ch], Z + i * 16)
                    sp.dma_start(x[:, ch, :, :], rows(a["s_x3"], i * L + ch * CH, CH)).then_inc(x_in[ch], 16)
                for ch in range(NCH):
                    g = i * NCH + ch
                    s.hold(sp, v_read, Z + g * V_JOBS + NV + 2)
                    sp.dma_start(a["s_lg"][:, bass.ds(g * (TT * E), TT * E)], lg[:, ch, :, :].rearrange("p t e -> p (t e)")).then_inc(lg_out[ch], 16)
                    s.hold(sp, v_read, Z + (g + 1) * V_JOBS + NV)
                    sp.dma_start(rows(a["s_x4"], i * L + ch * CH, CH), x[:, ch, :, :]).then_inc(x_out[ch], 16)
            for ch in range(NCH):
                sp.wait_ge(x_out[ch], Z + B * 16)
                sp.wait_ge(lg_out[ch], Z + B * 16)

        @block.tensor
        def _(pe):
            pe.wait_ge(consts, Z + 80)
            with pe.Fori(0, B) as i:
                for ch in range(NCH):
                    g = i * NCH + ch
                    pe.wait_ge(xn_in[ch], Z + (i + 1) * 16)
                    for k in range(KD):
                        pe.wait_ge(t_read, Z + g * KD + k + 1)
                        for t in range(TT):
                            last = nc.tensor.transpose(ps_t[:, k % NT, t * P:(t + 1) * P], xn[:, ch, t, k * P:(k + 1) * P], ident[:, :])
                        last.then_inc(t_full, 1)
                    pe.wait_ge(t_read, Z + (g + 1) * KD + NT)
                    for t in range(TT):
                        if t % 2 == 0:
                            pe.wait_ge(v_read, Z + g * V_JOBS + t // 2 + 1)
                        for k in range(KD):
                            last = nc.tensor.matmul(ps_v[:, t // 2, (t % 2) * E:(t % 2 + 1) * E], xT[:, k, t * P:(t + 1) * P], cent[:, k, :],
                                                    start=(k == 0), stop=(k == KD - 1))
                        if t % 2:
                            last.then_inc(v_full, 1)
                    for m in range(KS):
                        for n, wt in enumerate((wg, wu)):
                            if n == 0:
                                pe.wait_ge(h_ok, Z + g * KS + m + 1)
                            for k in range(KD):
                                last = nc.tensor.matmul(ps_g[:, (2 * m + n) % NG, :], wt[:, k, m * P:(m + 1) * P], xT[:, k, :],
                                                        start=(k == 0), stop=(k == KD - 1))
                            last.then_inc(g_full, 1)
                    pe.wait_ge(h_ok, Z + (g + 1) * KS + 2)
                    for t in range(TT):
                        pe.wait_ge(v_read, Z + g * V_JOBS + 2 + t + 1)
                        for k in range(KS):
                            last = nc.tensor.matmul(ps_v[:, t % NV, :], hT[:, k, t * P:(t + 1) * P], wd[:, k, :],
                                                    start=(k == 0), stop=(k == KS - 1))
                        last.then_inc(v_full, 1)

        @block.scalar
        def _(act):
            with act.Fori(0, B) as i:
                for ch in range(NCH):
                    g = i * NCH + ch
                    for m in range(KS):
                        act.wait_ge(g_full, Z + g * 2 * KS + 2 * m + 1)
                        act.wait_ge(h_ok, Z + g * KS + m + 1)
                        nc.scalar.activation(sg[:, m % 2, :], ps_g[:, 2 * m % NG, :], ACT.Silu).then_inc(silu_ok, 1)

        @block.vector
        def _(dve):
            nc.vector.nop().then_inc(t_read, NT)
            nc.vector.nop().then_inc(h_ok, 2)
            nc.vector.nop().then_inc(v_read, NV)
            with dve.Fori(0, B) as i:
                for ch in range(NCH):
                    g = i * NCH + ch
                    dve.wait_ge(g_full, Z + g * 2 * KS)
                    for k in range(KD):
                        dve.wait_ge(t_full, Z + g * KD + k + 1)
                        nc.vector.tensor_copy(xT[:, k, :], ps_t[:, k % NT, :]).then_inc(t_read, 1)
                    dve.wait_ge(lg_out[ch], Z + i * 16)
                    for t in range(2):
                        dve.wait_ge(v_full, Z + g * V_JOBS + t + 1)
                        nc.vector.tensor_copy(lg[:, ch, 2 * t:2 * t + 2, :].rearrange("p t e -> p (t e)"), ps_v[:, t, 0:2 * E]).then_inc(v_read, 1)
                    dve.wait_ge(v_full, Z + g * V_JOBS)
                    for m in range(KS):
                        dve.wait_ge(silu_ok, Z + g * KS + m + 1)
                        dve.wait_ge(g_full, Z + g * 2 * KS + 2 * m + 2)
                        nc.vector.tensor_tensor(hT[:, m, :], sg[:, m % 2, :], ps_g[:, (2 * m + 1) % NG, :], ALU.mult).then_inc(h_ok, 1)
                    dve.wait_ge(x_in[ch], Z + (i + 1) * 16)
                    for t in range(TT):
                        dve.wait_ge(v_full, Z + g * V_JOBS + 2 + t + 1)
                        nc.vector.scalar_tensor_tensor(out=x[:, ch, t, :], in0=ps_v[:, t % NV, :], scalar=RATIO, in1=x[:, ch, t, :],
                                                       op0=ALU.mult, op1=ALU.add).then_inc(v_read, 1)


def route_tokens(nc, a):
    NTE = TOK_TILES * E
    K256 = T // SLOT_TILE
    with Scope(nc, "route") as s:
        lg = s.sb("lg", [P, TOK_TILES, E])
        gb = s.sb("gb", [P, E])
        rev = s.sb("rev", [P, E])
        full_at = s.sb("full_at", [P, K256])
        tile_no = s.sb("tile_no", [P, N_TILES])
        earlier = s.sb("earlier", [P, P])
        ones = s.sb("ones", [P, P])
        aff = s.sb("aff", [P, TOK_TILES, E])
        cand = s.sb("cand", [P, TOK_TILES, E])
        tmp = s.sb("tmp", [P, TOK_TILES, E])
        one = s.sb("one", [P, TOPK, TOK_TILES, E])
        both = s.sb("both", [P, TOK_TILES, E])
        top = s.sb("top", [P, TOK_TILES])
        ta = s.sb("ta", [P, TOPK, TOK_TILES])
        wsum = s.sb("wsum", [P, TOK_TILES])
        wt = s.sb("wt", [P, TOPK, TOK_TILES])
        run = s.sb("run", [P, 2, TOK_TILES, E])
        pos = s.sb("pos", [P, TOK_TILES, E])
        cmp = s.sb("cmp", [P, E, K256])
        tiles = s.sb("tiles", [P, E])
        cum = s.sb("cum", [P, 2, E])
        base = s.sb("base", [P, E])
        cmp_t = s.sb("cmp_t", [P, N_TILES, E])
        ex_f = s.sb("ex_f", [P, N_TILES])
        ex_i = s.sb("ex_i", [P, N_TILES], I32)
        slot = s.sb("slot", [P, TOPK, TOK_TILES])
        slot_i = s.sb("slot_i", [P, TOPK, TOK_TILES], I32)
        xn = s.sb("xn", [P, TOK_TILES, D])
        ps_w = s.ps("ps_w", [P, 512])
        ps_n = s.ps("ps_n", [P, 512])
        loads, xn_in, clamp_ok, exp_ok, both_ok, pref_ok, st, out_ok, outs = (s.sem(n) for n in (
            "loads", "xn_in", "clamp_ok", "exp_ok", "both_ok", "pref_ok", "st", "out_ok", "outs"))
        sent = s.pool_dma_sem("sent")
        block = s.block()

        @block.sync
        def _(sp):
            sp.dma_start(lg[:, :, :].rearrange("p t e -> p (t e)"), a["s_lg"]).then_inc(loads, 16)
            sp.dma_start(gb[:, :], a["gate_b"].to_broadcast([P, E])).then_inc(loads, 16)
            sp.dma_start(rev[:, :], a["c_rev"].to_broadcast([P, E])).then_inc(loads, 16)
            sp.dma_start(full_at[:, :], a["c_full_at"].to_broadcast([P, K256])).then_inc(loads, 16)
            sp.dma_start(tile_no[:, :], a["c_tile_no"].to_broadcast([P, N_TILES])).then_inc(loads, 16)
            sp.dma_start(earlier[:, :], a["c_before"]).then_inc(loads, 16)
            sp.dma_start(ones[:, :], a["c_ones"]).then_inc(loads, 16)
            sp.dma_start(xn[:, :, :], rows(a["s_n3"], 0, T)).then_inc(xn_in, 16)
            sp.wait_ge(out_ok, Z + 2)
            sp.dma_start(a["s_expert"], ex_i[0:1, :]).then_inc(outs, 16)
            sp.dma_start(a["s_slot"], slot_i[:, :, :].rearrange("p k t -> p (k t)")).then_inc(outs, 16)
            sp.dma_start(a["s_wt"], wt[:, :, :].rearrange("p k t -> p (k t)")).then_inc(outs, 16)
            sp.wait_ge(outs, Z + 48)

        @block.scalar
        def _(act):
            act.wait_ge(clamp_ok, Z + 1)
            nc.scalar.activation(aff[:, :, :], lg[:, :, :], ACT.Exp, scale=-1.0).then_inc(exp_ok, 1)

        @block.tensor
        def _(pe):
            pe.wait_ge(loads, Z + 7 * 16)
            pe.wait_ge(both_ok, Z + 1)
            m = both[:, :, :].rearrange("p t e -> p (t e)")
            nc.tensor.matmul(ps_w[:, 0:NTE], earlier[:, :], m, start=True, stop=True)
            nc.tensor.matmul(ps_n[:, 0:NTE], ones[:, :], m, start=True, stop=True).then_inc(pref_ok, 1)

        @block.vector
        def _(dve):
            steps = [0]

            def after(ins):
                steps[0] += 1
                ins.then_inc(st, 1)
                dve.wait_ge(st, Z + steps[0])

            v = nc.vector
            shape = [P, TOK_TILES, E]
            per_token = lambda x: x.unsqueeze(2).to_broadcast(shape)
            per_expert = lambda x: x.unsqueeze(1).to_broadcast(shape)
            dve.wait_ge(loads, Z + 7 * 16)
            v.tensor_scalar(lg[:, :, :], lg[:, :, :], -87.0, None, ALU.max).then_inc(clamp_ok, 1)
            dve.wait_ge(exp_ok, Z + 1)
            after(v.tensor_scalar(aff[:, :, :], aff[:, :, :], 1.0, None, ALU.add))
            after(v.reciprocal(aff[:, :, :], aff[:, :, :]))
            after(v.tensor_tensor(cand[:, :, :], aff[:, :, :], per_expert(gb[:, :]), ALU.add))
            for k in range(TOPK):
                after(v.tensor_reduce(top[:, :], cand[:, :, :], AX.X, ALU.max))
                after(v.tensor_tensor(tmp[:, :, :], cand[:, :, :], per_token(top[:, :]), ALU.is_equal))
                after(v.tensor_tensor(tmp[:, :, :], tmp[:, :, :], per_expert(rev[:, :]), ALU.mult))
                after(v.tensor_reduce(top[:, :], tmp[:, :, :], AX.X, ALU.max))
                after(v.tensor_tensor(one[:, k, :, :], per_expert(rev[:, :]), per_token(top[:, :]), ALU.is_equal))
                after(v.tensor_tensor(tmp[:, :, :], one[:, k, :, :], aff[:, :, :], ALU.mult))
                after(v.tensor_reduce(ta[:, k, :], tmp[:, :, :], AX.X, ALU.add))
                if k == 0:
                    after(v.scalar_tensor_tensor(out=cand[:, :, :], in0=one[:, 0, :, :], scalar=-3.0e38, in1=cand[:, :, :],
                                                 op0=ALU.mult, op1=ALU.add))
            v.tensor_tensor(both[:, :, :], one[:, 0, :, :], one[:, 1, :, :], ALU.add).then_inc(both_ok, 1)
            after(v.tensor_tensor(wsum[:, :], ta[:, 0, :], ta[:, 1, :], ALU.add))
            after(v.tensor_scalar(wsum[:, :], wsum[:, :], RT_EPS, None, ALU.add))
            after(v.reciprocal(wsum[:, :], wsum[:, :]))
            after(v.tensor_tensor(wt[:, :, :], ta[:, :, :], wsum[:, :].unsqueeze(1).to_broadcast([P, TOPK, TOK_TILES]), ALU.mult))
            dve.wait_ge(pref_ok, Z + 1)
            after(v.tensor_copy(run[:, 0, :, :].rearrange("p t e -> p (t e)"), ps_n[:, 0:NTE]))
            src, width = 0, 1
            while width < TOK_TILES:
                after(v.tensor_copy(run[:, 1 - src, 0:width, :], run[:, src, 0:width, :]))
                after(v.tensor_tensor(run[:, 1 - src, width:, :], run[:, src, width:, :], run[:, src, 0:TOK_TILES - width, :], ALU.add))
                src, width = 1 - src, 2 * width
            total = run[:, src, TOK_TILES - 1, :]
            after(v.tensor_tensor(cmp[:, :, :], total.unsqueeze(2).to_broadcast([P, E, K256]),
                                  full_at[:, :].unsqueeze(1).to_broadcast([P, E, K256]), ALU.is_gt))
            after(v.tensor_reduce(tiles[:, :], cmp[:, :, :], AX.X, ALU.add))
            after(v.tensor_copy(cum[:, 0, :], tiles[:, :]))
            cs, width = 0, 1
            while width < E:
                after(v.tensor_copy(cum[:, 1 - cs, 0:width], cum[:, cs, 0:width]))
                after(v.tensor_tensor(cum[:, 1 - cs, width:], cum[:, cs, width:], cum[:, cs, 0:E - width], ALU.add))
                cs, width = 1 - cs, 2 * width
            after(v.tensor_tensor(base[:, :], cum[:, cs, :], tiles[:, :], ALU.subtract))
            after(v.tensor_scalar(base[:, :], base[:, :], float(SLOT_TILE), None, ALU.mult))
            after(v.tensor_tensor(pos[:, :, :].rearrange("p t e -> p (t e)"), ps_w[:, 0:NTE],
                                  run[:, src, :, :].rearrange("p t e -> p (t e)"), ALU.add))
            after(v.tensor_tensor(pos[:, :, :].rearrange("p t e -> p (t e)"), pos[:, :, :].rearrange("p t e -> p (t e)"),
                                  ps_n[:, 0:NTE], ALU.subtract))
            after(v.tensor_tensor(pos[:, :, :], pos[:, :, :], per_expert(base[:, :]), ALU.add))
            for k in range(TOPK):
                after(v.tensor_tensor(tmp[:, :, :], one[:, k, :, :], pos[:, :, :], ALU.mult))
                after(v.tensor_reduce(slot[:, k, :], tmp[:, :, :], AX.X, ALU.add))
            v.tensor_copy(slot_i[:, :, :], slot[:, :, :]).then_inc(out_ok, 1)
            after(v.tensor_tensor(cmp_t[:, :, :], cum[:, cs, :].unsqueeze(1).to_broadcast([P, N_TILES, E]),
                                  tile_no[:, :].unsqueeze(2).to_broadcast([P, N_TILES, E]), ALU.is_le))
            after(v.tensor_reduce(ex_f[:, :], cmp_t[:, :, :], AX.X, ALU.add))
            after(v.tensor_scalar(ex_f[:, :], ex_f[:, :], float(E - 1), None, ALU.min))
            v.tensor_copy(ex_i[:, :], ex_f[:, :]).then_inc(out_ok, 1)

        @block.gpsimd
        def _(pool):
            pool.wait_ge(xn_in, Z + 16)
            pool.wait_ge(out_ok, Z + 1)
            for k in range(TOPK):
                for j in range(TOK_TILES):
                    nc.gpsimd.indirect_dma_start(a["s_xs"], bass.IndirectOffsetOnAxis(ap=slot_i[:, k, j:j + 1].bitcast(U32), axis=0),
                                                 xn[:, j, :], None).then_inc(sent, 16)
            pool.wait_ge(sent, 16 * TOPK * TOK_TILES)


def experts(nc, a):
    ST = SLOT_TILE // P
    KI = I_E // P
    W = 2
    with Scope(nc, "moe") as s:
        ex = s.sb("ex", [1, N_TILES], I32)
        ident = s.sb("ident", [P, P])
        wg = s.sb("wg", [P, W, KD, I_E])
        wu = s.sb("wu", [P, W, KD, I_E])
        wd = s.sb("wd", [P, W, KI, D])
        xs = s.sb("xs", [P, W, ST, D])
        xT = s.sb("xT", [P, W, KD, SLOT_TILE])
        sg = s.sb("sg", [P, W, KI * SLOT_TILE])
        hT = s.sb("hT", [P, W, KI, SLOT_TILE])
        y = s.sb("y", [P, W, ST, D])
        ps_t = s.ps("ps_t", [P, 2, 2, SLOT_TILE])
        ps_g = s.ps("ps_g", [P, 2, KI * SLOT_TILE])
        ps_u = s.ps("ps_u", [P, 2, KI * SLOT_TILE])
        ps_y = s.ps("ps_y", [P, ST, D])
        consts, ex_in, t_full, t_read, g_full, u_full, silu_ok, h_ok, y_full, y_read = (s.sem(n) for n in (
            "consts", "ex_in", "t_full", "t_read", "g_full", "u_full", "silu_ok", "h_ok", "y_full", "y_read"))
        w_in, x_in, y_out = (s.sems(n, W) for n in ("w_in", "x_in", "y_out"))
        block = s.block()
        PAIRS = N_TILES // W

        @block.sync
        def _(sp):
            def load_x(j, w):
                sp.dma_start(xs[:, w, :, :], rows(a["s_xs"], j * SLOT_TILE, SLOT_TILE)).then_inc(x_in[w], 16)

            def load_w(j, w):
                e = sp.value_load(ex[0:1, bass.ds(j, 1)], min_val=0, max_val=E - 1)
                for dst, name in ((wg, "wg"), (wu, "wu"), (wd, "wd")):
                    sp.dma_start(dst[:, w, :, :], a[name][bass.ds(e, 1), :, :].rearrange("e (k p) n -> p (e k) n", p=P)).then_inc(w_in[w], 16)

            def store(j, w):
                s.hold(sp, y_read, Z + (j + 1) * ST + ST)
                sp.dma_start(rows(a["s_ys"], j * SLOT_TILE, SLOT_TILE), y[:, w, :, :]).then_inc(y_out[w], 16)

            def load_after(j, w):
                s.hold(sp, t_full, Z + (j + 1) * 2)
                load_x(j + W, w)
                s.hold(sp, y_full, Z + (j + 1) * ST)
                load_w(j + W, w)

            sp.dma_start(ident[:, :], a["c_ident"]).then_inc(consts, 16)
            sp.dma_start(ex[:, :], a["s_expert"]).then_inc(ex_in, 16)
            for w in range(W):
                load_x(w, w)
            sp.wait_ge(ex_in, Z + 16)
            for w in range(W):
                load_w(w, w)
            with sp.Fori(0, PAIRS - 1) as i:
                for w in range(W):
                    load_after(i * W + w, w)
                    store(i * W + w, w)
            for j in range((PAIRS - 1) * W, N_TILES):
                if j + W < N_TILES:
                    load_after(j, j % W)
                store(j, j % W)
            for w in range(W):
                sp.wait_ge(y_out[w], Z + (N_TILES - w + 1) // W * 16)

        @block.tensor
        def _(pe):
            def turn(j, w, n):
                pe.wait_ge(x_in[w], Z + (n + 1) * 16)
                for kk in range(2):
                    pe.wait_ge(t_read, Z + j * 2 + kk + 1)
                    for k in range(2):
                        for t in range(ST):
                            last = nc.tensor.transpose(ps_t[:, kk, k, t * P:(t + 1) * P],
                                                       xs[:, w, t, (2 * kk + k) * P:(2 * kk + k + 1) * P], ident[:, :])
                    last.then_inc(t_full, 1)

            def step(j, w, n, more):
                pe.wait_ge(t_read, Z + (j + 1) * 2 + 2)
                pe.wait_ge(w_in[w], Z + (n + 1) * 48)
                pe.wait_ge(h_ok, Z + j + 1)
                for ps, wt, done in ((ps_g, wg, g_full), (ps_u, wu, u_full)):
                    for m in range(KI):
                        for k in range(KD):
                            last = nc.tensor.matmul(ps[:, w, m * SLOT_TILE:(m + 1) * SLOT_TILE], wt[:, w, k, m * P:(m + 1) * P],
                                                    xT[:, w, k, :], start=(k == 0), stop=(k == KD - 1))
                    last.then_inc(done, 1)
                if more:
                    turn(j + 1, 1 - w, n + w)
                pe.wait_ge(h_ok, Z + j + 1 + W)
                for t in range(ST):
                    pe.wait_ge(y_read, Z + j * ST + t + 1)
                    for m in range(KI):
                        last = nc.tensor.matmul(ps_y[:, t, :], hT[:, w, m, t * P:(t + 1) * P], wd[:, w, m, :],
                                                start=(m == 0), stop=(m == KI - 1))
                    last.then_inc(y_full, 1)

            pe.wait_ge(consts, Z + 16)
            turn(0, 0, 0)
            with pe.Fori(0, PAIRS) as i:
                for w in range(W):
                    step(i * W + w, w, i, True)
            step(N_TILES - 1, 0, PAIRS, False)

        @block.scalar
        def _(act):
            def step(j, w, n):
                act.wait_ge(g_full, Z + j + 1)
                act.wait_ge(h_ok, Z + j + 1)
                nc.scalar.activation(sg[:, w, :], ps_g[:, w, :], ACT.Silu).then_inc(silu_ok, 1)
                act.wait_ge(y_out[w], Z + n * 16)
                for t in range(ST):
                    act.wait_ge(y_full, Z + j * ST + t + 1)
                    nc.scalar.copy(y[:, w, t, :], ps_y[:, t, :]).then_inc(y_read, 1)

            nc.scalar.nop().then_inc(y_read, ST)
            with act.Fori(0, PAIRS) as i:
                for w in range(W):
                    step(i * W + w, w, i)
            step(N_TILES - 1, 0, PAIRS)

        @block.vector
        def _(dve):
            def turned(j, w):
                if not isinstance(j, int) or j >= 1:
                    dve.wait_ge(u_full, Z + j - 1)
                for kk in range(2):
                    dve.wait_ge(t_full, Z + j * 2 + kk + 1)
                    nc.vector.tensor_copy(xT[:, w, 2 * kk:2 * kk + 2, :], ps_t[:, kk, :, :]).then_inc(t_read, 1)

            def step(j, w, more):
                dve.wait_ge(silu_ok, Z + j + 1)
                dve.wait_ge(u_full, Z + j + 1)
                nc.vector.tensor_tensor(hT[:, w, :, :].rearrange("p m t -> p (m t)"), sg[:, w, :], ps_u[:, w, :],
                                        ALU.mult).then_inc(h_ok, 1)
                if more:
                    turned(j + 1, 1 - w)

            nc.vector.nop().then_inc(t_read, 2)
            nc.vector.nop().then_inc(h_ok, W)
            turned(0, 0)
            with dve.Fori(0, PAIRS) as i:
                for w in range(W):
                    step(i * W + w, w, True)
            step(N_TILES - 1, 0, False)


def combine(nc, a):
    with Scope(nc, "end") as s:
        slot = s.sb("slot", [P, TOPK, TOK_TILES], I32)
        wt = s.sb("wt", [P, TOPK, TOK_TILES])
        got = s.sb("got", [P, TOPK, TOK_TILES, D])
        x = s.sb("x", [P, TOK_TILES, D])
        slot_in, wt_in, add_ok, out_sent = (s.sem(n) for n in ("slot_in", "wt_in", "add_ok", "out_sent"))
        x_in = s.sems("x_in", NCH * B)
        got_in = [s.pool_dma_sem(f"got_in{j}") for j in range(TOK_TILES)]
        block = s.block()

        @block.sync
        def _(sp):
            sp.dma_start(slot[:, :, :].rearrange("p k t -> p (k t)"), a["s_slot"]).then_inc(slot_in, 16)
            sp.dma_start(wt[:, :, :].rearrange("p k t -> p (k t)"), a["s_wt"]).then_inc(wt_in, 16)
            for g in range(NCH * B):
                sp.dma_start(x[:, g * TT:(g + 1) * TT, :], rows(a["s_x4"], g * CH, CH)).then_inc(x_in[g], 16)
            for g in range(NCH * B):
                sp.wait_ge(add_ok, Z + (g + 1) * TT * TOPK)
                sp.dma_start(rows(a["out"], g * CH, CH), x[:, g * TT:(g + 1) * TT, :]).then_inc(out_sent, 16)
            sp.wait_ge(out_sent, Z + NCH * B * 16)

        @block.gpsimd
        def _(pool):
            pool.wait_ge(slot_in, Z + 16)
            for j in range(TOK_TILES):
                for k in range(TOPK):
                    nc.gpsimd.indirect_dma_start(got[:, k, j, :], None, a["s_ys"],
                                                 bass.IndirectOffsetOnAxis(ap=slot[:, k, j:j + 1].bitcast(U32), axis=0)).then_inc(got_in[j], 16)

        @block.vector
        def _(dve):
            dve.wait_ge(wt_in, Z + 16)
            for j in range(TOK_TILES):
                if j % TT == 0:
                    dve.wait_ge(x_in[j // TT], Z + 16)
                dve.wait_ge(got_in[j], TOPK * 16)
                for k in range(TOPK):
                    if k:
                        dve.wait_ge(add_ok, Z + j * TOPK + k)
                    nc.vector.scalar_tensor_tensor(out=x[:, j, :], in0=got[:, k, j, :], scalar=wt[:, k, j:j + 1], in1=x[:, j, :],
                                                   op0=ALU.mult, op1=ALU.add).then_inc(add_ok, 1)


SCRATCH = {
    "s_b": ((P, T), F32), "s_c": ((3, NC_T, P, T), BF16),
    "s_delta": ((NC_T, P, T), F32), "s_du": ((NC_T, P, T), F32),
    "s_x1": ((T, D), F32), "s_n1": ((T, D), F32), "s_x2": ((T, D), F32),
    "s_score": ((P, TOK_TILES), F32), "s_score_row": ((1, T), F32), "s_dest": ((P, TOK_TILES), I32),
    "s_sel_in": ((T, D), F32), "s_sel_out": ((T, D), F32),
    "s_q": ((NHG, 2, P, T), F32), "s_k": ((NHG, 2, P, T), F32), "s_v": ((T, D), F32),
    "s_xs": ((N_TILES * SLOT_TILE, D), F32), "s_ys": ((N_TILES * SLOT_TILE, D), F32),
    "s_o": ((T, D), F32), "s_x3": ((T, D), F32), "s_n3": ((T, D), F32), "s_x4": ((T, D), F32),
    "s_expert": ((1, N_TILES), I32), "s_slot": ((P, TOPK * TOK_TILES), I32), "s_wt": ((P, TOPK * TOK_TILES), F32),
    "s_lg": ((P, TOK_TILES * E), F32),
    "s_y": ((NC_T, P, T), F32),
    "s_u": ((NC_T, P, T), F32), "s_z": ((NC_T, P, T), F32),
}
PHASES = [project_in, selective_scan, mix_out, rank_tokens, select_ffn, attend_in,
          attend, attend_out, shared_ffn,
          route_tokens, experts, combine]


def build(nc, a):
    for phase in PHASES:
        phase(nc, a)


def layout(inputs):
    import numpy as np

    v = {k: np.asarray(x) for k, x in inputs.items()}
    per_channel = lambda x: np.ascontiguousarray(x.reshape(NC_T, P, *x.shape[1:]).swapaxes(0, 1))
    w = v["L0_attn_W_in"]
    z, x, bm, cm, dtl = np.split(w, np.cumsum([D_INNER, P, P, D_INNER]), axis=0)
    cm = cm.reshape(NC_T, GPT, N_QUAD, 4, D).transpose(0, 2, 3, 1, 4).reshape(D_INNER, D)
    out = {
        "x": v["L0_attn_hidden_states"].reshape(T, D),
        "w_in": np.ascontiguousarray(np.concatenate([z, cm, dtl, x, bm]).T),
        "w_dt": np.ascontiguousarray(v["L0_attn_W_dt"].T),
        "b_dt": per_channel(v["L0_attn_b_dt"]),
        "conv_w": per_channel(v["L0_attn_conv_w"][:, 0, :]),
        "conv_b": per_channel(v["L0_attn_conv_b"]),
        "a_log": per_channel(v["L0_attn_A_log"]),
        "d_param": per_channel(v["L0_attn_D_param"]),
        "w_out": np.ascontiguousarray(v["L0_attn_W_out"].T),
        "w_r": v["L0_ffn_w_r"].reshape(1, D),
        "b_r": v["L0_ffn_b_r"].reshape(1, 1),
        "w1": v["L0_ffn_w1"],
        "b1": np.ascontiguousarray(v["L0_ffn_b1"].reshape(KF, P).T),
        "w2": v["L0_ffn_w2"],
        "b2": v["L0_ffn_b2"].reshape(1, D),
        "w_qkv": np.ascontiguousarray(v["L1_attn_w_project"].T),
        "w_o": np.ascontiguousarray(v["L1_attn_w_out"].T),
        "cent": np.ascontiguousarray(v["L1_ffn_centroids"].T),
        "gate_b": v["L1_ffn_gate_bias"].reshape(1, E),
        "wg_s": v["L1_ffn_wg_s"], "wu_s": v["L1_ffn_wu_s"], "wd_s": v["L1_ffn_wd_s"],
        "wg": v["L1_ffn_wg"], "wu": v["L1_ffn_wu"], "wd": v["L1_ffn_wd"],
    }
    p = np.arange(P)
    out["c_ident"] = np.eye(P, dtype=np.float32)
    rep = np.zeros((P, NC_T, P), np.float32)
    for c in range(NC_T):
        rep[16 * c + p % 16, c, p] = 1
    out["c_rep"] = rep
    sel = np.zeros((3, 4, GPT, 4, P), np.float32)
    for n in range(4):
        for g in range(GPT):
            sel[:, n, g, n, 16 * g:16 * g + 16] = 1
    out["c_sel"] = sel.reshape(C_ROWS, 4, P)
    mask = np.zeros((P, L), np.float32)
    mask[:, L - P:] = np.where(p[None, :] > p[:, None], np.float32(NEG), np.float32(0))
    out["c_mask"] = mask
    out["c_earlier"] = (p[None, :] < p[:, None]).astype(np.float32)
    out["c_before"] = (p[:, None] < p[None, :]).astype(np.float32)
    out["c_rev"] = (E - np.arange(E, dtype=np.float32)).reshape(1, E)
    out["c_full_at"] = (SLOT_TILE * np.arange(T // SLOT_TILE, dtype=np.float32)).reshape(1, -1)
    out["c_tile_no"] = np.arange(N_TILES, dtype=np.float32).reshape(1, -1)
    out["c_ones"] = np.ones((P, P), np.float32)
    return out


def kernel(**inputs):
    import numpy as _np
    import concourse.bacc as _bacc
    from concourse import mybir as _mybir
    from concourse.bass_utils import run_bass_kernel_spmd as _run

    nc = _bacc.Bacc("TRN2", target_bir_lowering=False, num_devices=1)
    arrays, args = {}, {}
    for name, arr in layout(inputs).items():
        arrays[f"in_{name}"] = arr
        args[name] = nc.dram_tensor(f"in_{name}", arr.shape, _mybir.dt.from_np(arr.dtype), kind="ExternalInput").ap()
    for name, (shape, dt) in SCRATCH.items():
        args[name] = nc.dram_tensor(name, shape, dt).ap()
    args["out"] = nc.dram_tensor("out_0_dram", (T, D), F32, kind="ExternalOutput").ap()
    build(nc, args)
    r = _run(nc, [arrays], core_ids=[0])
    return r.results[0]["out_0_dram"].reshape(B, L, D)
```

```python
from contextlib import ExitStack

import concourse.bass as bass
from concourse import mybir

F32 = mybir.dt.float32
F32R = mybir.dt.float32r
BF16 = mybir.dt.bfloat16
I32 = mybir.dt.int32
U32 = mybir.dt.uint32
ALU = mybir.AluOpType
ACT = mybir.ActivationFunctionType
AX = mybir.AxisListType

P = 128
B, L, D = 2, 1024, 512
T = B * L
KD = D // P
CH = 512
NCH = L // CH
TT = CH // P
EPS = 1e-5
Z = 1

D_INNER, D_STATE, D_CONV = 1024, 16, 4
NC_T = D_INNER // P
GPT = P // D_STATE
HALO = D_CONV - 1
C_ROWS = 3 * 32
N_QUAD = D_STATE // 4

DF = 2048
KF = DF // P
K_SEL = L // 2

NH, HD = 16, 32
HG = P // HD
NHG = NH // HG
NQT = L // P
NEG = -1.0e9

E, TOPK, I_E = 16, 2, 256
I_SH = 512
RATIO = 0.1
RT_EPS = 1e-9
SLOT_TILE = 256
N_TILES = (T * TOPK) // SLOT_TILE + E - 1
TOK_TILES = T // P


class Scope:

    def __init__(self, nc, name):
        self.nc, self.name, self.stack, self.held = nc, name, ExitStack(), []
        self.at_zero = []

    def __enter__(self):
        self.stack.__enter__()
        return self

    def __exit__(self, *a):
        self.stack.__exit__(*a)
        self.nc.clear_and_free_semaphores(self.held)

    def sb(self, name, shape, dt=F32):
        return self.stack.enter_context(self.nc.sbuf_tensor(f"{self.name}_{name}", shape, dt))

    def ps(self, name, shape, dt=F32):
        return self.stack.enter_context(self.nc.psum_tensor(f"{self.name}_{name}", shape, dt))

    def sem(self, name):
        self.held.append(self.nc.alloc_semaphore(name=f"{self.name}_{name}"))
        return self.held[-1]

    def pool_dma_sem(self, name):
        self.at_zero.append(self.sem(name))
        return self.at_zero[-1]

    def sems(self, name, n):
        return [self.sem(f"{name}{i}") for i in range(n)]

    def block(self):
        self.passed = self.sem("passed")
        for sem in self.held:
            if sem not in self.at_zero:
                self.nc.gpsimd.sem_inc(sem, Z)
        self.nc.all_engine_barrier()
        return self.stack.enter_context(self.nc.Block())

    def hold(self, eng, sem, value):
        eng.wait_ge(sem, value)
        eng.sem_inc(self.passed, 1)


def rows(ap, start, n):
    return ap[bass.ds(start, n), :].rearrange("(t p) n -> p t n", p=P)


def cols(ap, start, n):
    return ap[:, :, bass.ds(start, n)].rearrange("c p t -> p c t")



def exact_product(nc, dst, lhs, rhs):
    parts = [(l[m].bitcast(F32R), r[n].bitcast(F32R)) for l, r in zip(lhs, rhs) for m, n in ((0, 0), (0, 1), (1, 0))]
    for i, (l, r) in enumerate(parts):
        last = nc.tensor.matmul(dst, l, r, start=(i == 0), stop=(i == len(parts) - 1))
    return last


def over_chunks(eng, chunk):
    with eng.Fori(0, B - 1) as i:
        for ch in range(NCH):
            chunk(i, ch, True, True)
    for ch in range(NCH):
        chunk(B - 1, ch, ch + 1 < NCH, ch + 2 < NCH)


def project_in(nc, a):
    M_Z, M_C, M_DT, M_X, M_B = 0, NC_T, 2 * NC_T, 2 * NC_T + 1, 2 * NC_T + 2
    NT, NV, NA = 2, 2, 4
    T_JOBS, V_JOBS, A_JOBS = KD, NC_T + 1, 2 + 3 * NC_T
    J_DT, J_XR, J_Z = 2, 2 + NC_T, 2 + 2 * NC_T
    N_CONST = 6
    with Scope(nc, "proj") as s:
        w_in = s.sb("w_in", [P, KD, (M_B + 1) * P])
        w_dt = s.sb("w_dt", [P, D_INNER])
        ident = s.sb("ident", [P, P])
        rep = s.sb("rep", [P, NC_T, P])
        bdt = s.sb("bdt", [P, NC_T])
        bdt2 = s.sb("bdt2", [P, NC_T])
        cw = s.sb("cw", [P, NC_T, D_CONV])
        cb = s.sb("cb", [P, NC_T])
        x = s.sb("x", [P, NCH, TT, D])
        stats = s.sb("stats", [P, NCH, TT, 6])
        mv = s.sb("mv", [P, NCH, TT, 2])
        std = s.sb("std", [P, NCH, TT])
        rstd = s.sb("rstd", [P, NCH, TT])
        xnT = s.sb("xnT", [P, NCH, KD, CH])
        dtl_x = s.sb("dtl_x", [P, 2, CH])
        xr = s.sb("xr", [P, NC_T, HALO + CH])
        conv = s.sb("conv", [P, NC_T, CH])
        dt_x = s.sb("dt_x", [P, NC_T, CH])
        dt_e = s.sb("dt_e", [P, NC_T, CH])
        dt_l = s.sb("dt_l", [P, NC_T, CH])
        dt_d = s.sb("dt_d", [P, NC_T, CH])
        c_hi = s.sb("c_hi", [P, 2, CH], BF16)
        c_res = s.sb("c_res", [P, 2, CH])
        c_mid = s.sb("c_mid", [P, 2, CH], BF16)
        c_lo = s.sb("c_lo", [P, 2, CH], BF16)
        z = s.sb("z", [P, 2, CH])
        bT = s.sb("bT", [P, CH])

        ps_t = s.ps("ps_t", [P, NT, CH])
        ps_v = s.ps("ps_v", [P, NV, CH])
        ps_a = s.ps("ps_a", [P, NA, CH])

        consts, stats_ok, mv_ok, std_ok, rstd_ok, xn_ok = (s.sem(n) for n in (
            "consts", "stats_ok", "mv_ok", "std_ok", "rstd_ok", "xn_ok"))
        x_in = s.sems("x_in", NCH)
        t_full, t_read, v_full, v_read, a_full, a_read = (s.sem(n) for n in (
            "t_full", "t_read", "v_full", "v_read", "a_full", "a_read"))
        hi_ok, mid_ok, lo_ok = (s.sem(n) for n in ("hi_ok", "mid_ok", "lo_ok"))
        halo_ok, bdt2_ok, conv_step, u_ok = (s.sem(n) for n in ("halo_ok", "bdt2_ok", "conv_step", "u_ok"))
        abs_ok, exp_ok, ln_ok, sp_step, delta_ok, du_ok = (s.sem(n) for n in (
            "abs_ok", "exp_ok", "ln_ok", "sp_step", "delta_ok", "du_ok"))
        c_out, z_out = s.sems("c_out", 2), s.sems("z_out", 2)
        w_ok = s.sems("w_ok", 3)
        b_out, u_out, delta_out, du_out = (s.sem(n) for n in ("b_out", "u_out", "delta_out", "du_out"))
        block = s.block()
        SP_STEPS = 4

        @block.sync
        def _(sp):
            sp.dma_start(x[:, 0, :, :], rows(a["x"], 0, CH)).then_inc(x_in[0], 16)
            for dst, name in ((ident[:, :], "c_ident"), (w_dt[:, :], "w_dt"), (rep[:, :, :], "c_rep"),
                              (bdt[:, :], "b_dt"), (cw[:, :, :], "conv_w"), (cb[:, :], "conv_b")):
                sp.dma_start(dst, a[name]).then_inc(consts, 16)
            for n, m in enumerate(((M_DT, M_B + 1), (M_C, M_DT), (M_Z, M_C))):
                c = slice(m[0] * P, m[1] * P)
                sp.dma_start(w_in[:, :, c], a["w_in"][:, c].rearrange("(k p) n -> p k n", p=P)).then_inc(w_ok[n], 16)
            def chunk(i, ch, more, more_2):
                g = i * NCH + ch
                tok = i * L + ch * CH
                if more:
                    s.hold(sp, t_full, Z + g * T_JOBS)
                    sp.dma_start(x[:, 1 - ch, :, :], rows(a["x"], tok + CH, CH)).then_inc(x_in[1 - ch], 16)
                s.hold(sp, v_read, Z + g * V_JOBS + NV + 1)
                sp.dma_start(a["s_b"][:, bass.ds(tok, CH)], bT[:, :]).then_inc(b_out, 16)
                for c in range(NC_T):
                    s.hold(sp, lo_ok, Z + g * NC_T + c + 1)
                    for n, part in enumerate((c_hi, c_mid, c_lo)):
                        sp.dma_start(a["s_c"][n, c, :, bass.ds(tok, CH)], part[:, c % 2, :]).then_inc(c_out[c % 2], 16)
                s.hold(sp, u_ok, Z + (g + 1) * NC_T)
                sp.dma_start(cols(a["s_u"], tok, CH), conv[:, :, :]).then_inc(u_out, 16)
                for c in range(NC_T):
                    s.hold(sp, a_read, Z + g * A_JOBS + J_Z + c + NA + 1)
                    sp.dma_start(a["s_z"][c, :, bass.ds(tok, CH)], z[:, c % 2, :]).then_inc(z_out[c % 2], 16)
                s.hold(sp, delta_ok, Z + g + 1)
                sp.dma_start(cols(a["s_delta"], tok, CH), dt_l[:, :, :]).then_inc(delta_out, 16)
                s.hold(sp, du_ok, Z + g + 1)
                sp.dma_start(cols(a["s_du"], tok, CH), dt_e[:, :, :]).then_inc(du_out, 16)

            over_chunks(sp, chunk)
            for r in range(2):
                sp.wait_ge(c_out[r], Z + B * NCH * NC_T // 2 * 3 * 16)
                sp.wait_ge(z_out[r], Z + B * NCH * NC_T // 2 * 16)
            for done in (b_out, u_out, delta_out, du_out):
                sp.wait_ge(done, Z + B * NCH * 16)

        @block.gpsimd
        def _(pool):
            def chunk(i, ch, more, more_2):
                g = i * NCH + ch
                for c in range(NC_T):
                    n = g * NC_T + c
                    s.hold(pool, v_read, Z + g * V_JOBS + c + NV + 2)
                    s.hold(pool, c_out[c % 2], Z + (g * (NC_T // 2) + c // 2) * 48)
                    nc.gpsimd.tensor_copy(c_mid[:, c % 2, :], c_res[:, c % 2, :]).then_inc(mid_ok, 1)
                    pool.wait_ge(mid_ok, Z + n + 1)
                    nc.gpsimd.tensor_tensor(c_lo[:, c % 2, :], c_res[:, c % 2, :], c_mid[:, c % 2, :],
                                            ALU.subtract).then_inc(lo_ok, 1)

            over_chunks(pool, chunk)

        @block.tensor
        def _(pe):
            def turn(j, slot):
                pe.wait_ge(xn_ok, Z + (j + 1) * TT)
                for k in range(KD):
                    pe.wait_ge(t_read, Z + j * T_JOBS + k + 1)
                    for t in range(TT):
                        last = nc.tensor.transpose(ps_t[:, k % NT, t * P:(t + 1) * P],
                                                   x[:, slot, t, k * P:(k + 1) * P], ident[:, :])
                    last.then_inc(t_full, 1)

            pe.wait_ge(consts, Z + 16 * N_CONST)
            turn(0, 0)
            pe.wait_ge(w_ok[0], Z + 16)
            def chunk(i, ch, more, more_2):
                g = i * NCH + ch

                def project(dst, m):
                    for k in range(KD):
                        last = nc.tensor.matmul(dst, w_in[:, k, m * P:(m + 1) * P], xnT[:, ch, k, :],
                                                start=(k == 0), stop=(k == KD - 1))
                    return last

                def slot_a(job):
                    pe.wait_ge(a_read, Z + g * A_JOBS + job + 1)
                    return ps_a[:, (ch * A_JOBS + job) % NA, :]

                pe.wait_ge(t_read, Z + (g + 1) * T_JOBS + NT)
                for job, m in enumerate((M_DT, M_X)):
                    project(slot_a(job), m).then_inc(a_full, 1)
                pe.wait_ge(v_read, Z + g * V_JOBS + 1)
                project(ps_v[:, (ch * V_JOBS) % NV, :], M_B).then_inc(v_full, 1)
                pe.wait_ge(a_read, Z + g * A_JOBS + NA + 1)
                for c in range(NC_T):
                    nc.tensor.matmul(slot_a(J_DT + c), w_dt[:, c * P:(c + 1) * P], dtl_x[:, 0, :],
                                     start=True, stop=True).then_inc(a_full, 1)
                pe.wait_ge(a_read, Z + g * A_JOBS + NA + 2)
                for c in range(NC_T):
                    nc.tensor.matmul(slot_a(J_XR + c), rep[:, c, :], dtl_x[:, 1, :],
                                     start=True, stop=True).then_inc(a_full, 1)
                pe.wait_ge(w_ok[1], Z + 16)
                for c in range(NC_T):
                    pe.wait_ge(v_read, Z + g * V_JOBS + c + 2)
                    project(ps_v[:, (ch * V_JOBS + c + 1) % NV, :], M_C + c).then_inc(v_full, 1)
                pe.wait_ge(w_ok[2], Z + 16)
                for c in range(NC_T):
                    project(slot_a(J_Z + c), M_Z + c).then_inc(a_full, 1)
                    if c == NC_T // 2 and more:
                        turn(g + 1, 1 - ch)

            over_chunks(pe, chunk)

        @block.scalar
        def _(act):
            def deviation(j, slot):
                act.wait_ge(mv_ok, Z + (j + 1) * TT)
                nc.scalar.activation(std[:, slot, :], mv[:, slot, :, 1], ACT.Sqrt, bias=EPS).then_inc(std_ok, 1)

            nc.scalar.nop().then_inc(a_read, NA)
            deviation(0, 0)
            act.wait_ge(consts, Z + 16 * N_CONST)
            nc.scalar.mul(bdt2[:, :], bdt[:, :], 2.0).then_inc(bdt2_ok, 1)
            act.wait_ge(bdt2_ok, Z + 1)
            def chunk(i, ch, more, more_2):
                g = i * NCH + ch

                def bank(job):
                    act.wait_ge(a_full, Z + g * A_JOBS + job + 1)
                    return ps_a[:, (ch * A_JOBS + job) % NA, :]

                for job in range(2):
                    src = bank(job)
                    nc.scalar.copy(dtl_x[:, job, :], src).then_inc(a_read, 1)
                act.wait_ge(delta_ok, Z + g)
                for c in range(NC_T):
                    src = bank(J_DT + c)
                    nc.scalar.activation(dt_x[:, c, :], src, ACT.Identity, bias=bdt2[:, c:c + 1]).then_inc(a_read, 1)
                act.wait_ge(halo_ok, Z + g + 1)
                for c in range(NC_T):
                    src = bank(J_XR + c)
                    nc.scalar.copy(xr[:, c, HALO:HALO + CH], src).then_inc(a_read, 1)
                act.wait_ge(a_read, Z + g * A_JOBS + J_XR + NA)
                act.wait_ge(du_out, Z + g * 16)
                nc.scalar.activation(dt_e[:, :, :], dt_x[:, :, :], ACT.Abs).then_inc(abs_ok, 1)
                for c in range(NC_T):
                    act.wait_ge(v_full, Z + g * V_JOBS + c + 2)
                    act.wait_ge(c_out[c % 2], Z + (g * (NC_T // 2) + c // 2) * 48)
                    nc.scalar.copy(c_hi[:, c % 2, :], ps_v[:, (ch * V_JOBS + c + 1) % NV, :]).then_inc(hi_ok, 1)
                    if c == 1:
                        act.wait_ge(abs_ok, Z + g + 1)
                        nc.scalar.activation(dt_e[:, :, :], dt_e[:, :, :], ACT.Exp, scale=-1.0).then_inc(exp_ok, 1)
                    if c == 4:
                        act.wait_ge(exp_ok, Z + g + 1)
                        act.wait_ge(delta_out, Z + g * 16)
                        act.wait_ge(du_ok, Z + g)
                        nc.scalar.activation(dt_l[:, :, :], dt_e[:, :, :], ACT.Ln, bias=1.0).then_inc(ln_ok, 1)
                for c in range(NC_T):
                    act.wait_ge(conv_step, Z + (g * NC_T + c + 1) * D_CONV)
                    nc.scalar.activation(conv[:, c, :], conv[:, c, :], ACT.Silu, bias=cb[:, c:c + 1]).then_inc(u_ok, 1)
                for c in range(NC_T):
                    if c == NC_T // 4 and more:
                        deviation(g + 1, 1 - ch)
                    src = bank(J_Z + c)
                    act.wait_ge(z_out[c % 2], Z + (g * (NC_T // 2) + c // 2) * 16)
                    nc.scalar.activation(z[:, c % 2, :], src, ACT.Silu).then_inc(a_read, 1)

            over_chunks(act, chunk)

        @block.vector
        def _(dve):
            def statistics(j, slot, loads):
                dve.wait_ge(x_in[slot], Z + loads * 16)
                for t in range(TT):
                    nc.vector.bn_stats(stats[:, slot, t, :], x[:, slot, t, :]).then_inc(stats_ok, 1)
                s.hold(dve, stats_ok, Z + (j + 1) * TT)
                for t in range(TT):
                    nc.vector.bn_aggr(mv[:, slot, t, :], stats[:, slot, t, :]).then_inc(mv_ok, 1)

            def normalise(j, slot):
                dve.wait_ge(std_ok, Z + j + 1)
                nc.vector.reciprocal(rstd[:, slot, :], std[:, slot, :]).then_inc(rstd_ok, 1)
                dve.wait_ge(rstd_ok, Z + j + 1)
                for t in range(TT):
                    xt = x[:, slot, t, :]
                    nc.vector.tensor_scalar(xt, xt, mv[:, slot, t, 0:1], rstd[:, slot, t:t + 1], ALU.subtract, ALU.mult).then_inc(xn_ok, 1)

            def read_turned(j, slot):
                for k in range(KD):
                    dve.wait_ge(t_full, Z + j * T_JOBS + k + 1)
                    nc.vector.tensor_copy(xnT[:, slot, k, :], ps_t[:, k % NT, :]).then_inc(t_read, 1)

            nc.vector.nop().then_inc(t_read, NT)
            nc.vector.nop().then_inc(v_read, NV)
            statistics(0, 0, 1)
            normalise(0, 0)
            read_turned(0, 0)
            def chunk(i, ch, more, more_2):
                g = i * NCH + ch
                dve.wait_ge(conv_step, Z + g * NC_T * D_CONV)
                if ch == 0:
                    nc.vector.memset(xr[:, :, 0:HALO], 0.0).then_inc(halo_ok, 1)
                else:
                    nc.vector.tensor_copy(xr[:, :, 0:HALO], xr[:, :, CH:CH + HALO]).then_inc(halo_ok, 1)
                dve.wait_ge(v_full, Z + g * V_JOBS + 1)
                dve.wait_ge(b_out, Z + g * 16)
                nc.vector.tensor_copy(bT[:, :], ps_v[:, (ch * V_JOBS) % NV, :]).then_inc(v_read, 1)
                dve.wait_ge(u_out, Z + g * 16)
                for c in range(NC_T):
                    dve.wait_ge(a_read, Z + g * A_JOBS + J_XR + c + NA + 1)
                    for j in range(D_CONV):
                        step = (g * NC_T + c) * D_CONV + j
                        if j == 0:
                            nc.vector.tensor_scalar(conv[:, c, :], xr[:, c, 0:CH], cw[:, c, 0:1], None,
                                                    ALU.mult).then_inc(conv_step, 1)
                        else:
                            dve.wait_ge(conv_step, Z + step)
                            nc.vector.scalar_tensor_tensor(out=conv[:, c, :], in0=xr[:, c, j:j + CH], scalar=cw[:, c, j:j + 1],
                                                           in1=conv[:, c, :], op0=ALU.mult, op1=ALU.add).then_inc(conv_step, 1)
                    dve.wait_ge(hi_ok, Z + g * NC_T + c + 1)
                    if c >= 2:
                        dve.wait_ge(lo_ok, Z + g * NC_T + c - 1)
                    nc.vector.tensor_tensor(c_res[:, c % 2, :], ps_v[:, (ch * V_JOBS + c + 1) % NV, :], c_hi[:, c % 2, :],
                                            ALU.subtract).then_inc(v_read, 1)
                if more:
                    statistics(g + 1, 1 - ch, i + ch + 1)
                dve.wait_ge(ln_ok, Z + g + 1)
                nc.vector.tensor_scalar(dt_d[:, :, :], dt_e[:, :, :], 1.0, -1.0, ALU.add, ALU.add).then_inc(sp_step, 1)
                if more:
                    normalise(g + 1, 1 - ch)
                dve.wait_ge(sp_step, Z + g * SP_STEPS + 1)
                nc.vector.tensor_tensor(dt_d[:, :, :], dt_e[:, :, :], dt_d[:, :, :], ALU.subtract).then_inc(sp_step, 1)
                if more:
                    read_turned(g + 1, 1 - ch)
                dve.wait_ge(sp_step, Z + g * SP_STEPS + 2)
                nc.vector.tensor_tensor(dt_l[:, :, :], dt_l[:, :, :], dt_d[:, :, :], ALU.add).then_inc(sp_step, 1)
                dve.wait_ge(sp_step, Z + g * SP_STEPS + 3)
                nc.vector.tensor_tensor(dt_l[:, :, :], dt_l[:, :, :], dt_e[:, :, :], ALU.min).then_inc(sp_step, 1)
                dve.wait_ge(sp_step, Z + g * SP_STEPS + 4)
                nc.vector.scalar_tensor_tensor(out=dt_l[:, :, :], in0=dt_x[:, :, :], scalar=0.0, in1=dt_l[:, :, :],
                                               op0=ALU.max, op1=ALU.add).then_inc(delta_ok, 1)
                dve.wait_ge(delta_ok, Z + g + 1)
                dve.wait_ge(u_ok, Z + (g + 1) * NC_T)
                nc.vector.tensor_tensor(dt_e[:, :, :], dt_l[:, :, :], conv[:, :, :], ALU.mult).then_inc(du_ok, 1)

            over_chunks(dve, chunk)


def selective_scan(nc, a, w_out):
    NB, R, NH_ = 8, 4, 4
    AHEAD = 4
    N = D_STATE
    with Scope(nc, "scan") as s:
        ident = s.sb("ident", [P, P])
        sel32 = s.sb("sel32", [C_ROWS, 4, P])
        sel = s.sb("sel", [C_ROWS, 4, P], BF16)
        a_exp = s.sb("a_exp", [P, NC_T * N])
        d_all = s.sb("d_all", [P, NC_T])
        a_cur = s.sb("a_cur", [P, B, N])
        d_cur = s.sb("d_cur", [P, B])
        delta = s.sb("delta", [P, B, L])
        du = s.sb("du", [P, B, L])
        u = s.sb("u", [P, B, L])
        sz = s.sb("sz", [P, B, L])
        cs = s.sb("cs", [C_ROWS, B, N_QUAD, L], BF16)
        b_bc = s.sb("b_bc", [P, NB, L])
        decay = s.sb("decay", [P, R, L])
        inp = s.sb("inp", [P, R, L])
        h = s.sb("h", [P, NH_, L])
        hc = s.sb("hc", [P, R, L])
        y = s.sb("y", [P, B, L])
        ps_c = s.ps("ps_c", [P, 2, L])
        ps_y = s.ps("ps_y", [P, B, L])

        consts, sel_ok, aexp_ok, cur_ok = (s.sem(n) for n in ("consts", "sel_ok", "aexp_ok", "cur_ok"))
        g_in = s.sems("g_in", B)
        b_in = s.sems("b_in", NB)
        w_in = s.sem("w_in")
        exp_ok, inp_ok, scan_ok, hc_ok, c_full, sum_ok, skip_ok, fin_ok = (s.sem(n) for n in (
            "exp_ok", "inp_ok", "scan_ok", "hc_ok", "c_full", "sum_ok", "skip_ok", "fin_ok"))
        y_out = s.sems("y_out", B)
        block = s.block()
        G_LOADS = 4 + 3
        LOAD_AT = (4, 5, 7, 8, 10, 11, 13)
        UNITS = B * N
        FIN = 1

        def over_groups(eng, group):
            group(0, 0, None, (0, 1))
            with eng.Fori(0, NC_T - 1) as c:
                group(c, 1, (c, 0), (c + 1, 0))
                group(c + 1, 0, (c, 1), (c + 1, 1))
            group(NC_T - 1, 1, (NC_T - 1, 0), None)

        @block.sync
        def _(sp):
            def load_group(c, b, i):
                part = slice(b * L, (b + 1) * L)
                if i < 4:
                    dst, name = ((delta, "s_delta"), (du, "s_du"), (u, "s_u"), (sz, "s_z"))[i]
                    dst, src = dst[:, b, :], a[name][bass.ds(c, 1), :, part].rearrange("c p t -> (c p) t")
                else:
                    n = i - 4
                    dst = cs[32 * n:32 * n + 32, b, :, :]
                    src = a["s_c"][n, bass.ds(c, 1), :, part].rearrange("c (q r) t -> (c r) q t", q=N_QUAD)
                sp.dma_start(dst, src).then_inc(g_in[b], 16)

            def load_b(c, b, n):
                k = (b * N + n) % NB
                row = a["s_b"][bass.ds(c * N + n, 1), b * L:(b + 1) * L]
                sp.dma_start(b_bc[:, k, :], row.to_broadcast([P, L])).then_inc(b_in[k], 16)

            def finished(c, b):
                s.hold(sp, fin_ok, Z + c * B + b + FIN + 1)
                sp.dma_start(a["s_y"][bass.ds(c, 1), :, b * L:(b + 1) * L].rearrange("c p t -> (c p) t"), y[:, b, :]).then_inc(y_out[b], 16)

            def group(c, b, before, after):
                for n in range(N):
                    if n + AHEAD < N or after:
                        s.hold(sp, inp_ok, Z + (c * B + b) * N + n + AHEAD + 1)
                        load_b(*((c, b) if n + AHEAD < N else after), (n + AHEAD) % N)
                    if n == LOAD_AT[0] and before:
                        finished(*before)
                    if n in LOAD_AT and after:
                        load_group(*after, LOAD_AT.index(n))

            for i in range(G_LOADS):
                load_group(0, 0, i)
            for dst, name in ((a_exp[:, :], "a_log"), (ident[:, :], "c_ident"), (sel32[:, :, :], "c_sel"), (d_all[:, :], "d_param")):
                src = a[name].rearrange("p c n -> p (c n)") if name == "a_log" else a[name]
                sp.dma_start(dst, src).then_inc(consts, 16)
            for n in range(AHEAD):
                load_b(0, 0, n)
            over_groups(sp, group)
            sp.dma_start(w_out[:, :, :], a["w_out"].rearrange("(k p) n -> p k n", p=P)).then_inc(w_in, 16)
            finished(NC_T - 1, 1)
            for b in range(B):
                sp.wait_ge(y_out[b], Z + NC_T * 16)
            sp.wait_ge(w_in, Z + 16)

        @block.scalar
        def _(act):
            act.wait_ge(consts, Z + 4 * 16)
            nc.scalar.activation(a_exp[:, :], a_exp[:, :], ACT.Exp).then_inc(aexp_ok, 1)
            nc.scalar.copy(sel[:, :, :], sel32[:, :, :]).then_inc(sel_ok, 1)
            act.wait_ge(aexp_ok, Z + 1)

            def group(c, b, before, after):
                g = c * B + b
                act.wait_ge(fin_ok, Z + g - 1 + FIN)
                nc.scalar.mul(a_cur[:, b, :], a_exp[:, bass.ds(c * N, N)], -1.0).then_inc(cur_ok, 1)
                nc.scalar.copy(d_cur[:, b:b + 1], d_all[:, bass.ds(c, 1)]).then_inc(cur_ok, 1)
                act.wait_ge(cur_ok, Z + (g + 1) * 2)
                act.wait_ge(g_in[b], Z + (c + 1) * G_LOADS * 16)
                for n in range(N):
                    act.wait_ge(scan_ok, Z + g * N + n + 1)
                    nc.scalar.activation(decay[:, n % R, :], delta[:, b, :], ACT.Exp, scale=a_cur[:, b, n:n + 1]).then_inc(exp_ok, 1)

            over_groups(act, group)

        @block.gpsimd
        def _(pool):
            nc.gpsimd.nop().then_inc(inp_ok, NB)

            def group(c, b, before, after):
                s.hold(pool, g_in[b], Z + (c + 1) * G_LOADS * 16)
                for n in range(N):
                    k = (b * N + n) % NB
                    s.hold(pool, b_in[k], Z + (c * (UNITS // NB) + (b * N + n) // NB + 1) * 16)
                    s.hold(pool, scan_ok, Z + (c * B + b) * N + n + 1)
                    nc.gpsimd.tensor_tensor(inp[:, n % R, :], du[:, b, :], b_bc[:, k, :], ALU.mult).then_inc(inp_ok, 1)

            over_groups(pool, group)

        @block.vector
        def _(dve):
            nc.vector.nop().then_inc(scan_ok, R)
            nc.vector.nop().then_inc(hc_ok, NH_)
            nc.vector.nop().then_inc(fin_ok, FIN)

            def scan(U, n):
                dve.wait_ge(exp_ok, Z + U + 1)
                dve.wait_ge(inp_ok, Z + U + NB + 1)
                dve.wait_ge(hc_ok, Z + U + 1)
                nc.vector.tensor_tensor_scan(h[:, n % NH_, :], decay[:, n % R, :], inp[:, n % R, :], 0.0,
                                             ALU.mult, ALU.add).then_inc(scan_ok, 1)

            def finish(c, b):
                g = c * B + b
                dve.wait_ge(sum_ok, Z + (g + 1) * N + R)
                dve.wait_ge(y_out[b], Z + c * 16)
                dve.wait_ge(cur_ok, Z + (g + 1) * 2)
                nc.vector.scalar_tensor_tensor(out=y[:, b, :], in0=u[:, b, :], scalar=d_cur[:, b:b + 1], in1=ps_y[:, b, :],
                                               op0=ALU.mult, op1=ALU.add).then_inc(skip_ok, 1)
                dve.wait_ge(skip_ok, Z + g + 1)
                nc.vector.tensor_tensor(y[:, b, :], y[:, b, :], sz[:, b, :], ALU.mult).then_inc(fin_ok, 1)

            def group(c, b, before, after):
                scan((c * B + b) * N, 0)
                for n in range(N):
                    U = (c * B + b) * N + n
                    if n + 1 < N:
                        scan(U + 1, n + 1)
                    dve.wait_ge(c_full, Z + U + 1)
                    dve.wait_ge(scan_ok, Z + U + R + 1)
                    dve.wait_ge(sum_ok, Z + U + 1)
                    nc.vector.tensor_tensor(hc[:, n % R, :], h[:, n % NH_, :], ps_c[:, n % 2, :], ALU.mult).then_inc(hc_ok, 1)
                    if n == 1 and before:
                        finish(*before)

            over_groups(dve, group)
            finish(NC_T - 1, 1)

        @block.tensor
        def _(pe):
            nc.tensor.nop().then_inc(sum_ok, R)
            pe.wait_ge(consts, Z + 4 * 16)
            pe.wait_ge(sel_ok, Z + 1)

            def spread(c, b, n):
                if n == 0:
                    pe.wait_ge(g_in[b], Z + (c + 1) * G_LOADS * 16)
                pe.wait_ge(hc_ok, Z + (c * B + b) * N + n + NH_ - 1)
                for half in range(L // 512):
                    last = nc.tensor.matmul(ps_c[:, n % 2, half * 512:half * 512 + 512], sel[:, n % 4, :],
                                            cs[:, b, n // 4, half * 512:half * 512 + 512], start=True, stop=True)
                last.then_inc(c_full, 1)

            def group(c, b, before, after):
                g = c * B + b
                if not before:
                    spread(c, b, 0)
                pe.wait_ge(fin_ok, Z + g - 1 + FIN)
                for n in range(N):
                    if n + 1 < N:
                        spread(c, b, n + 1)
                    elif after:
                        spread(*after, 0)
                    pe.wait_ge(hc_ok, Z + g * N + n + NH_ + 1)
                    for half in range(L // 512):
                        last = nc.tensor.matmul(ps_y[:, b, half * 512:half * 512 + 512], ident[:, :],
                                                hc[:, n % R, half * 512:half * 512 + 512], start=(n == 0), stop=(n == N - 1))
                    last.then_inc(sum_ok, 1)

            over_groups(pe, group)


def mix_out(nc, a, w):
    NP = 4
    KI = NC_T
    with Scope(nc, "mix") as s:
        w_hi = s.sb("w_hi", [P, KI, D])
        w_lo = s.sb("w_lo", [P, KI, D])
        y = s.sb("y", [P, NCH, KI, CH])
        y_hi = s.sb("y_hi", [P, NCH, KI, CH])
        y_lo = s.sb("y_lo", [P, NCH, KI, CH])
        x = s.sb("x", [P, NCH, TT, D])
        xn = s.sb("xn", [P, NCH, TT, D])
        w_r = s.sb("w_r", [P, D])
        b_r = s.sb("b_r", [P, 1])
        stats = s.sb("stats", [P, NCH, TT, 6])
        mv = s.sb("mv", [P, NCH, TT, 2])
        std = s.sb("std", [P, NCH, TT])
        rstd = s.sb("rstd", [P, NCH, TT])
        prod = s.sb("prod", [P, TT, D])
        score = s.sb("score", [P, NCH, TT])
        ps = s.ps("ps", [P, NP, D])
        consts, full, read, stats_ok, mv_ok, std_ok, rstd_ok, xn_ok, dot_ok, score_ok = (s.sem(n) for n in (
            "consts", "full", "read", "stats_ok", "mv_ok", "std_ok", "rstd_ok", "xn_ok", "dot_ok", "score_ok"))
        w_hi_ok, w_ok, y_hi_ok, y_ok = (s.sem(n) for n in ("w_hi_ok", "w_ok", "y_hi_ok", "y_ok"))
        y_in, x_in, x_out, xn_out, score_out = (s.sems(n, NCH) for n in ("y_in", "x_in", "x_out", "xn_out", "score_out"))
        block = s.block()

        @block.sync
        def _(sp):
            def load_y(ch, tok):
                sp.dma_start(y[:, ch, :, :], cols(a["s_y"], tok, CH)).then_inc(y_in[ch], 16)

            def load_x(ch, tok):
                sp.dma_start(x[:, ch, :, :], rows(a["x"], tok, CH)).then_inc(x_in[ch], 16)

            for ch in range(NCH):
                load_y(ch, ch * CH)
                load_x(ch, ch * CH)
            sp.dma_start(w_r[:, :], a["w_r"].to_broadcast([P, D])).then_inc(consts, 16)
            sp.dma_start(b_r[:, :], a["b_r"].to_broadcast([P, 1])).then_inc(consts, 16)
            def chunk(i, ch, more, more_2):
                g = i * NCH + ch
                tok = i * L + ch * CH
                if more_2:
                    s.hold(sp, y_ok, Z + (g + 1) * KI)
                    load_y(ch, tok + L)
                s.hold(sp, read, Z + (g + 1) * TT + NP)
                sp.dma_start(rows(a["s_x1"], tok, CH), x[:, ch, :, :]).then_inc(x_out[ch], 16)
                s.hold(sp, xn_ok, Z + (g + 1) * TT)
                sp.dma_start(rows(a["s_n1"], tok, CH), xn[:, ch, :, :]).then_inc(xn_out[ch], 16)
                s.hold(sp, score_ok, Z + g + 1)
                sp.dma_start(a["s_score"][:, bass.ds(g * TT, TT)], score[:, ch, :]).then_inc(score_out[ch], 16)
                if more_2:
                    s.hold(sp, x_out[ch], Z + (i + 1) * 16)
                    load_x(ch, tok + L)

            over_chunks(sp, chunk)
            for ch in range(NCH):
                for done in (x_out, xn_out, score_out):
                    sp.wait_ge(done[ch], Z + B * 16)

        @block.tensor
        def _(pe):
            pe.wait_ge(w_ok, Z + KI)
            def chunk(i, ch, more, more_2):
                g = i * NCH + ch
                pe.wait_ge(y_ok, Z + (g + 1) * KI)
                for t in range(TT):
                    pe.wait_ge(read, Z + g * TT + t + 1)
                    c = slice(t * P, (t + 1) * P)
                    exact_product(nc, ps[:, t, :], [(y_hi[:, ch, k, c], y_lo[:, ch, k, c]) for k in range(KI)],
                                  [(w_hi[:, k, :], w_lo[:, k, :]) for k in range(KI)]).then_inc(full, 1)

            over_chunks(pe, chunk)

        @block.scalar
        def _(act):
            def first_part(slot, loads):
                act.wait_ge(y_in[slot], Z + loads * 16)
                for k in range(KI):
                    nc.scalar.copy(y_hi[:, slot, k, :].bitcast(F32R), y[:, slot, k, :]).then_inc(y_hi_ok, 1)

            for k in range(KI):
                nc.scalar.copy(w_hi[:, k, :].bitcast(F32R), w[:, k, :]).then_inc(w_hi_ok, 1)
            first_part(0, 1)
            def chunk(i, ch, more, more_2):
                if more:
                    act.wait_ge(full, Z + (i * NCH + ch) * TT)
                    first_part(1 - ch, i + ch + 1)
                act.wait_ge(mv_ok, Z + (i * NCH + ch + 1) * TT)
                nc.scalar.activation(std[:, ch, :], mv[:, ch, :, 1], ACT.Sqrt, bias=EPS).then_inc(std_ok, 1)

            over_chunks(act, chunk)

        @block.vector
        def _(dve):
            def second_part(j, slot):
                for k in range(KI):
                    dve.wait_ge(y_hi_ok, Z + j * KI + k + 1)
                    nc.vector.tensor_tensor(y_lo[:, slot, k, :].bitcast(F32R), y[:, slot, k, :], y_hi[:, slot, k, :],
                                            ALU.subtract).then_inc(y_ok, 1)

            nc.vector.nop().then_inc(read, NP)
            for k in range(KI):
                dve.wait_ge(w_hi_ok, Z + k + 1)
                nc.vector.tensor_tensor(w_lo[:, k, :].bitcast(F32R), w[:, k, :], w_hi[:, k, :], ALU.subtract).then_inc(w_ok, 1)
            second_part(0, 0)
            dve.wait_ge(consts, Z + 32)
            def chunk(i, ch, more, more_2):
                g = i * NCH + ch
                if more:
                    second_part(g + 1, 1 - ch)
                dve.wait_ge(x_in[ch], Z + (i + 1) * 16)
                for t in range(TT):
                    dve.wait_ge(full, Z + g * TT + t + 1)
                    nc.vector.tensor_tensor(x[:, ch, t, :], x[:, ch, t, :], ps[:, t, :], ALU.add).then_inc(read, 1)
                    dve.wait_ge(read, Z + g * TT + t + NP + 1)
                    nc.vector.bn_stats(stats[:, ch, t, :], x[:, ch, t, :]).then_inc(stats_ok, 1)
                s.hold(dve, stats_ok, Z + (g + 1) * TT)
                for t in range(TT):
                    nc.vector.bn_aggr(mv[:, ch, t, :], stats[:, ch, t, :]).then_inc(mv_ok, 1)
                dve.wait_ge(std_ok, Z + g + 1)
                nc.vector.reciprocal(rstd[:, ch, :], std[:, ch, :]).then_inc(rstd_ok, 1)
                dve.wait_ge(rstd_ok, Z + g + 1)
                dve.wait_ge(xn_out[ch], Z + i * 16)
                for t in range(TT):
                    nc.vector.tensor_scalar(xn[:, ch, t, :], x[:, ch, t, :], mv[:, ch, t, 0:1], rstd[:, ch, t:t + 1],
                                            ALU.subtract, ALU.mult).then_inc(xn_ok, 1)
                dve.wait_ge(score_out[ch], Z + i * 16)
                dve.wait_ge(dot_ok, Z + g * TT)
                for t in range(TT):
                    dve.wait_ge(xn_ok, Z + g * TT + t + 1)
                    nc.vector.tensor_tensor_reduce(prod[:, t, :], xn[:, ch, t, :], w_r[:, :], 1.0, 0.0,
                                                   ALU.mult, ALU.add, score[:, ch, t:t + 1]).then_inc(dot_ok, 1)
                dve.wait_ge(dot_ok, Z + (g + 1) * TT)
                nc.vector.tensor_scalar(score[:, ch, :], score[:, ch, :], b_r[:, 0:1], None, ALU.add).then_inc(score_ok, 1)

            over_chunks(dve, chunk)


def rank_tokens(nc, a, w1_hi, w1_lo):
    with Scope(nc, "rank") as s:
        col = s.sb("col", [P, TOK_TILES])
        colT = s.sb("colT", [TOK_TILES, P])
        ident = s.sb("ident", [P, P])
        row = s.sb("row", [P, T])
        earlier = s.sb("earlier", [P, P])
        scratch = s.sb("scratch", [P, TOK_TILES, L], BF16)
        scratch_own = s.sb("scratch_own", [P, TOK_TILES, P], BF16)
        cnt = s.sb("cnt", [P, 3, TOK_TILES])
        half = s.sb("half", [P, TOK_TILES])
        dest = s.sb("dest", [P, TOK_TILES])
        dest_i = s.sb("dest_i", [P, TOK_TILES], I32)
        xn = s.sb("xn", [P, TOK_TILES, D])
        zeros = s.sb("zeros", [P, TOK_TILES // 2, D])
        w1 = s.sb("w1", [P, 2, DF])
        ps = s.ps("ps", [TOK_TILES, P])
        col_in, row_in, xn_in, zero_ok, zero_out, colT_ok, colT_sb, colT_out, cnt_zero, cnt_ok, step, dest_ok, dest_out = (s.sem(n) for n in (
            "col_in", "row_in", "xn_in", "zero_ok", "zero_out", "colT_ok", "colT_sb", "colT_out", "cnt_zero", "cnt_ok", "step", "dest_ok", "dest_out"))
        w1_in = s.sems("w1_in", 2)
        w_hi_ok, w_ok = s.sem("w_hi_ok"), s.sem("w_ok")
        sent = s.pool_dma_sem("sent")
        block = s.block()
        N_CNT = 3 * NQT - 1
        N_STEP = 5

        @block.sync
        def _(sp):
            sp.dma_start(col[:, :], a["s_score"]).then_inc(col_in, 16)
            sp.dma_start(ident[:, :], a["c_ident"]).then_inc(col_in, 16)
            sp.dma_start(earlier[:, :], a["c_earlier"]).then_inc(row_in, 16)
            sp.wait_ge(colT_sb, Z + 1)
            sp.dma_start(a["s_score_row"].rearrange("o (t p) -> (o t) p", p=P), colT[:, :]).then_inc(colT_out, 16)
            sp.wait_ge(colT_out, Z + 16)
            sp.dma_start(row[:, :], a["s_score_row"].to_broadcast([P, T])).then_inc(row_in, 16)
            for k in range(2):
                sp.dma_start(w1[:, k, :], a["w1"][k * P:(k + 1) * P, :]).then_inc(w1_in[k], 16)
            sp.dma_start(xn[:, :, :], rows(a["s_n1"], 0, T)).then_inc(xn_in, 16)
            for k in range(2, KD):
                sp.wait_ge(w_ok, Z + k - 1)
                sp.dma_start(w1[:, k % 2, :], a["w1"][k * P:(k + 1) * P, :]).then_inc(w1_in[k % 2], 16)
            sp.wait_ge(zero_ok, Z + 1)
            sp.dma_start(rows(a["s_sel_out"], B * K_SEL, B * K_SEL), zeros[:, :, :]).then_inc(zero_out, 16)
            sp.wait_ge(dest_ok, Z + B)
            sp.dma_start(a["s_dest"], dest_i[:, :]).then_inc(dest_out, 16)
            sp.wait_ge(dest_out, Z + 16)
            sp.wait_ge(zero_out, Z + 16)

        @block.tensor
        def _(pe):
            pe.wait_ge(col_in, Z + 32)
            nc.tensor.transpose(ps[:, :], col[:, :], ident[:, :]).then_inc(colT_ok, 1)

        @block.scalar
        def _(act):
            act.wait_ge(colT_ok, Z + 1)
            nc.scalar.copy(colT[:, :], ps[:, :]).then_inc(colT_sb, 1)
            for k in range(KD):
                act.wait_ge(w1_in[k % 2], Z + (k // 2 + 1) * 16)
                nc.scalar.copy(w1_hi[:, k, :].bitcast(F32R), w1[:, k % 2, :]).then_inc(w_hi_ok, 1)

        @block.vector
        def _(dve):
            nc.vector.memset(cnt[:, :, :], 0.0).then_inc(cnt_zero, 1)
            dve.wait_ge(row_in, Z + 32)
            dve.wait_ge(col_in, Z + 32)
            dve.wait_ge(cnt_zero, Z + 1)
            for b in range(B):
                seq = row[:, b * L:(b + 1) * L]
                for t in range(NQT):
                    j = b * NQT + t
                    me = col[:, j:j + 1]
                    nc.vector.tensor_scalar(scratch[:, j, t * P:L], seq[:, t * P:L], me, 0.0, ALU.is_gt, ALU.add,
                                            accum_out=cnt[:, 0, j:j + 1]).then_inc(cnt_ok, 1)
                    nc.vector.scalar_tensor_tensor(out=scratch_own[:, j, :], in0=seq[:, t * P:(t + 1) * P], scalar=me, in1=earlier[:, :],
                                                   op0=ALU.is_equal, op1=ALU.mult, accum_out=cnt[:, 1, j:j + 1]).then_inc(cnt_ok, 1)
                    if t:
                        nc.vector.tensor_scalar(scratch[:, j, 0:t * P], seq[:, 0:t * P], me, 0.0, ALU.is_ge, ALU.add,
                                                accum_out=cnt[:, 2, j:j + 1]).then_inc(cnt_ok, 1)
                of = slice(b * NQT, (b + 1) * NQT)
                dve.wait_ge(cnt_ok, Z + (b + 1) * N_CNT)
                nc.vector.tensor_tensor(cnt[:, 0, of], cnt[:, 0, of], cnt[:, 1, of], ALU.add).then_inc(step, 1)
                dve.wait_ge(step, Z + b * N_STEP + 1)
                nc.vector.tensor_tensor(cnt[:, 0, of], cnt[:, 0, of], cnt[:, 2, of], ALU.add).then_inc(step, 1)
                dve.wait_ge(step, Z + b * N_STEP + 2)
                nc.vector.tensor_scalar(half[:, of], cnt[:, 0, of], float(K_SEL), float(K_SEL), ALU.is_ge, ALU.mult).then_inc(step, 1)
                dve.wait_ge(step, Z + b * N_STEP + 3)
                nc.vector.tensor_tensor(dest[:, of], cnt[:, 0, of], half[:, of], ALU.add).then_inc(step, 1)
                dve.wait_ge(step, Z + b * N_STEP + 4)
                nc.vector.tensor_scalar(dest[:, of], dest[:, of], float(b * K_SEL), None, ALU.add).then_inc(step, 1)
                dve.wait_ge(step, Z + b * N_STEP + 5)
                nc.vector.tensor_copy(dest_i[:, of], dest[:, of]).then_inc(dest_ok, 1)
            for k in range(2, KD):
                dve.wait_ge(w_hi_ok, Z + k + 1)
                nc.vector.tensor_tensor(w1_lo[:, k, :].bitcast(F32R), w1[:, k % 2, :], w1_hi[:, k, :], ALU.subtract)

        @block.gpsimd
        def _(pool):
            nc.gpsimd.memset(zeros[:, :, :], 0.0).then_inc(zero_ok, 1)
            for k in range(2):
                s.hold(pool, w_hi_ok, Z + k + 1)
                nc.gpsimd.tensor_tensor(w1_lo[:, k, :].bitcast(F32R), w1[:, k, :], w1_hi[:, k, :], ALU.subtract).then_inc(w_ok, 1)
            pool.wait_ge(xn_in, Z + 16)
            for j in range(TOK_TILES):
                if j % NQT == 0:
                    pool.wait_ge(dest_ok, Z + j // NQT + 1)
                nc.gpsimd.indirect_dma_start(a["s_sel_in"], bass.IndirectOffsetOnAxis(ap=dest_i[:, j:j + 1].bitcast(U32), axis=0),
                                             xn[:, j, :], None).then_inc(sent, 16)
            pool.wait_ge(sent, 16 * TOK_TILES)


def select_ffn(nc, a, w1_hi, w1_lo):
    NT, NA, NV = 2, 4, 2
    with Scope(nc, "ffn") as s:
        w2 = s.sb("w2", [P, KF, D])
        b1 = s.sb("b1", [P, KF])
        b2 = s.sb("b2", [P, D])
        ident = s.sb("ident", [P, P])
        xs = s.sb("xs", [P, TT, D])
        xT_hi = s.sb("xT_hi", [P, KD, CH])
        xT_lo = s.sb("xT_lo", [P, KD, CH])
        hT = s.sb("hT", [P, KF, CH])
        y = s.sb("y", [P, TT, D])
        ps_t = s.ps("ps_t", [P, NT, CH])
        ps_h = s.ps("ps_h", [P, NA, CH])
        ps_y = s.ps("ps_y", [P, NV, D])
        t_hi_ok, w2_in = s.sem("t_hi_ok"), s.sem("w2_in")
        consts, x_in, t_full, t_read, h_full, h_read, y_full, y_read, y_out = (s.sem(n) for n in (
            "consts", "x_in", "t_full", "t_read", "h_full", "h_read", "y_full", "y_read", "y_out"))
        block = s.block()

        @block.sync
        def _(sp):
            sp.dma_start(ident[:, :], a["c_ident"]).then_inc(consts, 16)
            sp.dma_start(b1[:, :], a["b1"]).then_inc(consts, 16)
            sp.dma_start(b2[:, :], a["b2"].to_broadcast([P, D])).then_inc(consts, 16)
            sp.dma_start(xs[:, :, :], rows(a["s_sel_in"], 0, CH)).then_inc(x_in, 16)
            sp.dma_start(w2[:, :, :], a["w2"].rearrange("(k p) n -> p k n", p=P)).then_inc(w2_in, 16)
            with sp.Fori(0, B) as b:
                s.hold(sp, t_full, Z + (b + 1) * KD)
                sp.dma_start(xs[:, :, :], rows(a["s_sel_in"], (B - 1) * CH, CH)).then_inc(x_in, 16)
                for t in range(TT):
                    s.hold(sp, y_read, Z + b * TT + t + NV + 1)
                    sp.dma_start(a["s_sel_out"][bass.ds(b * CH + t * P, P), :], y[:, t, :]).then_inc(y_out, 16)
            sp.wait_ge(y_out, Z + B * TT * 16)
            sp.wait_ge(x_in, Z + (B + 1) * 16)

        @block.tensor
        def _(pe):
            pe.wait_ge(consts, Z + 48)
            with pe.Fori(0, B) as b:
                pe.wait_ge(x_in, Z + (b + 1) * 16)
                for k in range(KD):
                    pe.wait_ge(t_read, Z + b * KD + k + 1)
                    for t in range(TT):
                        last = nc.tensor.transpose(ps_t[:, k % NT, t * P:(t + 1) * P], xs[:, t, k * P:(k + 1) * P], ident[:, :])
                    last.then_inc(t_full, 1)
                pe.wait_ge(t_read, Z + (b + 1) * KD + NT)
                for f in range(KF):
                    pe.wait_ge(h_read, Z + b * KF + f + 1)
                    c = slice(f * P, (f + 1) * P)
                    exact_product(nc, ps_h[:, f % NA, :], [(w1_hi[:, k, c], w1_lo[:, k, c]) for k in range(KD)],
                                  [(xT_hi[:, k, :], xT_lo[:, k, :]) for k in range(KD)]).then_inc(h_full, 1)
                pe.wait_ge(h_read, Z + (b + 1) * KF + NA)
                pe.wait_ge(w2_in, Z + 16)
                for t in range(TT):
                    pe.wait_ge(y_read, Z + b * TT + t + 1)
                    for f in range(KF):
                        last = nc.tensor.matmul(ps_y[:, t % NV, :], hT[:, f, t * P:(t + 1) * P], w2[:, f, :],
                                                start=(f == 0), stop=(f == KF - 1))
                    last.then_inc(y_full, 1)

        @block.scalar
        def _(act):
            nc.scalar.nop().then_inc(h_read, NA)
            act.wait_ge(consts, Z + 48)
            with act.Fori(0, B) as b:
                act.wait_ge(h_full, Z + b * KF)
                for k in range(KD):
                    act.wait_ge(t_full, Z + b * KD + k + 1)
                    nc.scalar.copy(xT_hi[:, k, :].bitcast(F32R), ps_t[:, k % NT, :]).then_inc(t_hi_ok, 1)
                act.wait_ge(y_full, Z + b * TT)
                for f in range(KF):
                    act.wait_ge(h_full, Z + b * KF + f + 1)
                    nc.scalar.activation(hT[:, f, :], ps_h[:, f % NA, :], ACT.Gelu_apprx_tanh, bias=b1[:, f:f + 1]).then_inc(h_read, 1)

        @block.vector
        def _(dve):
            nc.vector.nop().then_inc(t_read, NT)
            nc.vector.nop().then_inc(y_read, NV)
            dve.wait_ge(consts, Z + 48)
            with dve.Fori(0, B) as b:
                for k in range(KD):
                    dve.wait_ge(t_hi_ok, Z + b * KD + k + 1)
                    nc.vector.tensor_tensor(xT_lo[:, k, :].bitcast(F32R), ps_t[:, k % NT, :], xT_hi[:, k, :], ALU.subtract).then_inc(t_read, 1)
                dve.wait_ge(y_out, Z + b * TT * 16)
                for t in range(TT):
                    dve.wait_ge(y_full, Z + b * TT + t + 1)
                    nc.vector.tensor_tensor(y[:, t, :], ps_y[:, t % NV, :], b2[:, :], ALU.add).then_inc(y_read, 1)


def attend_in(nc, a):
    NT, NA, NV = 2, 4, 2
    QK_JOBS = 2 * NHG
    TURN_AT = 5
    with Scope(nc, "qkv") as s:
        w = s.sb("w", [P, 2, 3 * D])
        w_hi = s.sb("w_hi", [P, KD, 3 * D])
        w_lo = s.sb("w_lo", [P, KD, 3 * D])
        ident = s.sb("ident", [P, P])
        dest = s.sb("dest", [P, TOK_TILES], I32)
        got = s.sb("got", [P, TOK_TILES, D])
        x = s.sb("x", [P, NCH, TT, D])
        xn = s.sb("xn", [P, NCH, TT, D])
        stats = s.sb("stats", [P, NCH, TT, 6])
        mv = s.sb("mv", [P, NCH, TT, 2])
        std = s.sb("std", [P, NCH, TT])
        rstd = s.sb("rstd", [P, NCH, TT])
        xT_hi = s.sb("xT_hi", [P, NCH, KD, CH])
        xT_lo = s.sb("xT_lo", [P, NCH, KD, CH])
        qk_hi = s.sb("qk_hi", [P, QK_JOBS, CH])
        qk_lo = s.sb("qk_lo", [P, QK_JOBS, CH])
        v = s.sb("v", [P, TT, D])
        ps_t = s.ps("ps_t", [P, NT, CH])
        ps_a = s.ps("ps_a", [P, NA, CH])
        ps_v = s.ps("ps_v", [P, NV, D])
        consts, w_hi_ok, w_ok, dest_in, x2_ok, stats_ok, mv_ok, std_ok, rstd_ok, xn_ok = (s.sem(n) for n in (
            "consts", "w_hi_ok", "w_ok", "dest_in", "x2_ok", "stats_ok", "mv_ok", "std_ok", "rstd_ok", "xn_ok"))
        t_full, t_hi_ok, t_read, a_full, qk_hi_ok, a_read, v_full, v_read, qk_out, v_out = (s.sem(n) for n in (
            "t_full", "t_hi_ok", "t_read", "a_full", "qk_hi_ok", "a_read", "v_full", "v_read", "qk_out", "v_out"))
        got_in = [s.pool_dma_sem(f"got_in{g}") for g in range(B * NCH)]
        w_in, x_in, x_out = s.sems("w_in", 2), s.sems("x_in", NCH), s.sems("x_out", NCH)
        block = s.block()

        @block.sync
        def _(sp):
            sp.dma_start(dest[:, :], a["s_dest"]).then_inc(dest_in, 16)
            for ch in range(NCH):
                sp.dma_start(x[:, ch, :, :], rows(a["s_x1"], ch * CH, CH)).then_inc(x_in[ch], 16)
            sp.dma_start(ident[:, :], a["c_ident"]).then_inc(consts, 16)
            for k in range(KD):
                if k >= 2:
                    sp.wait_ge(w_ok, Z + k - 1)
                sp.dma_start(w[:, k % 2, :], a["w_qkv"][k * P:(k + 1) * P, :]).then_inc(w_in[k % 2], 16)
            def chunk(i, ch, more, more_2):
                g = i * NCH + ch
                tok = i * L + ch * CH
                s.hold(sp, x2_ok, Z + (g + 1) * TT)
                sp.dma_start(rows(a["s_x2"], tok, CH), x[:, ch, :, :]).then_inc(x_out[ch], 16)
                if more_2:
                    s.hold(sp, x_out[ch], Z + (i + 1) * 16)
                    s.hold(sp, xn_ok, Z + (g + 1) * TT)
                    sp.dma_start(x[:, ch, :, :], rows(a["s_x1"], tok + L, CH)).then_inc(x_in[ch], 16)
                s.hold(sp, a_read, Z + (g + 1) * QK_JOBS + NA)
                for n, name in enumerate(("s_q", "s_k")):
                    for part, src in enumerate((qk_hi, qk_lo)):
                        sp.dma_start(cols(a[name][:, part, :, :], tok, CH), src[:, n * NHG:(n + 1) * NHG, :]).then_inc(qk_out, 16)
                s.hold(sp, v_read, Z + (g + 1) * TT + NV)
                sp.dma_start(rows(a["s_v"], tok, CH), v[:, :, :]).then_inc(v_out, 16)

            over_chunks(sp, chunk)
            sp.wait_ge(qk_out, Z + B * NCH * 64)
            sp.wait_ge(v_out, Z + B * NCH * 16)
            for ch in range(NCH):
                sp.wait_ge(x_out[ch], Z + B * 16)

        @block.gpsimd
        def _(pool):
            pool.wait_ge(dest_in, Z + 16)
            for j in range(TOK_TILES):
                nc.gpsimd.indirect_dma_start(got[:, j, :], None, a["s_sel_out"],
                                             bass.IndirectOffsetOnAxis(ap=dest[:, j:j + 1].bitcast(U32), axis=0)).then_inc(got_in[j // TT], 16)

        @block.tensor
        def _(pe):
            def turn(j, slot):
                pe.wait_ge(xn_ok, Z + (j + 1) * TT)
                for k in range(KD):
                    pe.wait_ge(t_read, Z + j * KD + k + 1)
                    for t in range(TT):
                        last = nc.tensor.transpose(ps_t[:, k % NT, t * P:(t + 1) * P], xn[:, slot, t, k * P:(k + 1) * P], ident[:, :])
                    last.then_inc(t_full, 1)

            pe.wait_ge(consts, Z + 16)
            turn(0, 0)
            pe.wait_ge(w_ok, Z + KD)
            def chunk(i, ch, more, more_2):
                g = i * NCH + ch
                xT = lambda c: [(xT_hi[:, ch, k, c], xT_lo[:, ch, k, c]) for k in range(KD)]
                weights = lambda c: [(w_hi[:, k, c], w_lo[:, k, c]) for k in range(KD)]
                pe.wait_ge(t_read, Z + (g + 1) * KD + NT)
                for m in range(QK_JOBS):
                    if m == TURN_AT and more:
                        turn(g + 1, 1 - ch)
                    pe.wait_ge(a_read, Z + g * QK_JOBS + m + 1)
                    exact_product(nc, ps_a[:, m % NA, :], weights(slice(m * P, (m + 1) * P)), xT(slice(0, CH))).then_inc(a_full, 1)
                for t in range(TT):
                    pe.wait_ge(v_read, Z + g * TT + t + 1)
                    exact_product(nc, ps_v[:, t % NV, :], xT(slice(t * P, (t + 1) * P)), weights(slice(2 * D, 3 * D))).then_inc(v_full, 1)

            over_chunks(pe, chunk)

        @block.scalar
        def _(act):
            def deviation(j, slot):
                act.wait_ge(mv_ok, Z + (j + 1) * TT)
                nc.scalar.activation(std[:, slot, :], mv[:, slot, :, 1], ACT.Sqrt, bias=EPS).then_inc(std_ok, 1)

            def read_turned(j, slot):
                for k in range(KD):
                    act.wait_ge(t_full, Z + j * KD + k + 1)
                    nc.scalar.copy(xT_hi[:, slot, k, :].bitcast(F32R), ps_t[:, k % NT, :]).then_inc(t_hi_ok, 1)

            for k in range(KD):
                if k == KD // 2:
                    deviation(0, 0)
                act.wait_ge(w_in[k % 2], Z + (k // 2 + 1) * 16)
                nc.scalar.copy(w_hi[:, k, :].bitcast(F32R), w[:, k % 2, :]).then_inc(w_hi_ok, 1)
            read_turned(0, 0)
            def chunk(i, ch, more, more_2):
                g = i * NCH + ch
                if more:
                    deviation(g + 1, 1 - ch)
                act.wait_ge(qk_out, Z + g * 64)
                for m in range(QK_JOBS):
                    if m == TURN_AT and more:
                        act.wait_ge(v_full, Z + g * TT)
                        read_turned(g + 1, 1 - ch)
                    act.wait_ge(a_full, Z + g * QK_JOBS + m + 1)
                    nc.scalar.copy(qk_hi[:, m, :].bitcast(F32R), ps_a[:, m % NA, :]).then_inc(qk_hi_ok, 1)

            over_chunks(act, chunk)

        @block.vector
        def _(dve):
            def add_and_normalise(j, slot, loads):
                dve.wait_ge(x_in[slot], Z + loads * 16)
                nc.vector.tensor_tensor(x[:, slot, :, :], x[:, slot, :, :], got[:, bass.ds(j * TT, TT), :], ALU.add).then_inc(x2_ok, TT)
                dve.wait_ge(x2_ok, Z + (j + 1) * TT)
                for t in range(TT):
                    nc.vector.bn_stats(stats[:, slot, t, :], x[:, slot, t, :]).then_inc(stats_ok, 1)
                s.hold(dve, stats_ok, Z + (j + 1) * TT)
                for t in range(TT):
                    nc.vector.bn_aggr(mv[:, slot, t, :], stats[:, slot, t, :]).then_inc(mv_ok, 1)
                dve.wait_ge(std_ok, Z + j + 1)
                nc.vector.reciprocal(rstd[:, slot, :], std[:, slot, :]).then_inc(rstd_ok, 1)
                dve.wait_ge(rstd_ok, Z + j + 1)
                for t in range(TT):
                    nc.vector.tensor_scalar(xn[:, slot, t, :], x[:, slot, t, :], mv[:, slot, t, 0:1], rstd[:, slot, t:t + 1],
                                            ALU.subtract, ALU.mult).then_inc(xn_ok, 1)

            def read_turned(j, slot):
                for k in range(KD):
                    dve.wait_ge(t_hi_ok, Z + j * KD + k + 1)
                    nc.vector.tensor_tensor(xT_lo[:, slot, k, :].bitcast(F32R), ps_t[:, k % NT, :], xT_hi[:, slot, k, :],
                                            ALU.subtract).then_inc(t_read, 1)

            nc.vector.nop().then_inc(t_read, NT)
            nc.vector.nop().then_inc(a_read, NA)
            nc.vector.nop().then_inc(v_read, NV)
            for k in range(KD):
                if k == KD // 2:
                    dve.wait_ge(got_in[0], 16 * TT)
                    add_and_normalise(0, 0, 1)
                dve.wait_ge(w_hi_ok, Z + k + 1)
                nc.vector.tensor_tensor(w_lo[:, k, :].bitcast(F32R), w[:, k % 2, :], w_hi[:, k, :], ALU.subtract).then_inc(w_ok, 1)
            read_turned(0, 0)
            def chunk(i, ch, more, more_2):
                g = i * NCH + ch
                if more:
                    for n in range(ch + 1, ch + 2) if ch + 1 < NCH else range(NCH, B * NCH):
                        dve.wait_ge(got_in[n], 16 * TT)
                    add_and_normalise(g + 1, 1 - ch, i + ch + 1)
                dve.wait_ge(qk_out, Z + g * 64)
                for m in range(QK_JOBS):
                    if m == TURN_AT and more:
                        read_turned(g + 1, 1 - ch)
                    dve.wait_ge(qk_hi_ok, Z + g * QK_JOBS + m + 1)
                    nc.vector.tensor_tensor(qk_lo[:, m, :].bitcast(F32R), ps_a[:, m % NA, :], qk_hi[:, m, :],
                                            ALU.subtract).then_inc(a_read, 1)
                dve.wait_ge(v_out, Z + g * 16)
                for t in range(TT):
                    dve.wait_ge(v_full, Z + g * TT + t + 1)
                    nc.vector.tensor_copy(v[:, t, :], ps_v[:, t % NV, :]).then_inc(v_read, 1)

            over_chunks(dve, chunk)


def attend(nc, a, late_weights):
    R, NS, AHEAD = 4, 2, 2
    UQ = HG
    UB = NQT * UQ
    U = B * UB
    LATE = NQT // 2 * UQ
    NORM = 4
    SCALE = 1.0 / float(HD) ** 0.5
    HIGH = 3.0e38
    Z_ROWS = 2 * P
    with Scope(nc, "att") as s:
        ident = s.sb("ident", [P, P])
        mask = s.sb("mask", [P, L])
        q = s.sb("q", [P, B, HG, L])
        kT = s.sb("kT", [P, B, HG, L])
        v_rows = s.sb("v_rows", [P, B, NQT, P])
        v = s.sb("v", [P, B, NQT, HG, P])
        sm = s.sb("sm", [P, R, L])
        low = s.sb("low", [P, R])
        p = s.sb("p", [P, R, L])
        pT = s.sb("pT", [P, 2, NQT, P])
        total = s.sb("total", [P, NORM, HG])
        oT = s.sb("oT", [P, 2, P])
        rec = s.sb("rec", [P, 2, HG])
        o = s.sb("o", [P, B, NQT, HG, HD])
        zeros = s.sb("zeros", [P, Z_ROWS // P, D])
        ps_s = s.ps("ps_s", [P, NS, L])
        ps_t = s.ps("ps_t", [P, 2, 4, P])
        ps_o = s.ps("ps_o", [P, 2, 512])
        v_zero, v_ok, oT_ok, o_full = (s.sem(n) for n in ("v_zero", "v_ok", "oT_ok", "o_full"))
        consts, s_full, low_ok, exp_ok, t0_full, t1_full, e0_ok, e1_ok, pv_ok, rec_ok, norm_ok, z_ok = (s.sem(n) for n in (
            "consts", "s_full", "low_ok", "exp_ok", "t0_full", "t1_full", "e0_ok", "e1_ok", "pv_ok", "rec_ok", "norm_ok", "z_ok"))
        w_in = s.sem("w_in")
        z_out = s.pool_dma_sem("z_out")
        g_in, o_out = s.sems("g_in", B), s.sems("o_out", B)
        block = s.block()
        G_LOADS = 2 * P // HD + 1

        def unit(u):
            return u // UB, u % UB // UQ, u % UQ

        def late(i, u):
            return i * B * LATE + (u // UB) * LATE + (u % UB - LATE)

        @block.sync
        def _(sp):
            def load(group, b):
                part = slice(b * L, (b + 1) * L)
                for n in range(P // HD):
                    r = slice(n * HD, (n + 1) * HD)
                    for dst, name, which in ((q, "s_q", n // 2), (kT, "s_k", n % 2)):
                        sp.dma_start(dst[r, b, :, :], a[name][bass.ds(group, 1), which, :, part].rearrange(
                            "g (h d) t -> d (g h) t", d=HD)).then_inc(g_in[b], 16)
                sp.dma_start(v_rows[:, b, :, :],
                             a["s_v"][part, bass.ds(group * P, P)].rearrange("(t p) n -> p t n", p=P)).then_inc(g_in[b], 16)

            def store(group, b):
                s.hold(sp, norm_ok, Z + (group * B + b + 1) * NQT + NORM)
                sp.dma_start(a["s_o"][b * L:(b + 1) * L, bass.ds(group * P, P)].rearrange("(t p) n -> p t n", p=P),
                             o[:, b, :, :, :].rearrange("p t h d -> p t (h d)")).then_inc(o_out[b], 16)

            load(0, 0)
            sp.dma_start(mask[:, :], a["c_mask"]).then_inc(consts, 16)
            sp.dma_start(ident[:, :], a["c_ident"]).then_inc(consts, 16)
            load(0, 1)
            with sp.Fori(0, NHG - 1) as i:
                for b in range(B):
                    store(i, b)
                    load(i + 1, b)
            for w, name in late_weights:
                sp.dma_start(w[:, :, :], a[name].rearrange("(k p) n -> p k n", p=P)).then_inc(w_in, 16)
            for b in range(B):
                store(NHG - 1, b)
            for b in range(B):
                sp.wait_ge(o_out[b], Z + NHG * 16)
            sp.wait_ge(w_in, Z + len(late_weights) * 16)

        @block.gpsimd
        def _(pool):
            nc.gpsimd.memset(v[:, :, :, :, :], 0.0).then_inc(v_zero, 1)
            nc.gpsimd.memset(zeros[:, :, :], 0.0).then_inc(z_ok, 1)
            pool.wait_ge(v_zero, Z + 1)

            def place(group, b):
                s.hold(pool, g_in[b], Z + (group + 1) * G_LOADS * 16)
                for h in range(HG):
                    c = slice(h * HD, (h + 1) * HD)
                    nc.gpsimd.tensor_copy(v[:, b, :, h, c], v_rows[:, b, :, c]).then_inc(v_ok, 1)

            for b in range(B):
                place(0, b)
            pool.wait_ge(z_ok, Z + 1)
            with pool.Fori(0, N_TILES * SLOT_TILE // Z_ROWS) as i:
                nc.gpsimd.dma_start(rows(a["s_xs"], i * Z_ROWS, Z_ROWS), zeros[:, :, :]).then_inc(z_out, 16)
            with pool.Fori(1, NHG) as i:
                for b in range(B):
                    place(i, b)
            pool.wait_ge(z_out, N_TILES * SLOT_TILE // Z_ROWS * 16)

        @block.tensor
        def _(pe):
            pe.wait_ge(consts, Z + 32)
            with pe.Fori(0, NHG) as i:

                def score(u):
                    b, t, h = unit(u)
                    if u % UB == 0:
                        pe.wait_ge(g_in[b], Z + (i + 1) * G_LOADS * 16)
                    pe.wait_ge(low_ok, Z + i * U + u + 1)
                    keys = (t + 1) * P
                    for k in range(0, keys, 512):
                        n = min(512, keys - k)
                        last = nc.tensor.matmul(ps_s[:, u % NS, k:k + n], q[:, b, h, t * P:(t + 1) * P].bitcast(F32R),
                                                kT[:, b, h, k:k + n].bitcast(F32R), start=True, stop=True)
                    last.then_inc(s_full, 1)

                def turn(u):
                    b, t, h = unit(u)
                    pe.wait_ge(exp_ok, Z + i * U + u + R + 1)
                    for half in range(t // 4 + 1):
                        if half == 0:
                            pe.wait_ge(e0_ok, Z + i * U + u)
                        else:
                            pe.wait_ge(e1_ok, Z + late(i, u))
                        for k in range(4 * half, min(4 * half + 4, t + 1)):
                            last = nc.tensor.transpose(ps_t[:, half, k % 4, :], p[:, u % R, k * P:(k + 1) * P], ident[:, :])
                        last.then_inc((t0_full, t1_full)[half], 1)

                def weigh(u):
                    b, t, h = unit(u)
                    if h == 0:
                        pe.wait_ge(norm_ok, Z + (i * B + b) * NQT + t + NORM - 1)
                        if t == 0:
                            pe.wait_ge(v_ok, Z + (i * B + b + 1) * HG)
                    pe.wait_ge(e0_ok, Z + i * U + u + 1)
                    if t >= 4:
                        pe.wait_ge(e1_ok, Z + late(i, u) + 1)
                    for k in range(t + 1):
                        last = nc.tensor.matmul(ps_o[:, t % 2, 0:P], v[:, b, k, h, :], pT[:, u % 2, k, :],
                                                start=(h == 0 and k == 0), stop=(h == HG - 1 and k == t))
                    last.then_inc(pv_ok, 1)

                def turn_back(n):
                    pe.wait_ge(oT_ok, Z + i * B * NQT + n + 1)
                    nc.tensor.transpose(ps_o[:, n % 2, P:2 * P], oT[:, n % 2, :], ident[:, :]).then_inc(o_full, 1)

                for u in range(AHEAD + 1):
                    score(u)
                for u in range(U):
                    if u + AHEAD + 1 < U:
                        score(u + AHEAD + 1)
                    turn(u)
                    if u:
                        weigh(u - 1)
                    if u >= UQ and u % UQ == 2:
                        turn_back(u // UQ - 1)
                weigh(U - 1)
                turn_back(U // UQ - 1)

        @block.scalar
        def _(act):
            nc.scalar.nop().then_inc(exp_ok, R)
            with act.Fori(0, NHG) as i:

                def exponential(u):
                    b, t, h = unit(u)
                    keys = (t + 1) * P
                    if h == 0:
                        act.wait_ge(norm_ok, Z + (i * B + b) * NQT + t + 1)
                    act.wait_ge(low_ok, Z + i * U + u + NS + 1)
                    act.wait_ge(pv_ok, Z + i * U + u + 1)
                    nc.scalar.activation(p[:, u % R, 0:keys], sm[:, u % R, 0:keys], ACT.Exp, bias=low[:, u % R:u % R + 1],
                                         scale=-1.0, accum_out=total[:, t % NORM, h:h + 1]).then_inc(exp_ok, 1)

                def read_out(n):
                    act.wait_ge(pv_ok, Z + i * U + (n + 1) * UQ + R)
                    nc.scalar.copy(oT[:, n % 2, :], ps_o[:, n % 2, 0:P]).then_inc(oT_ok, 1)

                for u in range(AHEAD):
                    exponential(u)
                for u in range(U):
                    if u + AHEAD < U:
                        exponential(u + AHEAD)
                    b, t, h = unit(u)
                    if t >= 4:
                        act.wait_ge(t1_full, Z + late(i, u) + 1)
                        act.wait_ge(pv_ok, Z + i * U + u + R - 1)
                        nc.scalar.copy(pT[:, u % 2, 4:t + 1, :], ps_t[:, 1, 0:t - 3, :]).then_inc(e1_ok, 1)
                    if u >= UQ and u % UQ == 1:
                        read_out(u // UQ - 1)
                read_out(U // UQ - 1)

        @block.vector
        def _(dve):
            nc.vector.nop().then_inc(low_ok, NS)
            nc.vector.nop().then_inc(norm_ok, NORM)
            nc.vector.nop().then_inc(pv_ok, R)
            dve.wait_ge(consts, Z + 32)
            with dve.Fori(0, NHG) as i:

                def bound(u):
                    b, t, h = unit(u)
                    keys = (t + 1) * P
                    dve.wait_ge(s_full, Z + i * U + u + 1)
                    s.hold(dve, exp_ok, Z + i * U + u + 1)
                    nc.vector.tensor_tensor_reduce(sm[:, u % R, 0:keys], ps_s[:, u % NS, 0:keys], mask[:, L - keys:L], -SCALE, HIGH,
                                                   ALU.add, ALU.min, low[:, u % R:u % R + 1]).then_inc(low_ok, 1)

                def normalise(n):
                    b, t = n // NQT, n % NQT
                    g = i * B * NQT + n
                    s.hold(dve, exp_ok, Z + i * U + (n + 1) * UQ + R)
                    dve.wait_ge(norm_ok, Z + g + NORM - 1)
                    nc.vector.reciprocal(rec[:, t % 2, :], total[:, t % NORM, :]).then_inc(rec_ok, 1)
                    s.hold(dve, o_full, Z + g + 1)
                    dve.wait_ge(rec_ok, Z + g + 1)
                    if t == 0:
                        dve.wait_ge(o_out[b], Z + i * 16)
                    nc.vector.tensor_tensor(o[:, b, t, :, :], ps_o[:, t % 2, P:2 * P].rearrange("p (h d) -> p h d", d=HD), rec[:, t % 2, :].unsqueeze(2).to_broadcast([P, HG, HD]),
                                            ALU.mult).then_inc(norm_ok, 1)

                for u in range(AHEAD):
                    bound(u)
                for u in range(U):
                    if u + AHEAD < U:
                        bound(u + AHEAD)
                    b, t, h = unit(u)
                    n = min(t + 1, 4)
                    dve.wait_ge(t0_full, Z + i * U + u + 1)
                    dve.wait_ge(pv_ok, Z + i * U + u + R - 1)
                    nc.vector.tensor_copy(pT[:, u % 2, 0:n, :], ps_t[:, 0, 0:n, :]).then_inc(e0_ok, 1)
                    if u >= UQ and u % UQ == 3:
                        normalise(u // UQ - 1)
                normalise(U // UQ - 1)


def attend_out(nc, a, w):
    NT, NP = 2, 4
    TURN_AT = 2
    with Scope(nc, "att_out") as s:
        ident = s.sb("ident", [P, P])
        w_hi = s.sb("w_hi", [P, KD, D])
        w_lo = s.sb("w_lo", [P, KD, D])
        o = s.sb("o", [P, NCH, TT, D])
        oT_hi = s.sb("oT_hi", [P, NCH, KD, CH])
        oT_lo = s.sb("oT_lo", [P, NCH, KD, CH])
        x = s.sb("x", [P, NCH, TT, D])
        xn = s.sb("xn", [P, NCH, TT, D])
        stats = s.sb("stats", [P, NCH, TT, 6])
        mv = s.sb("mv", [P, NCH, TT, 2])
        std = s.sb("std", [P, NCH, TT])
        rstd = s.sb("rstd", [P, NCH, TT])
        ps_t = s.ps("ps_t", [P, NT, CH])
        ps = s.ps("ps", [P, NP, D])
        consts, w_hi_ok, w_ok, t_full, t_hi_ok, t_read, full, read, stats_ok, mv_ok, std_ok, rstd_ok, xn_ok = (s.sem(n) for n in (
            "consts", "w_hi_ok", "w_ok", "t_full", "t_hi_ok", "t_read", "full", "read", "stats_ok", "mv_ok", "std_ok", "rstd_ok", "xn_ok"))
        o_in, x_in, x_out, xn_out = (s.sems(n, NCH) for n in ("o_in", "x_in", "x_out", "xn_out"))
        block = s.block()

        @block.sync
        def _(sp):
            def load_o(ch, tok):
                sp.dma_start(o[:, ch, :, :], rows(a["s_o"], tok, CH)).then_inc(o_in[ch], 16)

            def load_x(ch, tok):
                sp.dma_start(x[:, ch, :, :], rows(a["s_x2"], tok, CH)).then_inc(x_in[ch], 16)

            sp.dma_start(ident[:, :], a["c_ident"]).then_inc(consts, 16)
            for ch in range(NCH):
                load_o(ch, ch * CH)
                load_x(ch, ch * CH)
            def chunk(i, ch, more, more_2):
                g = i * NCH + ch
                tok = i * L + ch * CH
                if more_2:
                    s.hold(sp, t_full, Z + (g + 1) * KD)
                    load_o(ch, tok + L)
                s.hold(sp, read, Z + (g + 1) * TT + NP)
                sp.dma_start(rows(a["s_x3"], tok, CH), x[:, ch, :, :]).then_inc(x_out[ch], 16)
                s.hold(sp, xn_ok, Z + (g + 1) * TT)
                sp.dma_start(rows(a["s_n3"], tok, CH), xn[:, ch, :, :]).then_inc(xn_out[ch], 16)
                if more_2:
                    s.hold(sp, x_out[ch], Z + (i + 1) * 16)
                    load_x(ch, tok + L)

            over_chunks(sp, chunk)
            for ch in range(NCH):
                for done in (x_out, xn_out):
                    sp.wait_ge(done[ch], Z + B * 16)

        @block.tensor
        def _(pe):
            def turn(j, slot, loads):
                pe.wait_ge(o_in[slot], Z + loads * 16)
                for k in range(KD):
                    pe.wait_ge(t_read, Z + j * KD + k + 1)
                    for t in range(TT):
                        last = nc.tensor.transpose(ps_t[:, k % NT, t * P:(t + 1) * P], o[:, slot, t, k * P:(k + 1) * P], ident[:, :])
                    last.then_inc(t_full, 1)

            pe.wait_ge(consts, Z + 16)
            turn(0, 0, 1)
            pe.wait_ge(w_ok, Z + KD)
            def chunk(i, ch, more, more_2):
                g = i * NCH + ch
                pe.wait_ge(t_read, Z + (g + 1) * KD + NT)
                for t in range(TT):
                    if t == TURN_AT and more:
                        turn(g + 1, 1 - ch, i + ch + 1)
                    pe.wait_ge(read, Z + g * TT + t + 1)
                    c = slice(t * P, (t + 1) * P)
                    exact_product(nc, ps[:, t, :], [(oT_hi[:, ch, k, c], oT_lo[:, ch, k, c]) for k in range(KD)],
                                  [(w_hi[:, k, :], w_lo[:, k, :]) for k in range(KD)]).then_inc(full, 1)

            over_chunks(pe, chunk)

        @block.scalar
        def _(act):
            def read_turned(j, slot):
                for k in range(KD):
                    act.wait_ge(t_full, Z + j * KD + k + 1)
                    nc.scalar.copy(oT_hi[:, slot, k, :].bitcast(F32R), ps_t[:, k % NT, :]).then_inc(t_hi_ok, 1)

            for k in range(KD):
                nc.scalar.copy(w_hi[:, k, :].bitcast(F32R), w[:, k, :]).then_inc(w_hi_ok, 1)
            read_turned(0, 0)
            def chunk(i, ch, more, more_2):
                g = i * NCH + ch
                if more:
                    act.wait_ge(full, Z + g * TT)
                    read_turned(g + 1, 1 - ch)
                act.wait_ge(mv_ok, Z + (g + 1) * TT)
                nc.scalar.activation(std[:, ch, :], mv[:, ch, :, 1], ACT.Sqrt, bias=EPS).then_inc(std_ok, 1)

            over_chunks(act, chunk)

        @block.vector
        def _(dve):
            def read_turned(j, slot):
                for k in range(KD):
                    dve.wait_ge(t_hi_ok, Z + j * KD + k + 1)
                    nc.vector.tensor_tensor(oT_lo[:, slot, k, :].bitcast(F32R), ps_t[:, k % NT, :], oT_hi[:, slot, k, :],
                                            ALU.subtract).then_inc(t_read, 1)

            nc.vector.nop().then_inc(t_read, NT)
            nc.vector.nop().then_inc(read, NP)
            for k in range(KD):
                dve.wait_ge(w_hi_ok, Z + k + 1)
                nc.vector.tensor_tensor(w_lo[:, k, :].bitcast(F32R), w[:, k, :], w_hi[:, k, :], ALU.subtract).then_inc(w_ok, 1)
            read_turned(0, 0)
            def chunk(i, ch, more, more_2):
                g = i * NCH + ch
                dve.wait_ge(x_in[ch], Z + (i + 1) * 16)
                for t in range(TT):
                    if t == TURN_AT and more:
                        read_turned(g + 1, 1 - ch)
                    dve.wait_ge(full, Z + g * TT + t + 1)
                    nc.vector.tensor_tensor(x[:, ch, t, :], x[:, ch, t, :], ps[:, t, :], ALU.add).then_inc(read, 1)
                    dve.wait_ge(read, Z + g * TT + t + NP + 1)
                    nc.vector.bn_stats(stats[:, ch, t, :], x[:, ch, t, :]).then_inc(stats_ok, 1)
                s.hold(dve, stats_ok, Z + (g + 1) * TT)
                for t in range(TT):
                    nc.vector.bn_aggr(mv[:, ch, t, :], stats[:, ch, t, :]).then_inc(mv_ok, 1)
                dve.wait_ge(std_ok, Z + g + 1)
                nc.vector.reciprocal(rstd[:, ch, :], std[:, ch, :]).then_inc(rstd_ok, 1)
                dve.wait_ge(rstd_ok, Z + g + 1)
                dve.wait_ge(xn_out[ch], Z + i * 16)
                for t in range(TT):
                    nc.vector.tensor_scalar(xn[:, ch, t, :], x[:, ch, t, :], mv[:, ch, t, 0:1], rstd[:, ch, t:t + 1],
                                            ALU.subtract, ALU.mult).then_inc(xn_ok, 1)

            over_chunks(dve, chunk)


def shared_ffn(nc, a, wg, wu, wd):
    NT, NG, NV = 2, 4, 2
    KS = I_SH // P
    TURN_AT = 2
    with Scope(nc, "shr") as s:
        wg_hi, wg_lo, wu_hi, wu_lo = (s.sb(n, [P, KD, I_SH]) for n in ("wg_hi", "wg_lo", "wu_hi", "wu_lo"))
        wd_hi, wd_lo = (s.sb(n, [P, KS, D]) for n in ("wd_hi", "wd_lo"))
        cent = s.sb("cent", [P, KD, E])
        ident = s.sb("ident", [P, P])
        xn = s.sb("xn", [P, NCH, TT, D])
        x = s.sb("x", [P, NCH, TT, D])
        xT = s.sb("xT", [P, KD, CH])
        xT_hi = s.sb("xT_hi", [P, NCH, KD, CH])
        xT_lo = s.sb("xT_lo", [P, NCH, KD, CH])
        sg = s.sb("sg", [P, 2, CH])
        h = s.sb("h", [P, 2, CH])
        hT_hi = s.sb("hT_hi", [P, KS, CH])
        hT_lo = s.sb("hT_lo", [P, KS, CH])
        lg = s.sb("lg", [P, NCH, TT, E])
        ps_t = s.ps("ps_t", [P, NT, CH])
        ps_g = s.ps("ps_g", [P, NG, CH])
        ps_v = s.ps("ps_v", [P, NV, D])
        consts, w_hi_ok, w_ok, t_full, t_read, t_hi_ok, t_lo_ok, g_full, silu_ok, h_ok, h_hi_ok, h_lo_ok, v_full, v_read = (s.sem(n) for n in (
            "consts", "w_hi_ok", "w_ok", "t_full", "t_read", "t_hi_ok", "t_lo_ok", "g_full", "silu_ok", "h_ok", "h_hi_ok", "h_lo_ok", "v_full", "v_read"))
        xn_in, x_in, x_out, lg_out = (s.sems(n, NCH) for n in ("xn_in", "x_in", "x_out", "lg_out"))
        block = s.block()
        V_JOBS = 2 + TT

        @block.sync
        def _(sp):
            def load_xn(ch, tok):
                sp.dma_start(xn[:, ch, :, :], rows(a["s_n3"], tok, CH)).then_inc(xn_in[ch], 16)

            def load_x(ch, tok):
                sp.dma_start(x[:, ch, :, :], rows(a["s_x3"], tok, CH)).then_inc(x_in[ch], 16)

            sp.dma_start(ident[:, :], a["c_ident"]).then_inc(consts, 16)
            sp.dma_start(cent[:, :, :], a["cent"].rearrange("(k p) n -> p k n", p=P)).then_inc(consts, 16)
            for ch in range(NCH):
                load_xn(ch, ch * CH)
                load_x(ch, ch * CH)
            def chunk(i, ch, more, more_2):
                g = i * NCH + ch
                if more_2:
                    s.hold(sp, t_full, Z + (g + 1) * KD)
                    load_xn(ch, (i + 1) * L + ch * CH)
                s.hold(sp, v_read, Z + g * V_JOBS + NV + 2)
                sp.dma_start(a["s_lg"][:, bass.ds(g * (TT * E), TT * E)], lg[:, ch, :, :].rearrange("p t e -> p (t e)")).then_inc(lg_out[ch], 16)
                s.hold(sp, v_read, Z + (g + 1) * V_JOBS + NV)
                sp.dma_start(rows(a["s_x4"], i * L + ch * CH, CH), x[:, ch, :, :]).then_inc(x_out[ch], 16)
                if more_2:
                    s.hold(sp, x_out[ch], Z + (i + 1) * 16)
                    load_x(ch, (i + 1) * L + ch * CH)

            over_chunks(sp, chunk)
            for ch in range(NCH):
                sp.wait_ge(x_out[ch], Z + B * 16)
                sp.wait_ge(lg_out[ch], Z + B * 16)

        @block.tensor
        def _(pe):
            def turn(j, slot, loads):
                pe.wait_ge(xn_in[slot], Z + loads * 16)
                for k in range(KD):
                    pe.wait_ge(t_read, Z + j * KD + k + 1)
                    for t in range(TT):
                        last = nc.tensor.transpose(ps_t[:, k % NT, t * P:(t + 1) * P], xn[:, slot, t, k * P:(k + 1) * P], ident[:, :])
                    last.then_inc(t_full, 1)

            pe.wait_ge(consts, Z + 32)
            turn(0, 0, 1)
            def chunk(i, ch, more, more_2):
                g = i * NCH + ch
                pe.wait_ge(t_read, Z + (g + 1) * KD + NT)
                for t in range(TT):
                    if t % 2 == 0:
                        pe.wait_ge(v_read, Z + g * V_JOBS + t // 2 + 1)
                    for k in range(KD):
                        last = nc.tensor.matmul(ps_v[:, t // 2, (t % 2) * E:(t % 2 + 1) * E], xT[:, k, t * P:(t + 1) * P], cent[:, k, :],
                                                start=(k == 0), stop=(k == KD - 1))
                    if t % 2:
                        last.then_inc(v_full, 1)
                pe.wait_ge(t_lo_ok, Z + (g + 1) * KD)
                pe.wait_ge(w_ok, Z + 3 * KD)
                xT_parts = [(xT_hi[:, ch, k, :], xT_lo[:, ch, k, :]) for k in range(KD)]
                for m in range(KS):
                    if m == TURN_AT and more:
                        turn(g + 1, 1 - ch, i + ch + 1)
                    c = slice(m * P, (m + 1) * P)
                    pe.wait_ge(h_ok, Z + g * KS + m + 1)
                    for n, (hi, lo) in enumerate(((wg_hi, wg_lo), (wu_hi, wu_lo))):
                        exact_product(nc, ps_g[:, (2 * m + n) % NG, :], [(hi[:, k, c], lo[:, k, c]) for k in range(KD)],
                                      xT_parts).then_inc(g_full, 1)
                pe.wait_ge(h_lo_ok, Z + (g + 1) * KS)
                for t in range(TT):
                    c = slice(t * P, (t + 1) * P)
                    pe.wait_ge(v_read, Z + g * V_JOBS + 2 + t + 1)
                    exact_product(nc, ps_v[:, t % NV, :], [(hT_hi[:, k, c], hT_lo[:, k, c]) for k in range(KS)],
                                  [(wd_hi[:, k, :], wd_lo[:, k, :]) for k in range(KS)]).then_inc(v_full, 1)

            over_chunks(pe, chunk)

        @block.scalar
        def _(act):
            def first_part(j, slot):
                for k in range(KD):
                    act.wait_ge(t_read, Z + j * KD + k + NT + 1)
                    nc.scalar.copy(xT_hi[:, slot, k, :].bitcast(F32R), xT[:, k, :]).then_inc(t_hi_ok, 1)

            first_part(0, 0)
            for hi, w in ((wg_hi, wg), (wu_hi, wu), (wd_hi, wd)):
                for k in range(KD):
                    nc.scalar.copy(hi[:, k, :].bitcast(F32R), w[:, k, :]).then_inc(w_hi_ok, 1)
            def chunk(i, ch, more, more_2):
                g = i * NCH + ch
                for m in range(KS):
                    if m == TURN_AT and more:
                        act.wait_ge(g_full, Z + g * 2 * KS)
                        first_part(g + 1, 1 - ch)
                    act.wait_ge(g_full, Z + g * 2 * KS + 2 * m + 1)
                    act.wait_ge(h_ok, Z + g * KS + m + 1)
                    nc.scalar.activation(sg[:, m % 2, :], ps_g[:, 2 * m % NG, :], ACT.Silu).then_inc(silu_ok, 1)
                    if m == 0:
                        act.wait_ge(v_full, Z + g * V_JOBS)
                    act.wait_ge(h_ok, Z + g * KS + m + 3)
                    nc.scalar.copy(hT_hi[:, m, :].bitcast(F32R), h[:, m % 2, :]).then_inc(h_hi_ok, 1)

            over_chunks(act, chunk)

        @block.gpsimd
        def _(pool):
            def second_part(j, slot):
                for k in range(KD):
                    s.hold(pool, t_hi_ok, Z + j * KD + k + 1)
                    nc.gpsimd.tensor_tensor(xT_lo[:, slot, k, :].bitcast(F32R), xT[:, k, :], xT_hi[:, slot, k, :],
                                            ALU.subtract).then_inc(t_lo_ok, 1)

            second_part(0, 0)
            def chunk(i, ch, more, more_2):
                g = i * NCH + ch
                for m in range(KS):
                    if m == TURN_AT and more:
                        second_part(g + 1, 1 - ch)
                    s.hold(pool, h_hi_ok, Z + g * KS + m + 1)
                    nc.gpsimd.tensor_tensor(hT_lo[:, m, :].bitcast(F32R), h[:, m % 2, :], hT_hi[:, m, :],
                                            ALU.subtract).then_inc(h_lo_ok, 1)

            over_chunks(pool, chunk)

        @block.vector
        def _(dve):
            def read_turned(j):
                dve.wait_ge(t_lo_ok, Z + j * KD)
                for k in range(KD):
                    dve.wait_ge(t_full, Z + j * KD + k + 1)
                    nc.vector.tensor_copy(xT[:, k, :], ps_t[:, k % NT, :]).then_inc(t_read, 1)

            nc.vector.nop().then_inc(t_read, NT)
            nc.vector.nop().then_inc(h_ok, 2)
            nc.vector.nop().then_inc(v_read, NV)
            read_turned(0)
            for n, (hi, lo, w) in enumerate(((wg_hi, wg_lo, wg), (wu_hi, wu_lo, wu), (wd_hi, wd_lo, wd))):
                for k in range(KD):
                    dve.wait_ge(w_hi_ok, Z + n * KD + k + 1)
                    nc.vector.tensor_tensor(lo[:, k, :].bitcast(F32R), w[:, k, :], hi[:, k, :], ALU.subtract).then_inc(w_ok, 1)
            def chunk(i, ch, more, more_2):
                g = i * NCH + ch
                dve.wait_ge(lg_out[ch], Z + i * 16)
                for t in range(2):
                    dve.wait_ge(v_full, Z + g * V_JOBS + t + 1)
                    nc.vector.tensor_copy(lg[:, ch, 2 * t:2 * t + 2, :].rearrange("p t e -> p (t e)"), ps_v[:, t, 0:2 * E]).then_inc(v_read, 1)
                for m in range(KS):
                    if m == TURN_AT and more:
                        read_turned(g + 1)
                    dve.wait_ge(silu_ok, Z + g * KS + m + 1)
                    dve.wait_ge(g_full, Z + g * 2 * KS + 2 * m + 2)
                    dve.wait_ge(h_lo_ok, Z + g * KS + m - 1 if m >= 2 else Z + g * KS)
                    nc.vector.tensor_tensor(h[:, m % 2, :], sg[:, m % 2, :], ps_g[:, (2 * m + 1) % NG, :], ALU.mult).then_inc(h_ok, 1)
                dve.wait_ge(x_in[ch], Z + (i + 1) * 16)
                for t in range(TT):
                    dve.wait_ge(v_full, Z + g * V_JOBS + 2 + t + 1)
                    nc.vector.scalar_tensor_tensor(out=x[:, ch, t, :], in0=ps_v[:, t % NV, :], scalar=RATIO, in1=x[:, ch, t, :],
                                                   op0=ALU.mult, op1=ALU.add).then_inc(v_read, 1)

            over_chunks(dve, chunk)


def route_tokens(nc, a):
    NTE = TOK_TILES * E
    K256 = T // SLOT_TILE
    with Scope(nc, "route") as s:
        lg = s.sb("lg", [P, TOK_TILES, E])
        gb = s.sb("gb", [P, E])
        rev = s.sb("rev", [P, E])
        full_at = s.sb("full_at", [P, K256])
        tile_no = s.sb("tile_no", [P, N_TILES])
        earlier = s.sb("earlier", [P, P])
        ones = s.sb("ones", [P, P])
        aff = s.sb("aff", [P, TOK_TILES, E])
        cand = s.sb("cand", [P, TOK_TILES, E])
        tmp = s.sb("tmp", [P, TOK_TILES, E])
        one = s.sb("one", [P, TOPK, TOK_TILES, E])
        both = s.sb("both", [P, TOK_TILES, E])
        top = s.sb("top", [P, TOK_TILES])
        ta = s.sb("ta", [P, TOPK, TOK_TILES])
        wsum = s.sb("wsum", [P, TOK_TILES])
        wt = s.sb("wt", [P, TOPK, TOK_TILES])
        run = s.sb("run", [P, 2, TOK_TILES, E])
        pos = s.sb("pos", [P, TOK_TILES, E])
        cmp = s.sb("cmp", [P, E, K256])
        tiles = s.sb("tiles", [P, E])
        cum = s.sb("cum", [P, 2, E])
        base = s.sb("base", [P, E])
        cmp_t = s.sb("cmp_t", [P, N_TILES, E])
        ex_f = s.sb("ex_f", [P, N_TILES])
        ex_i = s.sb("ex_i", [P, N_TILES], I32)
        slot = s.sb("slot", [P, TOPK, TOK_TILES])
        slot_i = s.sb("slot_i", [P, TOPK, TOK_TILES], I32)
        xn = s.sb("xn", [P, TOK_TILES, D])
        ps_w = s.ps("ps_w", [P, 512])
        ps_n = s.ps("ps_n", [P, 512])
        loads, xn_in, clamp_ok, exp_ok, both_ok, pref_ok, st, out_ok, outs = (s.sem(n) for n in (
            "loads", "xn_in", "clamp_ok", "exp_ok", "both_ok", "pref_ok", "st", "out_ok", "outs"))
        sent = s.pool_dma_sem("sent")
        block = s.block()

        @block.sync
        def _(sp):
            sp.dma_start(lg[:, :, :].rearrange("p t e -> p (t e)"), a["s_lg"]).then_inc(loads, 16)
            sp.dma_start(gb[:, :], a["gate_b"].to_broadcast([P, E])).then_inc(loads, 16)
            sp.dma_start(rev[:, :], a["c_rev"].to_broadcast([P, E])).then_inc(loads, 16)
            sp.dma_start(full_at[:, :], a["c_full_at"].to_broadcast([P, K256])).then_inc(loads, 16)
            sp.dma_start(tile_no[:, :], a["c_tile_no"].to_broadcast([P, N_TILES])).then_inc(loads, 16)
            sp.dma_start(earlier[:, :], a["c_before"]).then_inc(loads, 16)
            sp.dma_start(ones[:, :], a["c_ones"]).then_inc(loads, 16)
            sp.dma_start(xn[:, :, :], rows(a["s_n3"], 0, T)).then_inc(xn_in, 16)
            sp.wait_ge(out_ok, Z + 2)
            sp.dma_start(a["s_expert"], ex_i[0:1, :]).then_inc(outs, 16)
            sp.dma_start(a["s_slot"], slot_i[:, :, :].rearrange("p k t -> p (k t)")).then_inc(outs, 16)
            sp.dma_start(a["s_wt"], wt[:, :, :].rearrange("p k t -> p (k t)")).then_inc(outs, 16)
            sp.wait_ge(outs, Z + 48)

        @block.scalar
        def _(act):
            act.wait_ge(clamp_ok, Z + 1)
            nc.scalar.activation(aff[:, :, :], lg[:, :, :], ACT.Exp, scale=-1.0).then_inc(exp_ok, 1)

        @block.tensor
        def _(pe):
            pe.wait_ge(loads, Z + 7 * 16)
            pe.wait_ge(both_ok, Z + 1)
            m = both[:, :, :].rearrange("p t e -> p (t e)")
            nc.tensor.matmul(ps_w[:, 0:NTE], earlier[:, :], m, start=True, stop=True)
            nc.tensor.matmul(ps_n[:, 0:NTE], ones[:, :], m, start=True, stop=True).then_inc(pref_ok, 1)

        @block.vector
        def _(dve):
            steps = [0]

            def after(ins):
                steps[0] += 1
                ins.then_inc(st, 1)
                dve.wait_ge(st, Z + steps[0])

            v = nc.vector
            shape = [P, TOK_TILES, E]
            per_token = lambda x: x.unsqueeze(2).to_broadcast(shape)
            per_expert = lambda x: x.unsqueeze(1).to_broadcast(shape)
            dve.wait_ge(loads, Z + 7 * 16)
            v.tensor_scalar(lg[:, :, :], lg[:, :, :], -87.0, None, ALU.max).then_inc(clamp_ok, 1)
            dve.wait_ge(exp_ok, Z + 1)
            after(v.tensor_scalar(aff[:, :, :], aff[:, :, :], 1.0, None, ALU.add))
            after(v.reciprocal(aff[:, :, :], aff[:, :, :]))
            after(v.tensor_tensor(cand[:, :, :], aff[:, :, :], per_expert(gb[:, :]), ALU.add))
            for k in range(TOPK):
                after(v.tensor_reduce(top[:, :], cand[:, :, :], AX.X, ALU.max))
                after(v.tensor_tensor(tmp[:, :, :], cand[:, :, :], per_token(top[:, :]), ALU.is_equal))
                after(v.tensor_tensor(tmp[:, :, :], tmp[:, :, :], per_expert(rev[:, :]), ALU.mult))
                after(v.tensor_reduce(top[:, :], tmp[:, :, :], AX.X, ALU.max))
                after(v.tensor_tensor(one[:, k, :, :], per_expert(rev[:, :]), per_token(top[:, :]), ALU.is_equal))
                after(v.tensor_tensor(tmp[:, :, :], one[:, k, :, :], aff[:, :, :], ALU.mult))
                after(v.tensor_reduce(ta[:, k, :], tmp[:, :, :], AX.X, ALU.add))
                if k == 0:
                    after(v.scalar_tensor_tensor(out=cand[:, :, :], in0=one[:, 0, :, :], scalar=-3.0e38, in1=cand[:, :, :],
                                                 op0=ALU.mult, op1=ALU.add))
            v.tensor_tensor(both[:, :, :], one[:, 0, :, :], one[:, 1, :, :], ALU.add).then_inc(both_ok, 1)
            after(v.tensor_tensor(wsum[:, :], ta[:, 0, :], ta[:, 1, :], ALU.add))
            after(v.tensor_scalar(wsum[:, :], wsum[:, :], RT_EPS, None, ALU.add))
            after(v.reciprocal(wsum[:, :], wsum[:, :]))
            after(v.tensor_tensor(wt[:, :, :], ta[:, :, :], wsum[:, :].unsqueeze(1).to_broadcast([P, TOPK, TOK_TILES]), ALU.mult))
            dve.wait_ge(pref_ok, Z + 1)
            after(v.tensor_copy(run[:, 0, :, :].rearrange("p t e -> p (t e)"), ps_n[:, 0:NTE]))
            src, width = 0, 1
            while width < TOK_TILES:
                after(v.tensor_copy(run[:, 1 - src, 0:width, :], run[:, src, 0:width, :]))
                after(v.tensor_tensor(run[:, 1 - src, width:, :], run[:, src, width:, :], run[:, src, 0:TOK_TILES - width, :], ALU.add))
                src, width = 1 - src, 2 * width
            total = run[:, src, TOK_TILES - 1, :]
            after(v.tensor_tensor(cmp[:, :, :], total.unsqueeze(2).to_broadcast([P, E, K256]),
                                  full_at[:, :].unsqueeze(1).to_broadcast([P, E, K256]), ALU.is_gt))
            after(v.tensor_reduce(tiles[:, :], cmp[:, :, :], AX.X, ALU.add))
            after(v.tensor_copy(cum[:, 0, :], tiles[:, :]))
            cs, width = 0, 1
            while width < E:
                after(v.tensor_copy(cum[:, 1 - cs, 0:width], cum[:, cs, 0:width]))
                after(v.tensor_tensor(cum[:, 1 - cs, width:], cum[:, cs, width:], cum[:, cs, 0:E - width], ALU.add))
                cs, width = 1 - cs, 2 * width
            after(v.tensor_tensor(base[:, :], cum[:, cs, :], tiles[:, :], ALU.subtract))
            after(v.tensor_scalar(base[:, :], base[:, :], float(SLOT_TILE), None, ALU.mult))
            after(v.tensor_tensor(pos[:, :, :].rearrange("p t e -> p (t e)"), ps_w[:, 0:NTE],
                                  run[:, src, :, :].rearrange("p t e -> p (t e)"), ALU.add))
            after(v.tensor_tensor(pos[:, :, :].rearrange("p t e -> p (t e)"), pos[:, :, :].rearrange("p t e -> p (t e)"),
                                  ps_n[:, 0:NTE], ALU.subtract))
            after(v.tensor_tensor(pos[:, :, :], pos[:, :, :], per_expert(base[:, :]), ALU.add))
            for k in range(TOPK):
                after(v.tensor_tensor(tmp[:, :, :], one[:, k, :, :], pos[:, :, :], ALU.mult))
                after(v.tensor_reduce(slot[:, k, :], tmp[:, :, :], AX.X, ALU.add))
            v.tensor_copy(slot_i[:, :, :], slot[:, :, :]).then_inc(out_ok, 1)
            after(v.tensor_tensor(cmp_t[:, :, :], cum[:, cs, :].unsqueeze(1).to_broadcast([P, N_TILES, E]),
                                  tile_no[:, :].unsqueeze(2).to_broadcast([P, N_TILES, E]), ALU.is_le))
            after(v.tensor_reduce(ex_f[:, :], cmp_t[:, :, :], AX.X, ALU.add))
            after(v.tensor_scalar(ex_f[:, :], ex_f[:, :], float(E - 1), None, ALU.min))
            v.tensor_copy(ex_i[:, :], ex_f[:, :]).then_inc(out_ok, 1)

        @block.gpsimd
        def _(pool):
            pool.wait_ge(xn_in, Z + 16)
            pool.wait_ge(out_ok, Z + 1)
            for k in range(TOPK):
                for j in range(TOK_TILES):
                    nc.gpsimd.indirect_dma_start(a["s_xs"], bass.IndirectOffsetOnAxis(ap=slot_i[:, k, j:j + 1].bitcast(U32), axis=0),
                                                 xn[:, j, :], None).then_inc(sent, 16)
            pool.wait_ge(sent, 16 * TOPK * TOK_TILES)


def experts(nc, a):
    ST = SLOT_TILE // P
    KI = I_E // P
    W = 2
    with Scope(nc, "moe") as s:
        ex = s.sb("ex", [1, N_TILES], I32)
        ident = s.sb("ident", [P, P])
        wg = s.sb("wg", [P, W, KD, I_E])
        wu = s.sb("wu", [P, W, KD, I_E])
        wd = s.sb("wd", [P, W, KI, D])
        xs = s.sb("xs", [P, W, ST, D])
        xT = s.sb("xT", [P, W, KD, SLOT_TILE])
        sg = s.sb("sg", [P, W, KI * SLOT_TILE])
        hT = s.sb("hT", [P, W, KI, SLOT_TILE])
        hT_hi = s.sb("hT_hi", [P, W, KI, SLOT_TILE])
        hT_lo = s.sb("hT_lo", [P, W, KI, SLOT_TILE])
        wd_hi = s.sb("wd_hi", [P, W, KI, D])
        wd_lo = s.sb("wd_lo", [P, W, KI, D])
        y = s.sb("y", [P, W, ST, D])
        ps_t = s.ps("ps_t", [P, 2, 2, SLOT_TILE])
        ps_g = s.ps("ps_g", [P, 2, KI * SLOT_TILE])
        ps_u = s.ps("ps_u", [P, 2, KI * SLOT_TILE])
        ps_y = s.ps("ps_y", [P, ST, D])
        consts, ex_in, t_full, t_read, g_full, u_full, silu_ok, h_ok, y_full, y_read = (s.sem(n) for n in (
            "consts", "ex_in", "t_full", "t_read", "g_full", "u_full", "silu_ok", "h_ok", "y_full", "y_read"))
        wd_hi_ok, wd_lo_ok, h_hi_ok, h_lo_ok = (s.sem(n) for n in ("wd_hi_ok", "wd_lo_ok", "h_hi_ok", "h_lo_ok"))
        w_in, wd_in, x_in, y_out = (s.sems(n, W) for n in ("w_in", "wd_in", "x_in", "y_out"))
        block = s.block()
        PAIRS = N_TILES // W

        @block.sync
        def _(sp):
            def load_x(j, w):
                sp.dma_start(xs[:, w, :, :], rows(a["s_xs"], j * SLOT_TILE, SLOT_TILE)).then_inc(x_in[w], 16)

            def load_w(j, w):
                e = sp.value_load(ex[0:1, bass.ds(j, 1)], min_val=0, max_val=E - 1)
                for dst, name, done in ((wg, "wg", w_in), (wu, "wu", w_in), (wd, "wd", wd_in)):
                    sp.dma_start(dst[:, w, :, :], a[name][bass.ds(e, 1), :, :].rearrange("e (k p) n -> p (e k) n", p=P)).then_inc(done[w], 16)

            def store(j, w):
                s.hold(sp, y_read, Z + (j + 1) * ST + ST)
                sp.dma_start(rows(a["s_ys"], j * SLOT_TILE, SLOT_TILE), y[:, w, :, :]).then_inc(y_out[w], 16)

            def load_after(j, w):
                s.hold(sp, t_full, Z + (j + 1) * 2)
                load_x(j + W, w)
                s.hold(sp, u_full, Z + j + 1)
                s.hold(sp, wd_lo_ok, Z + j + 1)
                load_w(j + W, w)

            sp.dma_start(ident[:, :], a["c_ident"]).then_inc(consts, 16)
            sp.dma_start(ex[:, :], a["s_expert"]).then_inc(ex_in, 16)
            for w in range(W):
                load_x(w, w)
            sp.wait_ge(ex_in, Z + 16)
            for w in range(W):
                load_w(w, w)
            with sp.Fori(0, PAIRS - 1) as i:
                for w in range(W):
                    load_after(i * W + w, w)
                    store(i * W + w, w)
            for j in range((PAIRS - 1) * W, N_TILES):
                if j + W < N_TILES:
                    load_after(j, j % W)
                store(j, j % W)
            for w in range(W):
                sp.wait_ge(y_out[w], Z + (N_TILES - w + 1) // W * 16)

        @block.tensor
        def _(pe):
            def turn(j, w, n):
                pe.wait_ge(x_in[w], Z + (n + 1) * 16)
                for kk in range(2):
                    pe.wait_ge(t_read, Z + j * 2 + kk + 1)
                    for k in range(2):
                        for t in range(ST):
                            last = nc.tensor.transpose(ps_t[:, kk, k, t * P:(t + 1) * P],
                                                       xs[:, w, t, (2 * kk + k) * P:(2 * kk + k + 1) * P], ident[:, :])
                    last.then_inc(t_full, 1)

            def gates_and_ups(j, w, n):
                pe.wait_ge(t_read, Z + (j + 1) * 2 + 2)
                pe.wait_ge(w_in[w], Z + (n + 1) * 32)
                pe.wait_ge(h_ok, Z + j + 1)
                for ps, wt, done in ((ps_g, wg, g_full), (ps_u, wu, u_full)):
                    for m in range(KI):
                        for k in range(KD):
                            last = nc.tensor.matmul(ps[:, w, m * SLOT_TILE:(m + 1) * SLOT_TILE], wt[:, w, k, m * P:(m + 1) * P],
                                                    xT[:, w, k, :], start=(k == 0), stop=(k == KD - 1))
                    last.then_inc(done, 1)

            def outputs(j, w):
                pe.wait_ge(h_lo_ok, Z + j + 1)
                pe.wait_ge(wd_lo_ok, Z + j + 1)
                for t in range(ST):
                    pe.wait_ge(y_read, Z + j * ST + t + 1)
                    c = slice(t * P, (t + 1) * P)
                    exact_product(nc, ps_y[:, t, :], [(hT_hi[:, w, m, c], hT_lo[:, w, m, c]) for m in range(KI)],
                                  [(wd_hi[:, w, m, :], wd_lo[:, w, m, :]) for m in range(KI)]).then_inc(y_full, 1)

            def step(j, w, n, more, more_2):
                if more:
                    gates_and_ups(j + 1, 1 - w, n + w)
                if more_2:
                    turn(j + 2, w, n + 1)
                outputs(j, w)

            pe.wait_ge(consts, Z + 16)
            turn(0, 0, 0)
            gates_and_ups(0, 0, 0)
            turn(1, 1, 0)
            with pe.Fori(0, PAIRS - 1) as i:
                for w in range(W):
                    step(i * W + w, w, i, True, True)
            for j in range((PAIRS - 1) * W, N_TILES):
                step(j, j % W, j // W, j + 1 < N_TILES, j + 2 < N_TILES)

        @block.scalar
        def _(act):
            def step(j, w, n):
                act.wait_ge(g_full, Z + j + 1)
                act.wait_ge(h_ok, Z + j + 1)
                nc.scalar.activation(sg[:, w, :], ps_g[:, w, :], ACT.Silu).then_inc(silu_ok, 1)
                act.wait_ge(wd_in[w], Z + (n + 1) * 16)
                act.wait_ge(y_full, Z + j * ST)
                nc.scalar.copy(wd_hi[:, w, :, :].bitcast(F32R), wd[:, w, :, :]).then_inc(wd_hi_ok, 1)
                act.wait_ge(h_ok, Z + j + 1 + W)
                nc.scalar.copy(hT_hi[:, w, :, :].bitcast(F32R), hT[:, w, :, :]).then_inc(h_hi_ok, 1)

            def read_out(j, w, n):
                act.wait_ge(y_out[w], Z + n * 16)
                for t in range(ST):
                    act.wait_ge(y_full, Z + j * ST + t + 1)
                    nc.scalar.copy(y[:, w, t, :], ps_y[:, t, :]).then_inc(y_read, 1)

            nc.scalar.nop().then_inc(y_read, ST)
            step(0, 0, 0)
            with act.Fori(0, PAIRS) as i:
                for w in range(W):
                    read_out(i * W + w, w, i)
                    step(i * W + w + 1, 1 - w, i + w)
            read_out(N_TILES - 1, 0, PAIRS)

        @block.gpsimd
        def _(pool):
            def step(j, w):
                s.hold(pool, wd_hi_ok, Z + j + 1)
                nc.gpsimd.tensor_tensor(wd_lo[:, w, :, :].bitcast(F32R), wd[:, w, :, :], wd_hi[:, w, :, :], ALU.subtract).then_inc(wd_lo_ok, 1)
                s.hold(pool, h_hi_ok, Z + j + 1)
                nc.gpsimd.tensor_tensor(hT_lo[:, w, :, :].bitcast(F32R), hT[:, w, :, :], hT_hi[:, w, :, :], ALU.subtract).then_inc(h_lo_ok, 1)

            with pool.Fori(0, PAIRS) as i:
                for w in range(W):
                    step(i * W + w, w)
            step(N_TILES - 1, 0)

        @block.vector
        def _(dve):
            def turned(j, w):
                if not isinstance(j, int) or j >= W:
                    dve.wait_ge(u_full, Z + j - 1)
                for kk in range(2):
                    dve.wait_ge(t_full, Z + j * 2 + kk + 1)
                    nc.vector.tensor_copy(xT[:, w, 2 * kk:2 * kk + 2, :], ps_t[:, kk, :, :]).then_inc(t_read, 1)

            def step(j, w, more_2):
                dve.wait_ge(silu_ok, Z + j + 1)
                dve.wait_ge(u_full, Z + j + 1)
                if not isinstance(j, int) or j >= W:
                    dve.wait_ge(h_lo_ok, Z + j - 1)
                nc.vector.tensor_tensor(hT[:, w, :, :].rearrange("p m t -> p (m t)"), sg[:, w, :], ps_u[:, w, :],
                                        ALU.mult).then_inc(h_ok, 1)
                if more_2:
                    turned(j + 2, w)

            nc.vector.nop().then_inc(t_read, 2)
            nc.vector.nop().then_inc(h_ok, W)
            turned(0, 0)
            turned(1, 1)
            for j in range(W):
                step(j, j, True)
            with dve.Fori(1, PAIRS - 1) as i:
                for w in range(W):
                    step(i * W + w, w, True)
            for j in range((PAIRS - 1) * W, N_TILES):
                step(j, j % W, j + 2 < N_TILES)


def combine(nc, a):
    with Scope(nc, "end") as s:
        slot = s.sb("slot", [P, TOPK, TOK_TILES], I32)
        wt = s.sb("wt", [P, TOPK, TOK_TILES])
        got = s.sb("got", [P, TOPK, TOK_TILES, D])
        x = s.sb("x", [P, TOK_TILES, D])
        slot_in, wt_in, add_ok, out_sent = (s.sem(n) for n in ("slot_in", "wt_in", "add_ok", "out_sent"))
        x_in = s.sems("x_in", NCH * B)
        got_in = [s.pool_dma_sem(f"got_in{j}") for j in range(TOK_TILES)]
        block = s.block()

        @block.sync
        def _(sp):
            sp.dma_start(slot[:, :, :].rearrange("p k t -> p (k t)"), a["s_slot"]).then_inc(slot_in, 16)
            sp.dma_start(wt[:, :, :].rearrange("p k t -> p (k t)"), a["s_wt"]).then_inc(wt_in, 16)
            for g in range(NCH * B):
                sp.dma_start(x[:, g * TT:(g + 1) * TT, :], rows(a["s_x4"], g * CH, CH)).then_inc(x_in[g], 16)
            for g in range(NCH * B):
                sp.wait_ge(add_ok, Z + (g + 1) * TT * TOPK)
                sp.dma_start(rows(a["out"], g * CH, CH), x[:, g * TT:(g + 1) * TT, :]).then_inc(out_sent, 16)
            sp.wait_ge(out_sent, Z + NCH * B * 16)

        @block.gpsimd
        def _(pool):
            pool.wait_ge(slot_in, Z + 16)
            for j in range(TOK_TILES):
                for k in range(TOPK):
                    nc.gpsimd.indirect_dma_start(got[:, k, j, :], None, a["s_ys"],
                                                 bass.IndirectOffsetOnAxis(ap=slot[:, k, j:j + 1].bitcast(U32), axis=0)).then_inc(got_in[j], 16)

        @block.vector
        def _(dve):
            dve.wait_ge(wt_in, Z + 16)
            for j in range(TOK_TILES):
                if j % TT == 0:
                    dve.wait_ge(x_in[j // TT], Z + 16)
                dve.wait_ge(got_in[j], TOPK * 16)
                for k in range(TOPK):
                    if k:
                        dve.wait_ge(add_ok, Z + j * TOPK + k)
                    nc.vector.scalar_tensor_tensor(out=x[:, j, :], in0=got[:, k, j, :], scalar=wt[:, k, j:j + 1], in1=x[:, j, :],
                                                   op0=ALU.mult, op1=ALU.add).then_inc(add_ok, 1)


SCRATCH = {
    "s_b": ((P, T), F32), "s_c": ((3, NC_T, P, T), BF16),
    "s_delta": ((NC_T, P, T), F32), "s_du": ((NC_T, P, T), F32),
    "s_x1": ((T, D), F32), "s_n1": ((T, D), F32), "s_x2": ((T, D), F32),
    "s_score": ((P, TOK_TILES), F32), "s_score_row": ((1, T), F32), "s_dest": ((P, TOK_TILES), I32),
    "s_sel_in": ((T, D), F32), "s_sel_out": ((T, D), F32),
    "s_q": ((NHG, 2, P, T), F32), "s_k": ((NHG, 2, P, T), F32), "s_v": ((T, D), F32),
    "s_xs": ((N_TILES * SLOT_TILE, D), F32), "s_ys": ((N_TILES * SLOT_TILE, D), F32),
    "s_o": ((T, D), F32), "s_x3": ((T, D), F32), "s_n3": ((T, D), F32), "s_x4": ((T, D), F32),
    "s_expert": ((1, N_TILES), I32), "s_slot": ((P, TOPK * TOK_TILES), I32), "s_wt": ((P, TOPK * TOK_TILES), F32),
    "s_lg": ((P, TOK_TILES * E), F32),
    "s_y": ((NC_T, P, T), F32),
    "s_u": ((NC_T, P, T), F32), "s_z": ((NC_T, P, T), F32),
}


def build(nc, a):
    def weights(stack, name, k, n):
        return stack.enter_context(nc.sbuf_tensor(f"ahead_{name}", [P, k, n], F32))

    project_in(nc, a)
    with ExitStack() as st:
        w_out = weights(st, "w_out", NC_T, D)
        selective_scan(nc, a, w_out)
        mix_out(nc, a, w_out)
    with ExitStack() as st:
        w1_hi, w1_lo = weights(st, "w1_hi", KD, DF), weights(st, "w1_lo", KD, DF)
        rank_tokens(nc, a, w1_hi, w1_lo)
        select_ffn(nc, a, w1_hi, w1_lo)
    attend_in(nc, a)
    with ExitStack() as st:
        w_o, wg, wu = (weights(st, n, KD, D) for n in ("w_o", "wg_s", "wu_s"))
        wd = weights(st, "wd_s", I_SH // P, D)
        attend(nc, a, ((w_o, "w_o"), (wg, "wg_s"), (wu, "wu_s"), (wd, "wd_s")))
        attend_out(nc, a, w_o)
        shared_ffn(nc, a, wg, wu, wd)
    route_tokens(nc, a)
    experts(nc, a)
    combine(nc, a)


def layout(inputs):
    import numpy as np

    v = {k: np.asarray(x) for k, x in inputs.items()}
    per_channel = lambda x: np.ascontiguousarray(x.reshape(NC_T, P, *x.shape[1:]).swapaxes(0, 1))
    w = v["L0_attn_W_in"]
    z, x, bm, cm, dtl = np.split(w, np.cumsum([D_INNER, P, P, D_INNER]), axis=0)
    cm = cm.reshape(NC_T, GPT, N_QUAD, 4, D).transpose(0, 2, 3, 1, 4).reshape(D_INNER, D)
    out = {
        "x": v["L0_attn_hidden_states"].reshape(T, D),
        "w_in": np.ascontiguousarray(np.concatenate([z, cm, dtl, x, bm]).T),
        "w_dt": np.ascontiguousarray(v["L0_attn_W_dt"].T),
        "b_dt": per_channel(v["L0_attn_b_dt"]),
        "conv_w": per_channel(v["L0_attn_conv_w"][:, 0, :]),
        "conv_b": per_channel(v["L0_attn_conv_b"]),
        "a_log": per_channel(v["L0_attn_A_log"]),
        "d_param": per_channel(v["L0_attn_D_param"]),
        "w_out": np.ascontiguousarray(v["L0_attn_W_out"].T),
        "w_r": v["L0_ffn_w_r"].reshape(1, D),
        "b_r": v["L0_ffn_b_r"].reshape(1, 1),
        "w1": v["L0_ffn_w1"],
        "b1": np.ascontiguousarray(v["L0_ffn_b1"].reshape(KF, P).T),
        "w2": v["L0_ffn_w2"],
        "b2": v["L0_ffn_b2"].reshape(1, D),
        "w_qkv": np.ascontiguousarray(v["L1_attn_w_project"].T),
        "w_o": np.ascontiguousarray(v["L1_attn_w_out"].T),
        "cent": np.ascontiguousarray(v["L1_ffn_centroids"].T),
        "gate_b": v["L1_ffn_gate_bias"].reshape(1, E),
        "wg_s": v["L1_ffn_wg_s"], "wu_s": v["L1_ffn_wu_s"], "wd_s": v["L1_ffn_wd_s"],
        "wg": v["L1_ffn_wg"], "wu": v["L1_ffn_wu"], "wd": v["L1_ffn_wd"],
    }
    p = np.arange(P)
    out["c_ident"] = np.eye(P, dtype=np.float32)
    rep = np.zeros((P, NC_T, P), np.float32)
    for c in range(NC_T):
        rep[16 * c + p % 16, c, p] = 1
    out["c_rep"] = rep
    sel = np.zeros((3, 4, GPT, 4, P), np.float32)
    for n in range(4):
        for g in range(GPT):
            sel[:, n, g, n, 16 * g:16 * g + 16] = 1
    out["c_sel"] = sel.reshape(C_ROWS, 4, P)
    mask = np.zeros((P, L), np.float32)
    mask[:, L - P:] = np.where(p[None, :] > p[:, None], np.float32(NEG), np.float32(0))
    out["c_mask"] = mask
    out["c_earlier"] = (p[None, :] < p[:, None]).astype(np.float32)
    out["c_before"] = (p[:, None] < p[None, :]).astype(np.float32)
    out["c_rev"] = (E - np.arange(E, dtype=np.float32)).reshape(1, E)
    out["c_full_at"] = (SLOT_TILE * np.arange(T // SLOT_TILE, dtype=np.float32)).reshape(1, -1)
    out["c_tile_no"] = np.arange(N_TILES, dtype=np.float32).reshape(1, -1)
    out["c_ones"] = np.ones((P, P), np.float32)
    return out


def kernel(**inputs):
    import numpy as _np
    import concourse.bacc as _bacc
    from concourse import mybir as _mybir
    from concourse.bass_utils import run_bass_kernel_spmd as _run

    nc = _bacc.Bacc("TRN2", target_bir_lowering=False, num_devices=1)
    arrays, args = {}, {}
    for name, arr in layout(inputs).items():
        arrays[f"in_{name}"] = arr
        args[name] = nc.dram_tensor(f"in_{name}", arr.shape, _mybir.dt.from_np(arr.dtype), kind="ExternalInput").ap()
    for name, (shape, dt) in SCRATCH.items():
        args[name] = nc.dram_tensor(name, shape, dt).ap()
    args["out"] = nc.dram_tensor("out_0_dram", (T, D), F32, kind="ExternalOutput").ap()
    build(nc, args)
    r = _run(nc, [arrays], core_ids=[0])
    return r.results[0]["out_0_dram"].reshape(B, L, D)
```
